# Optimizing a Trainium2 kernel written in Bass

```python
import numpy as np
import jax
import jax.numpy as jnp

def _softmax(x, axis=-1):
    return jax.nn.softmax(x, axis=axis)

def _gelu(x):
    return jax.nn.gelu(x, approximate=True)

def _silu(x):
    return jax.nn.silu(x)

def _sigmoid(x):
    return jax.nn.sigmoid(x)

def _layernorm(x, axis=-1, eps=1e-05):
    m = jnp.mean(x, axis=axis, keepdims=True)
    v = jnp.var(x, axis=axis, keepdims=True)
    return (x - m) / jnp.sqrt(v + eps)

def _scatter_add(tgt, idx, src, axis=0):
    return tgt.at[idx].add(src)

def _segment_sum(src, seg, n):
    return jax.ops.segment_sum(src, seg, n)
kernel_name = 'mk_decoder_postln_d2_seqx_r2_fe30eb'

def setup_inputs(seed: int=0):
    np.random.seed(seed)
    _w = jnp.asarray

    def _rec_inputs():
        import jax
        import jax.numpy as jnp
        _rk = jax.random.key(seed)
        x = -0.0003929 + 0.9999 * jax.random.normal(jax.random.fold_in(_rk, 1), (8, 512, 512), jnp.float32)
        _lenS = 512 - jax.random.randint(jax.random.fold_in(_rk, 7), (8,), 0, max(1, 512 // 4) + 1, jnp.int32)
        _lenS2 = 77 - jax.random.randint(jax.random.fold_in(_rk, 8), (8,), 0, max(1, 77 // 4) + 1, jnp.int32)
        _ctx_1024P = jax.random.normal(jax.random.fold_in(_rk, 11), (8, 16, 512), jnp.float32)
        _ctx_1024c = jax.random.dirichlet(jax.random.fold_in(_rk, 511), 0.3 * jnp.ones((16,), jnp.float32), (8, 77))
        _ctx_1024t = jnp.einsum('bsk,bkd->bsd', _ctx_1024c, _ctx_1024P)
        _ctx_1024t = _ctx_1024t * jax.lax.rsqrt(jnp.mean(jnp.square(_ctx_1024t)) + 1e-12) * 0.953939
        ctx_1024 = -3.05549e-07 + 0.0199987 * (_ctx_1024t + 0.3 * jax.random.normal(jax.random.fold_in(_rk, 611), (8, 77, 512), jnp.float32))
        _validS = jnp.arange(512)[None, :] < _lenS[:, None]
        _validS2 = jnp.arange(77)[None, :] < _lenS2[:, None]
        _causal = jnp.tril(jnp.ones((512, 512), dtype=bool))
        mask_Bx1xSxS2_if1 = jnp.where(jnp.ones((8, 1, 512, 77), dtype=bool), 1, 0).astype(jnp.int32)
        return (x, ctx_1024, mask_Bx1xSxS2_if1)
    x, ctx_1024, mask_Bx1xSxS2_if1 = _rec_inputs()

    def _L0_attn_setup():
        import jax, jax.numpy as jnp
        import numpy as np
        N_HEAD = 16
        MIN_CTX = 128
        FULL_CTX = 512

        def _pruning_ratio(T):
            if T < MIN_CTX:
                return 1.0
            if T >= FULL_CTX:
                return 0.2
            progress = (T - MIN_CTX) / (FULL_CTX - MIN_CTX)
            return 0.5 - 0.3 * progress
        key = jax.random.key(seed)
        ks = jax.random.split(key, 3)
        B, T, C = (2, 1024, 512)
        x = jax.random.normal(ks[0], (B, T, C), jnp.float32)
        w_attn = jax.random.normal(ks[1], (3 * C, C), jnp.float32) * 0.02
        b_attn = jnp.zeros((3 * C,), jnp.float32)
        w_proj = jax.random.normal(ks[2], (C, C), jnp.float32) * 0.02
        b_proj = jnp.zeros((C,), jnp.float32)
        return {'x': x, 'w_attn': w_attn, 'b_attn': b_attn, 'w_proj': w_proj, 'b_proj': b_proj}
    _L0_attn_all = _L0_attn_setup()
    _L0_attn_in = {k: v for k, v in _L0_attn_all.items() if k in ('w_attn', 'b_attn', 'w_proj', 'b_proj')}
    del _L0_attn_all

    def _L0_xattn_setup():
        import jax, jax.numpy as jnp
        import numpy as np
        E, T, H, F = (8, 1024, 512, 2048)
        key = jax.random.key(seed)
        k1, k2, k3 = jax.random.split(key, 3)
        x = jax.random.normal(k1, (E, T, H), dtype=jnp.float32)
        w1 = jax.random.normal(k2, (E, F, H), dtype=jnp.float32) * 0.02
        w2 = jax.random.normal(k3, (E, F, H), dtype=jnp.float32) * 0.02
        return {'x': x, 'w1': w1, 'w2': w2}
    _L0_xattn_all = _L0_xattn_setup()
    _L0_xattn_in = {k: v for k, v in _L0_xattn_all.items() if k in ()}
    del _L0_xattn_all

    def _L0_ffn_setup():
        import jax, jax.numpy as jnp
        import numpy as np
        B, S, D = (1, 1024, 512)
        E, K, F = (64, 8, 384)
        SF = 384
        C = 256
        ROUTED_SCALE = 1.0

        def _moe_forward(x, router_w, w_gate, w_up, w_down, ws_gate_up, ws_down):
            T = x.shape[0]
            logits = x.astype(jnp.float32) @ router_w.T
            probs = jax.nn.softmax(logits, axis=-1)
            topk_w, topk_ids = jax.lax.top_k(probs, K)
            topk_w = topk_w / jnp.sum(topk_w, axis=-1, keepdims=True)
            topk_w = topk_w.astype(x.dtype)
            N = T * K
            flat_e = topk_ids.reshape(-1)
            flat_w = topk_w.reshape(-1)
            tok = jnp.arange(N) // K
            onehot = flat_e[:, None] == jnp.arange(E)[None, :]
            pos = jnp.cumsum(onehot, axis=0)[jnp.arange(N), flat_e] - 1
            valid = pos < C
            idx = jnp.where(valid, flat_e * C + pos, E * C)
            x_buf = jnp.zeros((E * C + 1, x.shape[1]), x.dtype).at[idx].set(x[tok])
            xb = x_buf[:E * C].reshape(E, C, -1)
            g = jnp.einsum('ecd,edf->ecf', xb, w_gate)
            u = jnp.einsum('ecd,edf->ecf', xb, w_up)
            h = jax.nn.silu(g) * u
            y = jnp.einsum('ecf,efd->ecd', h, w_down).reshape(E * C, -1)
            safe = jnp.where(valid, idx, 0)
            contrib = y[safe] * (flat_w * valid.astype(flat_w.dtype))[:, None]
            routed = jax.ops.segment_sum(contrib, tok, num_segments=T)
            routed = routed * ROUTED_SCALE
            gu = x @ ws_gate_up
            sg, su = (gu[:, :SF], gu[:, SF:])
            shared = jax.nn.silu(sg) * su @ ws_down
            return routed + shared
        key = jax.random.key(seed)
        ks = jax.random.split(key, 7)
        w = 0.02
        return {'hidden_states': jax.random.normal(ks[0], (B, S, D), jnp.float32), 'router_w': jax.random.normal(ks[1], (E, D), jnp.float32) * w, 'w_gate': jax.random.normal(ks[2], (E, D, F), jnp.float32) * w, 'w_up': jax.random.normal(ks[3], (E, D, F), jnp.float32) * w, 'w_down': jax.random.normal(ks[4], (E, F, D), jnp.float32) * w, 'ws_gate_up': jax.random.normal(ks[5], (D, 2 * SF), jnp.float32) * w, 'ws_down': jax.random.normal(ks[6], (SF, D), jnp.float32) * w}
    _L0_ffn_all = _L0_ffn_setup()
    _L0_ffn_in = {k: v for k, v in _L0_ffn_all.items() if k in ('router_w', 'w_gate', 'w_up', 'w_down', 'ws_gate_up', 'ws_down')}
    del _L0_ffn_all

    def _L1_attn_setup():
        import jax, jax.numpy as jnp
        import numpy as np
        D_MODEL = 512
        N_HEADS = 16
        D_K = D_MODEL // N_HEADS
        key = jax.random.key(seed)
        ks = jax.random.split(key, 5)
        s = 1.0 / np.sqrt(D_MODEL)
        x = jax.random.normal(ks[0], (4, 1024, D_MODEL), dtype=jnp.float32)
        Wq = jax.random.normal(ks[1], (D_MODEL, D_MODEL), dtype=jnp.float32) * s
        Wk = jax.random.normal(ks[2], (D_MODEL, D_MODEL), dtype=jnp.float32) * s
        Wv = jax.random.normal(ks[3], (D_MODEL, D_MODEL), dtype=jnp.float32) * s
        Wo = jax.random.normal(ks[4], (D_MODEL, D_MODEL), dtype=jnp.float32) * s
        z = jnp.zeros((D_MODEL,), dtype=jnp.float32)
        return {'x': x, 'Wq': Wq, 'bq': z, 'Wk': Wk, 'bk': z, 'Wv': Wv, 'bv': z, 'Wo': Wo, 'bo': z}
    _L1_attn_all = _L1_attn_setup()
    _L1_attn_in = {k: v for k, v in _L1_attn_all.items() if k in ('Wq', 'bq', 'Wk', 'bk', 'Wv', 'bv', 'Wo', 'bo')}
    del _L1_attn_all

    def _L1_xattn_setup():
        import jax, jax.numpy as jnp
        import numpy as np
        N, L, E, H = (4, 1024, 512, 16)
        D = E // H
        key = jax.random.key(seed)
        ks = jax.random.split(key, 8)
        return {'values': jax.random.normal(ks[0], (N, L, E), dtype=jnp.float32), 'keys': jax.random.normal(ks[1], (N, L, E), dtype=jnp.float32), 'query': jax.random.normal(ks[2], (N, L, E), dtype=jnp.float32), 'mask': jnp.ones((N, 1, L, L), dtype=jnp.int32), 'Wv': jax.random.normal(ks[3], (D, D), dtype=jnp.float32) * D ** (-0.5), 'Wk': jax.random.normal(ks[4], (D, D), dtype=jnp.float32) * D ** (-0.5), 'Wq': jax.random.normal(ks[5], (D, D), dtype=jnp.float32) * D ** (-0.5), 'Wo': jax.random.normal(ks[6], (E, E), dtype=jnp.float32) * E ** (-0.5), 'bo': jnp.zeros((E,), dtype=jnp.float32)}
    _L1_xattn_all = _L1_xattn_setup()
    _L1_xattn_in = {k: v for k, v in _L1_xattn_all.items() if k in ('Wv', 'Wk', 'Wq', 'Wo', 'bo')}
    del _L1_xattn_all

    def _L1_ffn_setup():
        import jax, jax.numpy as jnp
        import numpy as np
        B, L, C1, C2, K, K_IN = (4, 512, 512, 512, 32, 32)
        BN_EPS = 1e-05

        def _gated_bottleneck(x2d, conv_w, conv_b, gamma, beta, lin_w, lin_b):
            n = x2d.shape[0]
            g = conv_w.shape[0]
            xc = jnp.einsum('ngf,gf->ng', x2d.reshape(n, g, 4), conv_w) + conv_b
            mean = jnp.mean(xc, axis=0)
            var = jnp.mean((xc - mean) ** 2, axis=0)
            xn = (xc - mean) * jax.lax.rsqrt(var + BN_EPS) * gamma + beta
            xa = jax.nn.gelu(xn, approximate=False)
            return xa @ lin_w.T + lin_b
        key = jax.random.key(seed)
        ks = jax.random.split(key, 8)
        g = C1 // 4
        w_std = (2.0 / C2) ** 0.5
        lin_std = (1.0 / g) ** 0.5
        return {'x': jax.random.normal(ks[0], (B, L, C1), jnp.float32), 'weight': jax.random.normal(ks[1], (C1, C2), jnp.float32) * w_std, 'bias': jnp.zeros((C2,), jnp.float32), 'so_conv_w': jax.random.normal(ks[2], (g, 4), jnp.float32) * 0.5, 'so_conv_b': jnp.zeros((g,), jnp.float32), 'so_gamma': jnp.ones((g,), jnp.float32), 'so_beta': jnp.zeros((g,), jnp.float32), 'so_lin_w': jax.random.normal(ks[3], (C2, g), jnp.float32) * lin_std, 'so_lin_b': jnp.zeros((C2,), jnp.float32), 'si_conv_w': jax.random.normal(ks[4], (g, 4), jnp.float32) * 0.5, 'si_conv_b': jnp.zeros((g,), jnp.float32), 'si_gamma': jnp.ones((g,), jnp.float32), 'si_beta': jnp.zeros((g,), jnp.float32), 'si_lin_w': jax.random.normal(ks[5], (C1, g), jnp.float32) * lin_std, 'si_lin_b': jnp.zeros((C1,), jnp.float32)}
    _L1_ffn_all = _L1_ffn_setup()
    _L1_ffn_in = {k: v for k, v in _L1_ffn_all.items() if k in ('weight', 'bias', 'so_conv_w', 'so_conv_b', 'so_gamma', 'so_beta', 'so_lin_w', 'so_lin_b', 'si_conv_w', 'si_conv_b', 'si_gamma', 'si_beta', 'si_lin_w', 'si_lin_b')}
    del _L1_ffn_all
    return {'x': x, 'ctx_1024': ctx_1024, 'mask_Bx1xSxS2_if1': mask_Bx1xSxS2_if1, 'L0_attn_w_attn': _L0_attn_in['w_attn'], 'L0_attn_b_attn': _L0_attn_in['b_attn'], 'L0_attn_w_proj': _L0_attn_in['w_proj'], 'L0_attn_b_proj': _L0_attn_in['b_proj'], 'L0_ffn_router_w': _L0_ffn_in['router_w'], 'L0_ffn_w_gate': _L0_ffn_in['w_gate'], 'L0_ffn_w_up': _L0_ffn_in['w_up'], 'L0_ffn_w_down': _L0_ffn_in['w_down'], 'L0_ffn_ws_gate_up': _L0_ffn_in['ws_gate_up'], 'L0_ffn_ws_down': _L0_ffn_in['ws_down'], 'L1_attn_Wq': _L1_attn_in['Wq'], 'L1_attn_bq': _L1_attn_in['bq'], 'L1_attn_Wk': _L1_attn_in['Wk'], 'L1_attn_bk': _L1_attn_in['bk'], 'L1_attn_Wv': _L1_attn_in['Wv'], 'L1_attn_bv': _L1_attn_in['bv'], 'L1_attn_Wo': _L1_attn_in['Wo'], 'L1_attn_bo': _L1_attn_in['bo'], 'L1_xattn_Wv': _L1_xattn_in['Wv'], 'L1_xattn_Wk': _L1_xattn_in['Wk'], 'L1_xattn_Wq': _L1_xattn_in['Wq'], 'L1_xattn_Wo': _L1_xattn_in['Wo'], 'L1_xattn_bo': _L1_xattn_in['bo'], 'L1_ffn_weight': _L1_ffn_in['weight'], 'L1_ffn_bias': _L1_ffn_in['bias'], 'L1_ffn_so_conv_w': _L1_ffn_in['so_conv_w'], 'L1_ffn_so_conv_b': _L1_ffn_in['so_conv_b'], 'L1_ffn_so_gamma': _L1_ffn_in['so_gamma'], 'L1_ffn_so_beta': _L1_ffn_in['so_beta'], 'L1_ffn_so_lin_w': _L1_ffn_in['so_lin_w'], 'L1_ffn_so_lin_b': _L1_ffn_in['so_lin_b'], 'L1_ffn_si_conv_w': _L1_ffn_in['si_conv_w'], 'L1_ffn_si_conv_b': _L1_ffn_in['si_conv_b'], 'L1_ffn_si_gamma': _L1_ffn_in['si_gamma'], 'L1_ffn_si_beta': _L1_ffn_in['si_beta'], 'L1_ffn_si_lin_w': _L1_ffn_in['si_lin_w'], 'L1_ffn_si_lin_b': _L1_ffn_in['si_lin_b']}

def reference(x, ctx_1024, mask_Bx1xSxS2_if1, L0_attn_w_attn, L0_attn_b_attn, L0_attn_w_proj, L0_attn_b_proj, L0_ffn_router_w, L0_ffn_w_gate, L0_ffn_w_up, L0_ffn_w_down, L0_ffn_ws_gate_up, L0_ffn_ws_down, L1_attn_Wq, L1_attn_bq, L1_attn_Wk, L1_attn_bk, L1_attn_Wv, L1_attn_bv, L1_attn_Wo, L1_attn_bo, L1_xattn_Wv, L1_xattn_Wk, L1_xattn_Wq, L1_xattn_Wo, L1_xattn_bo, L1_ffn_weight, L1_ffn_bias, L1_ffn_so_conv_w, L1_ffn_so_conv_b, L1_ffn_so_gamma, L1_ffn_so_beta, L1_ffn_so_lin_w, L1_ffn_so_lin_b, L1_ffn_si_conv_w, L1_ffn_si_conv_b, L1_ffn_si_gamma, L1_ffn_si_beta, L1_ffn_si_lin_w, L1_ffn_si_lin_b):
    import jax
    import jax.numpy as jnp

    def _L0_attn_ref(x, w_attn, b_attn, w_proj, b_proj):
        import jax, jax.numpy as jnp
        import numpy as np
        N_HEAD = 16
        MIN_CTX = 128
        FULL_CTX = 512

        def _pruning_ratio(T):
            if T < MIN_CTX:
                return 1.0
            if T >= FULL_CTX:
                return 0.2
            progress = (T - MIN_CTX) / (FULL_CTX - MIN_CTX)
            return 0.5 - 0.3 * progress
        B, T, C = x.shape
        nh = N_HEAD
        hd = C // nh
        neg_inf = jnp.float32(-jnp.inf)
        qkv = x @ w_attn.T + b_attn
        q, k, v = jnp.split(qkv, 3, axis=2)
        to_heads = lambda t: t.reshape(B, T, nh, hd).transpose(0, 2, 1, 3)
        q, k, v = (to_heads(q), to_heads(k), to_heads(v))
        att = jnp.einsum('bhid,bhjd->bhij', q, k) / jnp.sqrt(jnp.float32(hd))
        i = jnp.arange(T)
        causal = i[None, :] <= i[:, None]
        att = jnp.where(causal[None, None], att, neg_inf)
        S = jax.nn.relu(att[:, 0])
        S = S.at[..., 0].set(0.0)
        S = S * (1.0 - jnp.eye(T, dtype=S.dtype))
        S_shifted = jnp.concatenate([jnp.zeros((B, 1, T), S.dtype), S[:, :-1]], axis=1)
        FF = jnp.cumsum(S_shifted, axis=1)
        att = att - FF[:, None]
        ratio = _pruning_ratio(T)
        memory_budget = max(1, int(T * ratio))
        if ratio < 1.0:
            FF_mod = jnp.where(causal[None], FF, jnp.inf)
            sorted_idx = jnp.argsort(FF_mod, axis=-1)
            rank = jnp.argsort(sorted_idx, axis=-1)
            eff_k = jnp.minimum(memory_budget - 1, i + 1)
            keep = rank < eff_k[None, :, None]
            keep = keep | jnp.eye(T, dtype=bool)[None]
            att = jnp.where(keep[:, None], att, neg_inf)
        y = jax.nn.softmax(att, axis=-1) @ v
        y = y.transpose(0, 2, 1, 3).reshape(B, T, C)
        return y @ w_proj.T + b_proj

    def _L0_xattn_ref(x, w1, w2):
        import jax, jax.numpy as jnp
        import numpy as np
        E, T, H, F = (8, 1024, 512, 2048)
        h = jnp.einsum('eth,efh->etf', x, w1)
        a = jax.nn.gelu(h, approximate=True)
        return jnp.einsum('etf,efh->eth', a, w2)

    def _L0_ffn_ref(hidden_states, router_w, w_gate, w_up, w_down, ws_gate_up, ws_down):
        import jax, jax.numpy as jnp
        import numpy as np
        B, S, D = (1, 1024, 512)
        E, K, F = (64, 8, 384)
        SF = 384
        C = 256
        ROUTED_SCALE = 1.0

        def _moe_forward(x, router_w, w_gate, w_up, w_down, ws_gate_up, ws_down):
            T = x.shape[0]
            logits = x.astype(jnp.float32) @ router_w.T
            probs = jax.nn.softmax(logits, axis=-1)
            topk_w, topk_ids = jax.lax.top_k(probs, K)
            topk_w = topk_w / jnp.sum(topk_w, axis=-1, keepdims=True)
            topk_w = topk_w.astype(x.dtype)
            N = T * K
            flat_e = topk_ids.reshape(-1)
            flat_w = topk_w.reshape(-1)
            tok = jnp.arange(N) // K
            onehot = flat_e[:, None] == jnp.arange(E)[None, :]
            pos = jnp.cumsum(onehot, axis=0)[jnp.arange(N), flat_e] - 1
            valid = pos < C
            idx = jnp.where(valid, flat_e * C + pos, E * C)
            x_buf = jnp.zeros((E * C + 1, x.shape[1]), x.dtype).at[idx].set(x[tok])
            xb = x_buf[:E * C].reshape(E, C, -1)
            g = jnp.einsum('ecd,edf->ecf', xb, w_gate)
            u = jnp.einsum('ecd,edf->ecf', xb, w_up)
            h = jax.nn.silu(g) * u
            y = jnp.einsum('ecf,efd->ecd', h, w_down).reshape(E * C, -1)
            safe = jnp.where(valid, idx, 0)
            contrib = y[safe] * (flat_w * valid.astype(flat_w.dtype))[:, None]
            routed = jax.ops.segment_sum(contrib, tok, num_segments=T)
            routed = routed * ROUTED_SCALE
            gu = x @ ws_gate_up
            sg, su = (gu[:, :SF], gu[:, SF:])
            shared = jax.nn.silu(sg) * su @ ws_down
            return routed + shared
        b, s, d = hidden_states.shape
        x = hidden_states.reshape(-1, d)
        out = _moe_forward(x, router_w, w_gate, w_up, w_down, ws_gate_up, ws_down)
        return out.reshape(b, s, d)

    def _L1_attn_ref(x, Wq, bq, Wk, bk, Wv, bv, Wo, bo):
        import jax, jax.numpy as jnp
        import numpy as np
        D_MODEL = 512
        N_HEADS = 16
        D_K = D_MODEL // N_HEADS
        B, S, _ = x.shape

        def proj(W, b):
            y = jnp.einsum('bsd,ed->bse', x, W) + b
            return y.reshape(B, S, N_HEADS, D_K).transpose(0, 2, 1, 3)
        q = proj(Wq, bq)
        k = proj(Wk, bk)
        v = proj(Wv, bv)
        scale = 1.0 / np.sqrt(D_K)
        attn = jnp.einsum('bhqd,bhkd->bhqk', q, k) * scale
        attn = jax.nn.softmax(attn, axis=-1)
        out = jnp.einsum('bhqk,bhkd->bhqd', attn, v)
        out = out.transpose(0, 2, 1, 3).reshape(B, S, D_MODEL)
        return jnp.einsum('bsd,ed->bse', out, Wo) + bo

    def _L1_xattn_ref(values, keys, query, mask, Wv, Wk, Wq, Wo, bo):
        import jax, jax.numpy as jnp
        import numpy as np
        N, L, E, H = (4, 1024, 512, 16)
        D = E // H
        n, lq, e = query.shape
        lk = keys.shape[1]
        v = values.reshape(n, lk, H, D) @ Wv.T
        k = keys.reshape(n, lk, H, D) @ Wk.T
        q = query.reshape(n, lq, H, D) @ Wq.T
        energy = jnp.einsum('nqhd,nkhd->nhqk', q, k)
        energy = jnp.where(mask == 0, jnp.float32(-1e+20), energy)
        attn = jax.nn.softmax(energy / jnp.sqrt(jnp.float32(e)), axis=3)
        out = jnp.einsum('nhqk,nkhd->nqhd', attn, v).reshape(n, lq, e)
        return out @ Wo.T + bo

    def _L1_ffn_ref(x, weight, bias, so_conv_w, so_conv_b, so_gamma, so_beta, so_lin_w, so_lin_b, si_conv_w, si_conv_b, si_gamma, si_beta, si_lin_w, si_lin_b):
        import jax, jax.numpy as jnp
        import numpy as np
        B, L, C1, C2, K, K_IN = (4, 512, 512, 512, 32, 32)
        BN_EPS = 1e-05

        def _gated_bottleneck(x2d, conv_w, conv_b, gamma, beta, lin_w, lin_b):
            n = x2d.shape[0]
            g = conv_w.shape[0]
            xc = jnp.einsum('ngf,gf->ng', x2d.reshape(n, g, 4), conv_w) + conv_b
            mean = jnp.mean(xc, axis=0)
            var = jnp.mean((xc - mean) ** 2, axis=0)
            xn = (xc - mean) * jax.lax.rsqrt(var + BN_EPS) * gamma + beta
            xa = jax.nn.gelu(xn, approximate=False)
            return xa @ lin_w.T + lin_b
        b, l, c1 = x.shape
        c2 = weight.shape[1]
        x2d = x.reshape(b * l, c1)
        bi = jnp.arange(b)[:, None, None]
        li = jnp.arange(l)[None, :, None]
        score_out = jax.nn.softmax(_gated_bottleneck(x2d, so_conv_w, so_conv_b, so_gamma, so_beta, so_lin_w, so_lin_b).reshape(b, l, c2), axis=-1)
        s_v_out, s_i_out = jax.lax.top_k(score_out, K)
        full = jnp.einsum('blc,co->blo', x, weight)
        out_k = jnp.take_along_axis(full, s_i_out, axis=-1) * s_v_out
        out_branch = jnp.zeros((b, l, c2), x.dtype).at[bi, li, s_i_out].add(out_k)
        score_in = jax.nn.softmax(_gated_bottleneck(x2d, si_conv_w, si_conv_b, si_gamma, si_beta, si_lin_w, si_lin_b).reshape(b, l, c1), axis=-1)
        s_v_in, s_i_in = jax.lax.top_k(score_in, K_IN)
        x_gated = jnp.take_along_axis(x, s_i_in, axis=-1) * s_v_in
        x_sparse = jnp.zeros((b, l, c1), x.dtype).at[bi, li, s_i_in].add(x_gated)
        in_branch = jnp.einsum('blc,co->blo', x_sparse, weight)
        return out_branch + in_branch + bias
    x = _layernorm(x + _L0_attn_ref(x, L0_attn_w_attn, L0_attn_b_attn, L0_attn_w_proj, L0_attn_b_proj), axis=-1)
    x = _layernorm(x + _L0_xattn_ref(x, ctx_1024, ctx_1024), axis=-1)
    x = _layernorm(x + _L0_ffn_ref(x, L0_ffn_router_w, L0_ffn_w_gate, L0_ffn_w_up, L0_ffn_w_down, L0_ffn_ws_gate_up, L0_ffn_ws_down), axis=-1)
    x = _layernorm(x + _L1_attn_ref(x, L1_attn_Wq, L1_attn_bq, L1_attn_Wk, L1_attn_bk, L1_attn_Wv, L1_attn_bv, L1_attn_Wo, L1_attn_bo), axis=-1)
    x = _layernorm(x + _L1_xattn_ref(ctx_1024, ctx_1024, x, mask_Bx1xSxS2_if1, L1_xattn_Wv, L1_xattn_Wk, L1_xattn_Wq, L1_xattn_Wo, L1_xattn_bo), axis=-1)
    x = _layernorm(x + _L1_ffn_ref(x, L1_ffn_weight, L1_ffn_bias, L1_ffn_so_conv_w, L1_ffn_so_conv_b, L1_ffn_so_gamma, L1_ffn_so_beta, L1_ffn_so_lin_w, L1_ffn_so_lin_b, L1_ffn_si_conv_w, L1_ffn_si_conv_b, L1_ffn_si_gamma, L1_ffn_si_beta, L1_ffn_si_lin_w, L1_ffn_si_lin_b), axis=-1)
    return x

_drawn_inputs = setup_inputs


def setup_inputs(seed=0):
    import zlib

    import numpy as np

    out = dict(_drawn_inputs(seed))
    spreads = {'L0_attn_b_attn': (0.0, 0.1),
     'L0_attn_b_proj': (0.0, 0.1),
     'L1_attn_bq': (0.0, 0.8),
     'L1_attn_bk': (0.0, 0.8),
     'L1_attn_bv': (0.0, 0.1),
     'L1_attn_bo': (0.0, 0.1),
     'L1_xattn_bo': (0.0, 0.1),
     'L1_ffn_bias': (0.0, 0.1),
     'L1_ffn_so_conv_b': (0.0, 0.8),
     'L1_ffn_so_gamma': (1.0, 0.6),
     'L1_ffn_so_beta': (0.0, 0.8),
     'L1_ffn_so_lin_b': (0.0, 0.8),
     'L1_ffn_si_conv_b': (0.0, 0.8),
     'L1_ffn_si_gamma': (1.0, 0.6),
     'L1_ffn_si_beta': (0.0, 0.8),
     'L1_ffn_si_lin_b': (0.0, 0.8)}
    factors = {'L0_ffn_router_w': 5.25,
     'L0_ffn_w_gate': 4.871,
     'L0_ffn_w_up': 4.776,
     'L0_ffn_w_down': 4.763,
     'L1_xattn_Wv': 5.806,
     'L1_xattn_Wk': 8.0,
     'L1_xattn_Wq': 8.0,
     'L1_xattn_Wo': 5.639,
     'L1_ffn_weight': 8.0,
     'L1_ffn_so_conv_w': 8.0,
     'L1_ffn_so_lin_w': 8.0,
     'L1_ffn_si_conv_w': 8.0,
     'L1_ffn_si_lin_w': 8.0}
    for name, (base, spread) in spreads.items():
        noise = np.random.default_rng([zlib.crc32(name.encode()), seed]).standard_normal(out[name].shape)
        drawn = base * np.exp(spread * noise) if base else spread * noise
        out[name] = jnp.asarray(drawn.astype(out[name].dtype))
    for name, factor in factors.items():
        out[name] = (out[name] * factor).astype(out[name].dtype)
    return out
```

```python
import numpy as np
import concourse.bass as bass
from concourse import mybir
from contextlib import ExitStack

FP32 = mybir.dt.float32
BF16 = mybir.dt.bfloat16
I32 = mybir.dt.int32
ALU = mybir.AluOpType
ACT = mybir.ActivationFunctionType
AX = mybir.AxisListType

P = 128
B, S, D = 8, 512, 512
T = B * S
NT = S // P
NC = D // P
H, DH = 16, 32
HG = P // DH
S2 = 77
E, TOPK, F = 64, 8, 384
NF = F // P
CAP = 256
NJ = CAP // P
XW = D + E
KEEP = int(S * 0.2) - 1
KGATE = 32
G = D // 4
EPS = 1e-5
QSCALE = 1.0 / float(np.sqrt(DH))
XSCALE = 1.0 / float(np.sqrt(D))
FAR = 1e30
TAKEN = -3e38
GELU_C, GELU_A = 0.7978845608028654, 0.044715


def chain_of(eng, sem):
    count = [0]

    def link(ins):
        count[0] += 1
        ins.then_inc(sem, 1)
        eng.wait_ge(sem, count[0])

    def skip(n):
        count[0] += n
        eng.wait_ge(sem, count[0])
    link.skip = skip
    return link


def pruned_attention_stage(nc, A, scr, cst, trips):
    ident, upper, ones, upper_b, ones_b = (cst[k] for k in ("ident", "upper", "ones", "upper_b", "ones_b"))
    with ExitStack() as ctx:
        def sb(name, shape, dt=FP32):
            return ctx.enter_context(nc.sbuf_tensor("l0_" + name, shape, dt))

        sems = []

        def sem(name):
            s = ctx.enter_context(nc.semaphore("l0_" + name))
            sems.append(s)
            return s

        bank = [ctx.enter_context(nc.psum_tensor(f"l0_bank{i}", [P, 512], FP32)) for i in range(8)]

        w_qkv = sb("w_qkv", [P, NC, 3 * D])
        w_proj = sb("w_proj", [P, NC, D])
        w_router = sb("w_router", [P, NC, E])
        w_sgu = sb("w_sgu", [P, NC, 2 * F])
        w_sdown = sb("w_sdown", [P, NF, D])
        b_qkv = sb("b_qkv", [P, 3 * NC])
        b_proj = sb("b_proj", [P, D])
        x = sb("x", [P, NT, D])
        xT = sb("xT", [P, NC, S])
        qT = sb("qT", [P, NC, S])
        kpad = sb("kpad", [P, H, S])
        v = sb("v", [P, NT, D])
        bias = sb("bias", [P, NT, S])
        probs = sb("probs", [P, 4, 2, S])
        pT = sb("pT", [P, HG, NT, S])
        x2w = sb("x2w", [P, NT, XW])
        gate = probs[:, :, 0, :]
        work = sb("work", [P, S + 3])
        top = sb("top", [P, 8])
        nmax = sb("nmax", [P, 4, 2])
        psums = sb("psums", [P, 4, 2])
        rsum = sb("rsum", [P, 4, 2])
        x1T, x2T, hid, acc = pT[:, 0, :, :], pT[:, 1, :, :], pT[:, 2, :, :], pT[:, 3, :, :]
        yT = xT
        ctx_rows = sb("ctx_rows", [P, D])
        ctx_T = sb("ctx_T", [P, NC, S2])
        gl = work[:, 0:S]
        gelu_out = sb("gelu_out", [P, S])
        stats = sb("stats", [P, NT, 6])
        mv = sb("mv", [P, NT, 2])
        vare = sb("vare", [P, NT])
        rstd = sb("rstd", [P, NT])
        expv = sb("expv", [P, NT, E])
        left = sb("left", [P, NT, E])
        mask = sb("mask", [P, NT, E])
        mask_b = sb("mask_b", [P, NT, E], BF16)
        run = sb("run", [P, NT + 1, E], BF16)
        nmx = sb("nmx", [P, NT])
        wsum = sb("wsum", [P, NT])
        m8 = sb("m8", [P, NT, 8])
        enc = sb("enc", [P, NT, E])
        slot1 = sb("slot1", [P, E])
        off = sb("off", [P, NT * 8])
        idx = sb("idx", [P, NT * 8], I32)
        tok = sb("tok", [P, NT])

        setup_in = sem("setup_in")
        setup_pool = sem("setup_pool")
        setup_slots = sem("setup_slots")
        setup_dve = sem("setup_dve")

        with nc.Block() as block:
            @block.sync
            def _(sp):
                for dst, src in ((w_qkv, A["w_qkv0"]), (w_proj, A["w_proj0"]), (w_router, A["w_router"]),
                                 (w_sgu, A["w_sgu"]), (w_sdown, A["w_sdown"])):
                    sp.dma_start(dst[:, :, :], src.rearrange("(c p) n -> p c n", p=P)).then_inc(setup_in, 16)
                sp.dma_start(b_qkv[:, :], A["b_qkv0"]).then_inc(setup_in, 16)
                sp.dma_start(b_proj[:, :], A["b_proj0"].rearrange("(a n) -> a n", a=1).to_broadcast([P, D]))\
                    .then_inc(setup_in, 16)
                sp.wait_ge(setup_pool, 4)
                sp.dma_start(scr["slots"][1:E * CAP + 1, :].rearrange("(e n) o -> e (n o)", n=CAP),
                             work[0:E, 0:CAP]).then_inc(setup_slots, 16)
                sp.dma_start(scr["slots"][0:1, :], work[0:1, 0:1]).then_inc(setup_slots, 16)
                for j in range(NJ):
                    sp.dma_start(scr["rows"][T + j * P:T + (j + 1) * P, :], x2w[:, 0, :]).then_inc(setup_slots, 16)
                    sp.dma_start(scr["acc"][T + j * P:T + (j + 1) * P, :], x2w[:, 0, 0:D]).then_inc(setup_slots, 16)
                sp.wait_ge(setup_slots, (2 + 2 * NJ) * 16)

            @block.gpsimd
            def _(pool):
                pool.iota(tok[:, :], pattern=[[P, NT]], base=0, channel_multiplier=1,
                          allow_small_or_imprecise_dtypes=True).then_inc(setup_pool, 1)
                pool.iota(slot1[:, :], pattern=[[CAP, E]], base=1, channel_multiplier=0,
                          allow_small_or_imprecise_dtypes=True).then_inc(setup_pool, 1)
                pool.iota(work[:, 0:CAP], pattern=[[1, CAP]], base=T, channel_multiplier=0,
                          allow_small_or_imprecise_dtypes=True).then_inc(setup_pool, 1)
                pool.memset(x2w[:, 0, :], 0.0).then_inc(setup_pool, 1)

            @block.vector
            def _(dve):
                dve.memset(kpad[:, :, :], 0.0)
                dve.memset(gelu_out[:, :], 0.0)
                dve.memset(ctx_rows[:, :], 0.0)
                dve.memset(run[:, 0, :], 0.0)
                dve.wait_ge(setup_in, 7 * 16)
                dve.tensor_scalar(b_qkv[:, 0:NC], b_qkv[:, 0:NC], QSCALE, None, ALU.mult)

        loaded = sem("loaded")
        proj_full, proj_drained = sem("proj_full"), sem("proj_drained")
        gate_full, gate_relu = sem("gate_full"), sem("gate_relu")
        gate_masked = sem("gate_masked")
        forget_full, forget_out = sem("forget_full"), sem("forget_out")
        forget_causal = sem("forget_causal")
        dropped = sem("dropped")
        bias_ready = sem("bias_ready")
        resid = sem("resid")
        chain_p1 = sem("chain_p1")

        def width(t):
            return (t + 1) * P

        PROJ = [("q", 0), ("k", 0), ("v", 0), ("v", 1), ("v", 2), ("v", 3), ("q", 1), ("k", 1),
                ("f", 0), ("q", 2), ("k", 2), ("q", 3), ("k", 3)]

        def project_and_gate(b):
            with nc.Block() as block:
                @block.sync
                def _(sp):
                    sp.dma_start(xT[:, :, :], A["xT"][b].rearrange("(c p) n -> p c n", p=P)).then_inc(loaded, 16)
                    sp.dma_start(x[:, :, :], A["x"][b].rearrange("(t p) n -> p t n", p=P)).then_inc(loaded, 16)
                    sp.dma_start(ctx_rows[0:S2, :], A["ctx"][b]).then_inc(loaded, 16)
                    sp.dma_start(ctx_T[:, :, :], A["ctxT"][b].rearrange("(c p) n -> p c n", p=P)).then_inc(loaded, 16)
                    sp.wait_ge(loaded, 64)

                @block.tensor
                def _(pe):
                    pe.wait_ge(loaded, 64)
                    j = 0
                    for kind, i in PROJ:
                        if kind == "f":
                            for t in range(NT):
                                pe.wait_ge(gate_masked, 2 * (t + 1))
                                if t >= 2:
                                    pe.wait_ge(forget_out, t - 1)
                                out = bank[6 + t % 2]
                                mm = pe.matmul(out[:, 0:width(t)], upper[:, :], gate[:, t, 0:width(t)],
                                               start=True, stop=True)
                                for u in range(t):
                                    mm = pe.matmul(out[:, 0:width(u)], ones[:, :], gate[:, u, 0:width(u)],
                                                   start=False, stop=True, skip_group_check=True)
                                mm.then_inc(forget_full, 1)
                            continue
                        if j >= 4:
                            pe.wait_ge(proj_drained, j - 3)
                        out = bank[j % 4]
                        for c in range(NC):
                            if kind == "v":
                                mm = pe.matmul(out[:, :], xT[:, c, i * P:(i + 1) * P], w_qkv[:, c, 2 * D:3 * D],
                                               start=(c == 0), stop=(c == NC - 1))
                            else:
                                at = i * P + (D if kind == "k" else 0)
                                mm = pe.matmul(out[:, :], w_qkv[:, c, at:at + P], xT[:, c, :],
                                               start=(c == 0), stop=(c == NC - 1))
                        mm.then_inc(proj_full, 1)
                        j += 1
                        if j == 2:
                            pe.wait_ge(proj_drained, 2)
                            for t in range(NT):
                                if t >= 2:
                                    pe.wait_ge(gate_relu, t - 1)
                                pe.matmul(bank[4 + t % 2][:, 0:width(t)], qT[:, 0, t * P:(t + 1) * P],
                                          kpad[:, 0, 0:width(t)], start=True, stop=True).then_inc(gate_full, 1)

                @block.scalar
                def _(act):
                    j = 0
                    for kind, i in PROJ:
                        if kind == "f":
                            for t in range(NT):
                                act.wait_ge(forget_full, t + 1)
                                act.activation(bias[:, t, 0:width(t)], bank[6 + t % 2][:, 0:width(t)], ACT.Copy,
                                               scale=-1.0).then_inc(forget_out, 1)
                            continue
                        act.wait_ge(proj_full, j + 1)
                        src = bank[j % 4]
                        if kind == "q":
                            last = act.activation(qT[:, i, :], src[:, :], ACT.Identity, scale=QSCALE,
                                                  bias=b_qkv[:, i:i + 1])
                        elif kind == "k":
                            for h in range(HG):
                                r = slice(h * DH, (h + 1) * DH)
                                last = act.activation(kpad[r, i * HG + h, :], src[r, :], ACT.Identity,
                                                      bias=b_qkv[r, NC + i:NC + i + 1])
                        else:
                            last = act.activation(v[:, i, :], src[:, :], ACT.Copy)
                        last.then_inc(proj_drained, 1)
                        j += 1

                @block.gpsimd
                def _(pool):
                    for t in range(NT):
                        pool.wait_ge(gate_relu, t + 1)
                        own = gate[:, t, t * P:(t + 1) * P]
                        pool.affine_select(out=own, in_=own, pattern=[[-1, P]], compare_op=ALU.is_gt, fill=0.0,
                                           base=0, channel_multiplier=1).then_inc(gate_masked, 1)
                        pool.wait_ge(gate_masked, 2 * t + 1)
                        pool.memset(gate[:, t, 0:1], 0.0).then_inc(gate_masked, 1)
                    for t in range(NT):
                        pool.wait_ge(forget_out, t + 1)
                        own = bias[:, t, t * P:(t + 1) * P]
                        pool.affine_select(out=own, in_=own, pattern=[[-1, P]], compare_op=ALU.is_ge, fill=-FAR,
                                           base=0, channel_multiplier=1).then_inc(forget_causal, 1)
                    pool.wait_ge(loaded, 64)
                    for t in range(NT):
                        pool.tensor_tensor(x[:, t, :], x[:, t, :], b_proj[:, :], ALU.add).then_inc(resid, 1)
                    for t in range(NT):
                        pool.wait_ge(dropped, t + 1)
                        own = bias[:, t, t * P:(t + 1) * P]
                        pool.affine_select(out=own, in_=own, pattern=[[-1, P]], compare_op=ALU.not_equal, fill=0.0,
                                           base=0, channel_multiplier=1).then_inc(bias_ready, 1)
                    pool.wait_ge(bias_ready, NT)

                @block.vector
                def _(dve):
                    link = chain_of(dve, chain_p1)
                    for t in range(NT):
                        dve.wait_ge(gate_full, t + 1)
                        dve.tensor_scalar(gate[:, t, 0:width(t)], bank[4 + t % 2][:, 0:width(t)], 0.0, None,
                                          ALU.max).then_inc(gate_relu, 1)
                    rounds = -(-KEEP // 8)
                    extra = rounds * 8 - KEEP
                    for t in range(NT):
                        w = width(t)
                        link(dve.memset(work[:, 0:extra], -TAKEN))
                        dve.wait_ge(forget_causal, t + 1)
                        link(dve.tensor_copy(work[:, extra:extra + w], bias[:, t, 0:w]))
                        for _ in range(rounds):
                            link(dve.max(top[:, :], work[:, 0:extra + w]))
                            link(dve.match_replace(work[:, 0:extra + w], top[:, :], work[:, 0:extra + w], TAKEN))
                        link(dve.tensor_scalar(work[:, extra:extra + w], work[:, extra:extra + w], TAKEN / 2, -FAR,
                                               ALU.is_gt, ALU.mult))
                        dve.tensor_tensor(bias[:, t, 0:w], bias[:, t, 0:w], work[:, extra:extra + w],
                                          ALU.min).then_inc(dropped, 1)
                        dve.wait_ge(dropped, t + 1)

        scores_full, scores_out = sem("scores_full"), sem("scores_out")
        exp_done = sem("exp_done")
        rsum_ready = sem("rsum_ready")
        probs_ready = sem("probs_ready")
        pT_full = sem("pT_full")
        pT_out_dve, pT_out_act = sem("pT_out_dve"), sem("pT_out_act")
        attn_full, attn_out = sem("attn_full"), sem("attn_out")
        LAG = 3

        UNITS = [(g, t, p) for g in range(NC) for t in range(NT) for p in range(2)]
        PER_G = 2 * NT

        def heads():
            N = len(UNITS)
            with nc.Block() as block:
                @block.tensor
                def _(pe):
                    for n in range(N + LAG + 1):
                        if n < N:
                            g, t, p = UNITS[n]
                            if n >= 2:
                                pe.wait_ge(scores_out, 2 * (n - 1))
                            for hh in range(2):
                                mm = pe.matmul(bank[2 * (n % 2) + hh][:, 0:width(t)], qT[:, g, t * P:(t + 1) * P],
                                               kpad[:, HG * g + 2 * p + hh, 0:width(t)], start=True, stop=True)
                            mm.then_inc(scores_full, 1)
                        m = n - LAG
                        if m >= PER_G and m % PER_G == 0:
                            g = m // PER_G - 1
                            pe.wait_ge(pT_out_dve, m)
                            pe.wait_ge(pT_out_act, m)
                            if g >= 1:
                                pe.wait_ge(attn_out, g)
                            for kc in range(NT):
                                for h in range(HG):
                                    mm = pe.matmul(bank[6][h * DH:(h + 1) * DH, kc * P:S],
                                                   v[:, kc, (HG * g + h) * DH:(HG * g + h + 1) * DH],
                                                   pT[:, h, kc, kc * P:S], start=(kc == 0), stop=True,
                                                   skip_group_check=True)
                            mm.then_inc(attn_full, 1)
                        if 0 <= m < N:
                            g, t, p = UNITS[m]
                            pe.wait_ge(probs_ready, m + 1)
                            for hh in range(2):
                                if m >= 1:
                                    pe.wait_ge(pT_out_act if hh else pT_out_dve, m)
                                for kc in range(t + 1):
                                    mm = pe.transpose(bank[4 + hh][:, kc * P:(kc + 1) * P],
                                                      probs[:, m % 4, hh, kc * P:(kc + 1) * P], ident[:, :])
                                mm.then_inc(pT_full, 1)

                @block.vector
                def _(dve):
                    for n in range(N + LAG):
                        if n < N:
                            g, t, p = UNITS[n]
                            dve.wait_ge(scores_full, n + 1)
                            if n >= 4:
                                dve.wait_ge(pT_full, 2 * (n - 3))
                            for hh in range(2):
                                dve.tensor_tensor_reduce(
                                    out=probs[:, n % 4, hh, 0:width(t)], in0=bank[2 * (n % 2) + hh][:, 0:width(t)],
                                    in1=bias[:, t, 0:width(t)], scale=-1.0, scalar=-TAKEN, op0=ALU.add, op1=ALU.min,
                                    accum_out=nmax[:, n % 4, hh:hh + 1]).then_inc(scores_out, 1)
                        m = n - 1
                        if 0 <= m < N:
                            dve.wait_ge(exp_done, 2 * m + 2)
                            dve.reciprocal(rsum[:, m % 4, :], psums[:, m % 4, :]).then_inc(rsum_ready, 1)
                        m = n - LAG
                        if 0 <= m < N:
                            g, t, p = UNITS[m]
                            dve.wait_ge(pT_full, 2 * m + 1)
                            if g >= 1:
                                dve.wait_ge(attn_full, g)
                            dve.tensor_copy(pT[:, 2 * p, 0:t + 1, t * P:(t + 1) * P],
                                            bank[4][:, 0:width(t)].rearrange("p (k q) -> p k q", q=P))\
                                .then_inc(pT_out_dve, 1)

                @block.scalar
                def _(act):
                    for n in range(N + LAG + 1):
                        if n < N:
                            g, t, p = UNITS[n]
                            for hh in range(2):
                                act.wait_ge(scores_out, 2 * n + hh + 1)
                                pr = probs[:, n % 4, hh, 0:width(t)]
                                act.activation(pr, pr, ACT.Exp, scale=-1.0, bias=nmax[:, n % 4, hh:hh + 1],
                                               accum_out=psums[:, n % 4, hh:hh + 1]).then_inc(exp_done, 1)
                        m = n - LAG
                        if 0 <= m < N:
                            g, t, p = UNITS[m]
                            act.wait_ge(pT_full, 2 * m + 2)
                            if g >= 1:
                                act.wait_ge(attn_full, g)
                            act.activation(pT[:, 2 * p + 1, 0:t + 1, t * P:(t + 1) * P],
                                           bank[5][:, 0:width(t)].rearrange("p (k q) -> p k q", q=P), ACT.Copy)\
                                .then_inc(pT_out_act, 1)
                        if m >= PER_G and m % PER_G == 0:
                            g = m // PER_G - 1
                            act.wait_ge(attn_full, g + 1)
                            act.activation(yT[:, g, :], bank[6][:, :], ACT.Identity,
                                           bias=b_qkv[:, 2 * NC + g:2 * NC + g + 1]).then_inc(attn_out, 1)

                @block.gpsimd
                def _(pool):
                    for n in range(N):
                        g, t, p = UNITS[n]
                        pool.wait_ge(rsum_ready, n + 1)
                        pr = probs[:, n % 4, :, 0:width(t)]
                        pool.tensor_tensor(pr, pr, rsum[:, n % 4, :].rearrange("p (h a) -> p h a", a=1)
                                           .to_broadcast([P, 2, width(t)]), ALU.mult).then_inc(probs_ready, 1)

        o_full, res1 = sem("o_full"), sem("res1")
        ln_var, ln_rstd = sem("ln_var"), sem("ln_rstd")
        ln_done = sem("ln_done")
        t_full, t_out = sem("t_full"), sem("t_out")
        cx_full = sem("cx_full")
        sq_done, poly_done, tanh_done, gelu_done = sem("sq_done"), sem("poly_done"), sem("tanh_done"), sem("gelu_done")
        cy_full, res2 = sem("cy_full"), sem("res2")
        route_full = sem("route_full")
        shift_done, expv_done = sem("shift_done"), sem("expv_done")
        mask_done = sem("mask_done")
        pos_full = sem("pos_full")
        w_done, idx_done = sem("w_done"), sem("idx_done")
        scattered = ctx.enter_context(nc.semaphore("l0_scattered"))
        scatter_over = sem("scatter_over")
        sg_full = sem("sg_full")
        stanh_done, hid_done, hid_mid = sem("stanh_done"), sem("hid_done"), sem("hid_mid")
        sd_full, acc_done = sem("sd_full"), sem("acc_done")
        stored = sem("stored")
        chain_p3 = sem("chain_p3")

        def tail(b):
            with nc.Block() as block:
                @block.tensor
                def _(pe):
                    for t in range(NT):
                        for c in range(NC):
                            mm = pe.matmul(bank[t][:, :], yT[:, c, t * P:(t + 1) * P], w_proj[:, c, :],
                                           start=(c == 0), stop=(c == NC - 1))
                        mm.then_inc(o_full, 1)
                    for t in range(NT):
                        pe.wait_ge(ln_done, t + 1)
                        for c in range(NC):
                            mm = pe.transpose(bank[4 + t][:, c * P:(c + 1) * P], x[:, t, c * P:(c + 1) * P], ident[:, :])
                        mm.then_inc(t_full, 1)
                    pe.wait_ge(t_out, NT)
                    for c in range(NC):
                        mm = pe.matmul(bank[0][0:S2, :], ctx_T[:, c, :], x1T[:, c, :], start=(c == 0), stop=(c == NC - 1))
                    mm.then_inc(cx_full, 1)
                    pe.wait_ge(gelu_done, 1)
                    for t in range(NT):
                        pe.matmul(bank[4 + t][:, :], gelu_out[:, t * P:(t + 1) * P], ctx_rows[:, :],
                                  start=True, stop=True).then_inc(cy_full, 1)
                    for t in range(NT):
                        pe.wait_ge(ln_done, NT + t + 1)
                        for c in range(NC):
                            mm = pe.transpose(bank[t][:, c * P:(c + 1) * P], x2w[:, t, c * P:(c + 1) * P], ident[:, :])
                        mm.then_inc(t_full, 1)
                    pe.wait_ge(t_out, 2 * NT)
                    for t in range(NT):
                        for c in range(NC):
                            mm = pe.matmul(bank[4][:, t * E:(t + 1) * E], x2T[:, c, t * P:(t + 1) * P],
                                           w_router[:, c, :], start=(c == 0), stop=(c == NC - 1))
                    mm.then_inc(route_full, 1)

                    def gate_up(f):
                        if f >= 2:
                            pe.wait_ge(hid_done, f - 1)
                        for half in range(2):
                            at = half * F + f * P
                            for c in range(NC):
                                mm = pe.matmul(bank[2 * (f % 2) + half][:, :], w_sgu[:, c, at:at + P], x2T[:, c, :],
                                               start=(c == 0), stop=(c == NC - 1))
                            mm.then_inc(sg_full, 1)

                    gate_up(0)
                    gate_up(1)
                    pe.wait_ge(mask_done, NT)
                    for t in range(NT):
                        pe.matmul(bank[5][:, t * E:(t + 1) * E], upper_b[:, :], mask_b[:, t, :], start=True, stop=False)
                        mm = pe.matmul(bank[5][:, t * E:(t + 1) * E], ones_b[:, :], run[:, t, :], start=False, stop=True)
                    mm.then_inc(pos_full, 1)
                    gate_up(2)
                    pe.wait_ge(hid_done, NF)
                    for t in range(NT):
                        out = bank[(2, 3, 6, 7)[t]]
                        for f in range(NF):
                            mm = pe.matmul(out[:, :], hid[:, f, t * P:(t + 1) * P], w_sdown[:, f, :],
                                           start=(f == 0), stop=(f == NF - 1))
                        mm.then_inc(sd_full, 1)

                @block.scalar
                def _(act):
                    for t in range(NT):
                        act.wait_ge(t_full, t + 1)
                        act.activation(x1T[:, :, t * P:(t + 1) * P],
                                       bank[4 + t][:, :].rearrange("p (c q) -> p c q", q=P), ACT.Copy).then_inc(t_out, 1)
                    act.wait_ge(cx_full, 1)
                    act.activation(gl[0:S2, :], bank[0][0:S2, :], ACT.Square).then_inc(sq_done, 1)
                    act.wait_ge(poly_done, 1)
                    act.activation(gl[0:S2, :], gl[0:S2, :], ACT.Tanh, scale=GELU_C).then_inc(tanh_done, 1)
                    for t in range(NT):
                        act.wait_ge(t_full, NT + t + 1)
                        act.activation(x2T[:, :, t * P:(t + 1) * P],
                                       bank[t][:, :].rearrange("p (c q) -> p c q", q=P), ACT.Copy).then_inc(t_out, 1)
                    act.wait_ge(shift_done, 1)
                    act.activation(expv[:, :, :], expv[:, :, :], ACT.Exp).then_inc(expv_done, 1)
                    for f in range(NF):
                        act.wait_ge(sg_full, 2 * f + 1)
                        act.activation(hid[:, f, :], bank[2 * (f % 2)][:, :], ACT.Tanh, scale=0.5).then_inc(stanh_done, 1)

                @block.vector
                def _(dve):
                    link = chain_of(dve, chain_p3)

                    def normalise(k, src, dst):
                        for t in range(NT):
                            dve.bn_stats(stats[:, t, :], src(t)).then_inc(chain_p3, 1)
                        link.skip(NT)
                        for t in range(NT):
                            dve.bn_aggr(mv[:, t, :], stats[:, t, :]).then_inc(chain_p3, 1)
                        link.skip(NT)
                        dve.tensor_scalar(vare[:, :], mv[:, :, 1], EPS, None, ALU.add).then_inc(ln_var, 1)
                        dve.wait_ge(ln_rstd, k + 1)
                        for t in range(NT):
                            dve.tensor_scalar(dst(t), src(t), mv[:, t, 0:1], rstd[:, t:t + 1], ALU.subtract, ALU.mult)\
                                .then_inc(ln_done, 1)
                        dve.wait_ge(ln_done, NT * (k + 1))

                    for t in range(NT):
                        dve.wait_ge(o_full, t + 1)
                        dve.tensor_tensor(x[:, t, :], bank[t][:, :], x[:, t, :], ALU.add).then_inc(res1, 1)
                    dve.wait_ge(res1, NT)
                    normalise(0, lambda t: x[:, t, :], lambda t: x[:, t, :])
                    dve.wait_ge(sq_done, 1)
                    link(dve.tensor_scalar(gl[0:S2, :], gl[0:S2, :], GELU_A, 1.0, ALU.mult, ALU.add))
                    dve.tensor_tensor(gl[0:S2, :], gl[0:S2, :], bank[0][0:S2, :], ALU.mult).then_inc(poly_done, 1)
                    dve.wait_ge(tanh_done, 1)
                    dve.scalar_tensor_tensor(out=gelu_out[0:S2, :], in0=gl[0:S2, :], scalar=1.0, in1=bank[0][0:S2, :],
                                             op0=ALU.add, op1=ALU.mult).then_inc(gelu_done, 1)
                    for t in range(NT):
                        dve.wait_ge(cy_full, t + 1)
                        dve.scalar_tensor_tensor(out=x2w[:, t, 0:D], in0=bank[4 + t][:, :], scalar=0.5, in1=x[:, t, :],
                                                 op0=ALU.mult, op1=ALU.add).then_inc(res2, 1)
                    dve.wait_ge(res2, NT)
                    normalise(1, lambda t: x2w[:, t, 0:D], lambda t: x2w[:, t, 0:D])

                    def over(a, n=E):
                        return a.rearrange("p (t o) -> p t o", o=1).to_broadcast([P, NT, n])

                    dve.wait_ge(route_full, 1)
                    logits = bank[4][:, 0:NT * E].rearrange("p (t e) -> p t e", e=E)
                    link(dve.tensor_reduce(nmx[:, :], logits, AX.X, ALU.max))
                    dve.tensor_tensor(expv[:, :, :], logits, over(nmx[:, :]), ALU.subtract).then_inc(shift_done, 1)
                    dve.wait_ge(expv_done, 1)
                    for t in range(NT):
                        dve.max(m8[:, t, :], expv[:, t, :]).then_inc(chain_p3, 1)
                    link.skip(NT)
                    for t in range(NT):
                        dve.match_replace(left[:, t, :], m8[:, t, :], expv[:, t, :], -1.0).then_inc(chain_p3, 1)
                    link.skip(NT)
                    link(dve.tensor_scalar(mask[:, :, :], left[:, :, :], -1.0, None, ALU.is_equal))
                    link(dve.tensor_copy(mask_b[:, :, :], mask[:, :, :]))
                    for t in range(NT):
                        dve.tensor_tensor(run[:, t + 1, :], run[:, t, :], mask_b[:, t, :], ALU.add).then_inc(mask_done, 1)
                        dve.wait_ge(mask_done, t + 1)
                    link(dve.tensor_tensor(expv[:, :, :], expv[:, :, :], mask[:, :, :], ALU.mult))
                    link(dve.tensor_reduce(wsum[:, :], expv[:, :, :], AX.X, ALU.add))
                    link(dve.reciprocal(wsum[:, :], wsum[:, :]))
                    dve.tensor_tensor(x2w[:, :, D:XW], expv[:, :, :], over(wsum[:, :]), ALU.mult).then_inc(w_done, 1)

                    def hidden(f):
                        dve.wait_ge(stanh_done, f + 1)
                        dve.scalar_tensor_tensor(out=hid[:, f, :], in0=hid[:, f, :], scalar=1.0, in1=bank[2 * (f % 2)][:, :],
                                                 op0=ALU.add, op1=ALU.mult).then_inc(hid_mid, 1)
                        dve.wait_ge(sg_full, 2 * f + 2)
                        dve.wait_ge(hid_mid, f + 1)
                        dve.tensor_tensor(hid[:, f, :], hid[:, f, :], bank[2 * (f % 2) + 1][:, :], ALU.mult).then_inc(hid_done, 1)

                    hidden(0)
                    hidden(1)
                    dve.wait_ge(pos_full, 1)
                    pos = bank[5][:, 0:NT * E].rearrange("p (t e) -> p t e", e=E)
                    link(dve.scalar_tensor_tensor(out=left[:, :, :], in0=pos, scalar=float(CAP), in1=mask[:, :, :],
                                                  op0=ALU.is_lt, op1=ALU.mult))
                    link(dve.tensor_tensor(enc[:, :, :], pos, slot1[:, :].rearrange("p (o e) -> p o e", o=1)
                                           .to_broadcast([P, NT, E]), ALU.add))
                    link(dve.tensor_tensor(enc[:, :, :], enc[:, :, :], left[:, :, :], ALU.mult))
                    for t in range(NT):
                        dve.max(m8[:, t, :], enc[:, t, :]).then_inc(chain_p3, 1)
                    link.skip(NT)
                    flat = m8[:, :, :].rearrange("p t k -> p (t k)")
                    link(dve.tensor_scalar(off[:, :], flat, 0.5, float(4 * E * CAP), ALU.is_lt, ALU.mult))
                    dve.tensor_tensor(idx[:, :], off[:, :], flat, ALU.add).then_inc(idx_done, 1)
                    link(dve.tensor_copy(run[:, 0, :], run[:, NT, :]))
                    hidden(2)
                    for t in range(NT):
                        dve.wait_ge(sd_full, t + 1)
                        dve.scalar_tensor_tensor(out=acc[:, t, :], in0=bank[(2, 3, 6, 7)[t]][:, :], scalar=0.5,
                                                 in1=x2w[:, t, 0:D], op0=ALU.mult, op1=ALU.add).then_inc(acc_done, 1)
                    dve.wait_ge(scattered, b * (16 * NT * TOPK) + 16 * NT * TOPK)
                    dve.tensor_scalar(tok[:, :], tok[:, :], float(S), None, ALU.add)

                @block.gpsimd
                def _(pool):
                    for k in range(2):
                        pool.wait_ge(ln_var, k + 1)
                        pool.tensor_tensor(rstd[:, :], vare[:, :], cst["mhalf"][:, 0:NT], ALU.pow).then_inc(ln_rstd, 1)
                    pool.wait_ge(idx_done, 1)
                    for k in range(NT * TOPK):
                        pool.indirect_dma_start(
                            out=scr["slots"][:, :], out_offset=bass.IndirectOffsetOnAxis(ap=idx[:, k:k + 1], axis=0),
                            in_=tok[:, k // TOPK:k // TOPK + 1], in_offset=None,
                            bounds_check=E * CAP, oob_is_err=False).then_inc(scattered, 16)
                    pool.wait_ge(scattered, b * (16 * NT * TOPK) + 16 * NT * TOPK)
                    pool.sem_inc(scatter_over, 1)

                @block.sync
                def _(sp):
                    sp.wait_ge(w_done, 1)
                    sp.dma_start(scr["rows"][0:T, :].rearrange("(b t p) n -> b p t n", p=P, t=NT)[b], x2w[:, :, :])\
                        .then_inc(stored, 16)
                    sp.wait_ge(acc_done, NT)
                    sp.dma_start(scr["acc"][0:T, :].rearrange("(b t p) n -> b p t n", p=P, t=NT)[b], acc[:, :, :])\
                        .then_inc(stored, 16)
                    sp.wait_ge(stored, 32)

        with nc.Fori(0, trips) as b:
            project_and_gate(b)
            heads()
            tail(b)
            with nc.Block() as block:
                @block.vector
                def _(dve):
                    for s in sems:
                        dve.sem_clear(s)


def constants(nc, ctx):
    def sb(name, shape, dt=FP32):
        return ctx.enter_context(nc.sbuf_tensor("cst_" + name, shape, dt))
    cst = {"ident": sb("ident", [P, P]), "upper": sb("upper", [P, P]), "ones": sb("ones", [P, P]),
           "upper_b": sb("upper_b", [P, P], BF16), "ones_b": sb("ones_b", [P, P], BF16), "mhalf": sb("mhalf", [P, NT]),
           "groups": sb("groups", [P, DH])}
    made = ctx.enter_context(nc.semaphore("constants_made"))
    with nc.Block() as block:
        @block.gpsimd
        def _(pool):
            pool.memset(cst["ones"][:, :], 1.0).then_inc(made, 1)
            pool.memset(cst["ones_b"][:, :], 1.0).then_inc(made, 1)
            pool.memset(cst["mhalf"][:, :], -0.5).then_inc(made, 1)
            pool.wait_ge(made, 3)
            for name, src, op in (("ident", "ones", ALU.is_equal), ("upper", "ones", ALU.is_gt),
                                  ("upper_b", "ones_b", ALU.is_gt)):
                pool.affine_select(out=cst[name][:, :], in_=cst[src][:, :], pattern=[[1, P]], compare_op=op,
                                   fill=0.0, base=0, channel_multiplier=-1).then_inc(made, 1)
            pool.wait_ge(made, 6)
    return cst


def experts_stage(nc, A, scr, cst):
    ident = cst["ident"]
    with ExitStack() as ctx:
        def sb(name, shape, dt=FP32):
            return ctx.enter_context(nc.sbuf_tensor("moe_" + name, shape, dt))

        def sem(name):
            return ctx.enter_context(nc.semaphore("moe_" + name))

        bank = [ctx.enter_context(nc.psum_tensor(f"moe_bank{i}", [P, 512], FP32)) for i in range(8)]
        NI = E // 2
        lists = sb("lists", [P, P])
        listsT = sb("listsT", [P, E * NJ])
        w_gu = [sb(f"w_gu{s}", [P, NC, 2 * F]) for s in range(2)]
        w_dn = [sb(f"w_dn{s}", [P, NF, D]) for s in range(2)]
        rows = [sb(f"rows{s}", [P, NJ, XW]) for s in range(2)]
        rowsT = [sb(f"rowsT{s}", [P, NC, CAP]) for s in range(2)]
        hid = [sb(f"hid{s}", [P, NF, CAP]) for s in range(2)]
        y = [sb(f"y{s}", [P, NJ, D]) for s in range(2)]
        gidx = [sb(f"gidx{s}", [P, NJ], I32) for s in range(2)]
        sidx = [sb(f"sidx{s}", [P, NJ], I32) for s in range(2)]
        wcur = [sb(f"wcur{s}", [P, NJ]) for s in range(2)]

        lists_in, lists_t, lists_out = sem("lists_in"), sem("lists_t"), sem("lists_out")
        gu_in = [sem(f"gu_in{s}") for s in range(2)]
        dn_in = [sem(f"dn_in{s}") for s in range(2)]
        gidx_ready, sidx_ready = sem("gidx_ready"), sem("sidx_ready")
        gathered = [sem(f"gathered{s}") for s in range(2)]
        t_full = sem("t_full")
        t_act, t_dve = sem("t_act"), sem("t_dve")
        w_taken = sem("w_taken")
        gu_full = sem("gu_full")
        tanh_done, hid_mid, hid_done = sem("tanh_done"), sem("hid_mid"), sem("hid_done")
        dn_full = sem("dn_full")
        y_done = sem("y_done")
        may_move = sem("may_move")
        added = sem("added")

        with nc.Block() as block:
            @block.sync
            def _(sp):
                sp.dma_start(lists[:, :], scr["slots"][1:E * CAP + 1, :].rearrange("(r n) o -> r (n o)", n=P))\
                    .then_inc(lists_in, 16)
                sp.wait_ge(lists_in, 16)

            @block.tensor
            def _(pe):
                pe.wait_ge(lists_in, 16)
                pe.transpose(bank[0][:, 0:P], lists[:, :], ident[:, :]).then_inc(lists_t, 1)

            @block.vector
            def _(dve):
                dve.wait_ge(lists_t, 1)
                dve.tensor_copy(listsT[:, :], bank[0][:, 0:P]).then_inc(lists_out, 1)
                dve.wait_ge(lists_out, 1)

        def over_pairs(eng, step):
            for s in range(2):
                step(s, s, 0, True, False)
            with eng.Fori(1, NI - 1) as i:
                for s in range(2):
                    step(i * 2 + s, s, i, False, False)
            for s in range(2):
                step(E - 2 + s, s, NI - 1, False, True)

        with nc.Block() as block:
            @block.sync
            def _(sp):
                def step(e, s, i, first, last):
                    if not first:
                        sp.wait_ge(gu_full, e * NF - NF)
                    sp.dma_start(w_gu[s][:, :, 0:F], A["w_gate"][e].rearrange("(c p) n -> p c n", p=P)).then_inc(gu_in[s], 16)
                    sp.dma_start(w_gu[s][:, :, F:2 * F], A["w_up"][e].rearrange("(c p) n -> p c n", p=P)).then_inc(gu_in[s], 16)
                    if not first:
                        sp.wait_ge(dn_full, e * NJ - NJ)
                    sp.dma_start(w_dn[s][:, :, :], A["w_down"][e].rearrange("(c p) n -> p c n", p=P)).then_inc(dn_in[s], 16)
                over_pairs(sp, step)

            @block.tensor
            def _(pe):
                def transposes(e, s, i, start=False):
                    pe.wait_ge(gathered[s], i * 32 + 32)
                    for j in range(NJ):
                        if not start:
                            pe.wait_ge(t_dve if j else t_act, e)
                        for c in range(NC):
                            mm = pe.transpose(bank[j][:, c * P:(c + 1) * P], rows[s][:, j, c * P:(c + 1) * P], ident[:, :])
                        mm.then_inc(t_full, 1)

                def down(e, s, i, start=False):
                    pe.wait_ge(dn_in[s], i * 16 + 16)
                    pe.wait_ge(hid_done, e * NF + NF)
                    for j in range(NJ):
                        if not start:
                            pe.wait_ge(y_done, e * NJ - NJ + j + 1)
                        for f in range(NF):
                            mm = pe.matmul(bank[5 + j][:, :], hid[s][:, f, j * P:(j + 1) * P], w_dn[s][:, f, :],
                                           start=(f == 0), stop=(f == NF - 1))
                        mm.then_inc(dn_full, 1)

                def step(e, s, i, first, last):
                    pe.wait_ge(gu_in[s], i * 32 + 32)
                    pe.wait_ge(t_act, e + 1)
                    pe.wait_ge(t_dve, e + 1)
                    for f in range(NF):
                        if not (first and s == 0):
                            pe.wait_ge(hid_done, e * NF - NF + f + 1)
                        for half in range(2):
                            for c in range(NC):
                                at = half * F + f * P
                                mm = pe.matmul(bank[2 + f][:, half * CAP:(half + 1) * CAP], w_gu[s][:, c, at:at + P],
                                               rowsT[s][:, c, :], start=(c == 0), stop=(c == NC - 1))
                        mm.then_inc(gu_full, 1)
                    if not (last and s == 1):
                        transposes(e + 1, 1 - s, i + s)
                    if not (first and s == 0):
                        down(e - 1, 1 - s, i + s - 1, start=(first and s == 1))

                transposes(0, 0, 0, start=True)
                over_pairs(pe, step)
                down(E - 1, 1, NI - 1)

            @block.scalar
            def _(act):
                def turn(e, s, first):
                    act.wait_ge(t_full, e * NJ + 1)
                    if not first:
                        act.wait_ge(gu_full, e * NF - NF)
                    act.activation(rowsT[s][:, :, 0:P], bank[0][:, :].rearrange("p (c q) -> p c q", q=P), ACT.Copy)\
                        .then_inc(t_act, 1)

                def out(e, s, first):
                    for j in range(NJ):
                        act.wait_ge(dn_full, e * NJ + j + 1)
                        if not first:
                            act.wait_ge(added, e * 32 - 32)
                        act.activation(y[s][:, j, :], bank[5 + j][:, :], ACT.Copy, scale=wcur[s][:, j:j + 1])\
                            .then_inc(y_done, 1)

                def step(e, s, i, first, last):
                    for f in range(NF):
                        act.wait_ge(gu_full, e * NF + f + 1)
                        if not first:
                            act.wait_ge(dn_full, e * NJ - NJ)
                        act.activation(hid[s][:, f, :], bank[2 + f][:, 0:CAP], ACT.Tanh, scale=0.5).then_inc(tanh_done, 1)
                    if not (last and s == 1):
                        turn(e + 1, 1 - s, first and s == 0)
                    if not (first and s == 0):
                        act.wait_ge(w_taken, e)
                        out(e - 1, 1 - s, (first and s == 1))

                turn(0, 0, True)
                over_pairs(act, step)
                out(E - 1, 1, False)

            @block.vector
            def _(dve):
                def prepare(e, s, i, first):
                    dve.wait_ge(t_full, e * NJ + 2)
                    if not first:
                        dve.wait_ge(gu_full, e * NF - NF)
                    dve.tensor_copy(rowsT[s][:, :, P:2 * P], bank[1][:, :].rearrange("p (c q) -> p c q", q=P))\
                        .then_inc(t_dve, 1)
                    if not first:
                        dve.wait_ge(y_done, e * NJ - NJ)
                        dve.wait_ge(added, e * 32 - 32)
                    dve.tensor_scalar(wcur[s][:, :], rows[s][:, :, bass.ds(e + D, 1)].rearrange("p j o -> p (j o)"),
                                      0.5, None, ALU.mult).then_inc(w_taken, 1)
                    dve.tensor_copy(sidx[s][:, :], listsT[:, bass.ds(e * NJ, NJ)]).then_inc(sidx_ready, 1)

                def gather_list(e, s):
                    dve.tensor_copy(gidx[s][:, :], listsT[:, bass.ds(e * NJ, NJ)]).then_inc(gidx_ready, 1)

                def step(e, s, i, first, last):
                    for f in range(NF):
                        dve.wait_ge(tanh_done, e * NF + f + 1)
                        dve.scalar_tensor_tensor(out=hid[s][:, f, :], in0=hid[s][:, f, :], scalar=1.0,
                                                 in1=bank[2 + f][:, 0:CAP], op0=ALU.add, op1=ALU.mult).then_inc(hid_mid, 1)
                        dve.wait_ge(hid_mid, e * NF + f + 1)
                        dve.tensor_tensor(hid[s][:, f, :], hid[s][:, f, :], bank[2 + f][:, CAP:2 * CAP], ALU.mult)\
                            .then_inc(hid_done, 1)
                    if not last:
                        dve.wait_ge(gathered[s], i * 32 + 32)
                        gather_list(e + 2, s)
                    if not (last and s == 1):
                        prepare(e + 1, 1 - s, i + s, first and s == 0)

                gather_list(0, 0)
                gather_list(1, 1)
                prepare(0, 0, 0, True)
                over_pairs(dve, step)

            @block.gpsimd
            def _(pool):
                def gather(e, s):
                    pool.wait_ge(gidx_ready, e + 1)
                    pool.sem_inc(may_move, 1)
                    for j in range(NJ):
                        pool.indirect_dma_start(
                            out=rows[s][:, j, :], out_offset=None, in_=scr["rows"][:, :],
                            in_offset=bass.IndirectOffsetOnAxis(ap=gidx[s][:, j:j + 1], axis=0)).then_inc(gathered[s], 16)

                def step(e, s, i, first, last):
                    if not last:
                        pool.wait_ge(t_full, e * NJ + NJ)
                        pool.wait_ge(w_taken, e + 1)
                        gather(e + 2, s)
                    if not (first and s == 0):
                        pool.wait_ge(added, e * 32)
                    pool.wait_ge(y_done, e * NJ + NJ)
                    pool.wait_ge(sidx_ready, e + 1)
                    pool.sem_inc(may_move, 1)
                    for j in range(NJ):
                        pool.indirect_dma_start(
                            out=scr["acc"][:, :], out_offset=bass.IndirectOffsetOnAxis(ap=sidx[s][:, j:j + 1], axis=0),
                            in_=y[s][:, j, :], in_offset=None, compute_op=ALU.add).then_inc(added, 16)

                gather(0, 0)
                gather(1, 1)
                over_pairs(pool, step)
                pool.wait_ge(added, E * 32)


def layer1_attention_stage(nc, A, scr, cst, trips):
    ident = cst["ident"]
    with ExitStack() as ctx:
        def sb(name, shape, dt=FP32):
            return ctx.enter_context(nc.sbuf_tensor("l1_" + name, shape, dt))

        sems = []

        def sem(name):
            s = ctx.enter_context(nc.semaphore("l1_" + name))
            sems.append(s)
            return s

        psum = ctx.enter_context(nc.psum_tensor("l1_psum", [P, 8, 512], FP32))
        bank = [psum[:, i, :] for i in range(8)]

        w_qkv = sb("w_qkv", [P, NC, 3 * D])
        w_o = sb("w_o", [P, NC, D])
        w_xo = sb("w_xo", [P, NC, D])
        w_xdiag = sb("w_xdiag", [P, 3, P])
        w_conv = sb("w_conv", [P, 2, NC, DH])
        wcol = sb("wcol", [P, 2, NC])
        b_conv = sb("b_conv", [P, 2])
        b_qkv = sb("b_qkv", [P, 3 * NC])
        b_o = sb("b_o", [P, D])
        b_xo = sb("b_xo", [P, D])
        x = sb("x", [P, NT, D])
        xT = sb("xT", [P, NC, S])
        qT = sb("qT", [P, NC, S])
        kpad = sb("kpad", [P, H, S])
        v = sb("v", [P, NT, D])
        probs = sb("probs", [P, 4, 2, S])
        pT = sb("pT", [P, HG, NT, S])
        yT = xT
        x4T, qxT, yxT, x5T = qT, v, qT, xT
        ctx_T = sb("ctx_T", [P, NC, S2])
        kxpad = sb("kxpad", [P, H, S2])
        vx = sb("vx", [P, D])
        pxT = pT[:, :, :, :].rearrange("p a b s -> p (a b) s")
        seen = sb("seen", [P, NT, S2], I32)
        floor = sb("floor", [P, NT, S2])
        px = [probs[:, i, 0, 0:HG * S2].rearrange("p (h k) -> p h k", h=HG) for i in range(4)]
        xc = probs[:, 0, :, :]
        nmax = sb("nmax", [P, 4, 2])
        psums = sb("psums", [P, 4, 2])
        rsum = sb("rsum", [P, 4, 2])
        xmax = sb("xmax", [P, 4, HG])
        xsum = sb("xsum", [P, 4, HG])
        xrsum = sb("xrsum", [P, 4, HG])
        stats = sb("stats", [P, NT, 6])
        mv = sb("mv", [P, NT, 2])
        vare = sb("vare", [P, NT])
        rstd = sb("rstd", [P, NT])

        setup_in, setup_zero, setup_conv = sem("setup_in"), sem("setup_zero"), sem("setup_conv")
        with nc.Block() as block:
            @block.sync
            def _(sp):
                for dst, src in ((w_qkv, A["w_qkv1"]), (w_o, A["w_o1"]), (w_xo, A["w_xo"])):
                    sp.dma_start(dst[:, :, :], src.rearrange("(c p) n -> p c n", p=P)).then_inc(setup_in, 16)
                sp.dma_start(b_qkv[:, :], A["b_qkv1"]).then_inc(setup_in, 16)
                for dst, src in ((b_o, A["b_o1"]), (b_xo, A["b_xo"])):
                    sp.dma_start(dst[:, :], src.rearrange("(a n) -> a n", a=1).to_broadcast([P, D])).then_inc(setup_in, 16)
                sp.dma_start(wcol[:, :, :], A["conv_w"]).then_inc(setup_in, 16)
                sp.dma_start(b_conv[:, :], A["conv_b"]).then_inc(setup_in, 16)
                sp.wait_ge(setup_zero, 1)
                for i in range(3):
                    for h in range(HG):
                        sp.dma_start(w_xdiag[h * DH:(h + 1) * DH, i, h * DH:(h + 1) * DH], A["w_x"][i])\
                            .then_inc(setup_in, 16)
                sp.wait_ge(setup_in, (8 + 3 * HG) * 16)

            @block.vector
            def _(dve):
                dve.memset(w_xdiag[:, :, :], 0.0).then_inc(setup_zero, 1)
                dve.memset(kpad[:, :, :], 0.0)
                dve.memset(kxpad[:, :, :], 0.0)
                dve.memset(vx[:, :], 0.0)
                dve.wait_ge(setup_in, (8 + 3 * HG) * 16)
                dve.tensor_scalar(b_qkv[:, 0:NC], b_qkv[:, 0:NC], QSCALE, None, ALU.mult)
                dve.wait_ge(setup_conv, 2)
                for br in range(2):
                    for c in range(NC):
                        dve.tensor_scalar(w_conv[:, br, c, :], cst["groups"][:, :], wcol[:, br, c:c + 1], None, ALU.mult)

            @block.gpsimd
            def _(pool):
                pool.affine_select(out=cst["groups"][:, :], in_=cst["ones"][:, 0:DH], pattern=[[-4, DH]],
                                   compare_op=ALU.is_ge, fill=0.0, base=0, channel_multiplier=1).then_inc(setup_conv, 1)
                pool.wait_ge(setup_conv, 1)
                pool.affine_select(out=cst["groups"][:, :], in_=cst["groups"][:, :], pattern=[[4, DH]],
                                   compare_op=ALU.is_ge, fill=0.0, base=3, channel_multiplier=-1).then_inc(setup_conv, 1)

        ln_var, ln_rstd, ln_done = sem("ln_var"), sem("ln_rstd"), sem("ln_done")
        chain_ln = sem("chain_ln")

        def normalise(dve, link, k, src, dst):
            for t in range(NT):
                dve.bn_stats(stats[:, t, :], src(t)).then_inc(chain_ln, 1)
            link.skip(NT)
            for t in range(NT):
                dve.bn_aggr(mv[:, t, :], stats[:, t, :]).then_inc(chain_ln, 1)
            link.skip(NT)
            dve.tensor_scalar(vare[:, :], mv[:, :, 1], EPS, None, ALU.add).then_inc(ln_var, 1)
            dve.wait_ge(ln_rstd, k + 1)
            for t in range(NT):
                dve.tensor_scalar(dst(t), src(t), mv[:, t, 0:1], rstd[:, t:t + 1], ALU.subtract, ALU.mult)\
                    .then_inc(ln_done, 1)
            dve.wait_ge(ln_done, NT * (k + 1))

        def reciprocal_root(pool, k):
            pool.wait_ge(ln_var, k + 1)
            pool.tensor_tensor(rstd[:, :], vare[:, :], cst["mhalf"][:, 0:NT], ALU.pow).then_inc(ln_rstd, 1)

        loaded, turned, turned_out = sem("loaded"), sem("turned"), sem("turned_out")
        floor_done, resid = sem("floor_done"), sem("resid")
        proj_full, proj_drained = sem("proj_full"), sem("proj_drained")
        PROJ = [("q", 0), ("k", 0), ("v", 0), ("v", 1), ("v", 2), ("v", 3), ("q", 1), ("k", 1),
                ("q", 2), ("k", 2), ("q", 3), ("k", 3), ("kx", 0), ("vx", 0)]

        def project(b):
            with nc.Block() as block:
                @block.sync
                def _(sp):
                    sp.dma_start(x[:, :, :], scr["acc"][0:T, :].rearrange("(b t p) n -> b p t n", p=P, t=NT)[b])\
                        .then_inc(loaded, 16)
                    sp.dma_start(ctx_T[:, :, :], A["ctxT"][b].rearrange("(c p) n -> p c n", p=P)).then_inc(loaded, 16)
                    sp.dma_start(seen[:, :, :], A["mask"][b].rearrange("(t p) n -> p t n", p=P)).then_inc(loaded, 16)
                    sp.wait_ge(loaded, 48)

                @block.tensor
                def _(pe):
                    for t in range(NT):
                        pe.wait_ge(ln_done, t + 1)
                        for c in range(NC):
                            mm = pe.transpose(bank[4 + t][:, c * P:(c + 1) * P], x[:, t, c * P:(c + 1) * P], ident[:, :])
                        mm.then_inc(turned, 1)
                    pe.wait_ge(turned_out, NT)
                    for j, (kind, i) in enumerate(PROJ):
                        if j >= 4:
                            pe.wait_ge(proj_drained, j - 3)
                        out = bank[j % 4]
                        if kind == "kx":
                            for c in range(NC):
                                mm = pe.matmul(out[:, c * S2:(c + 1) * S2], w_xdiag[:, 1, :], ctx_T[:, c, :],
                                               start=True, stop=True)
                        elif kind == "vx":
                            for c in range(NC):
                                mm = pe.matmul(out[0:S2, c * P:(c + 1) * P], ctx_T[:, c, :], w_xdiag[:, 2, :],
                                               start=True, stop=True)
                        else:
                            for c in range(NC):
                                if kind == "v":
                                    mm = pe.matmul(out, xT[:, c, i * P:(i + 1) * P], w_qkv[:, c, 2 * D:3 * D],
                                                   start=(c == 0), stop=(c == NC - 1))
                                else:
                                    at = i * P + (D if kind == "k" else 0)
                                    mm = pe.matmul(out, w_qkv[:, c, at:at + P], xT[:, c, :],
                                                   start=(c == 0), stop=(c == NC - 1))
                        mm.then_inc(proj_full, 1)

                @block.scalar
                def _(act):
                    for t in range(NT):
                        act.wait_ge(turned, t + 1)
                        act.activation(xT[:, :, t * P:(t + 1) * P], bank[4 + t].rearrange("p (c q) -> p c q", q=P),
                                       ACT.Copy).then_inc(turned_out, 1)
                    for j, (kind, i) in enumerate(PROJ):
                        act.wait_ge(proj_full, j + 1)
                        src = bank[j % 4]
                        if kind == "q":
                            last = act.activation(qT[:, i, :], src, ACT.Identity, scale=QSCALE, bias=b_qkv[:, i:i + 1])
                        elif kind == "k":
                            for h in range(HG):
                                r = slice(h * DH, (h + 1) * DH)
                                last = act.activation(kpad[r, i * HG + h, :], psum[r, j % 4, :], ACT.Identity,
                                                      bias=b_qkv[r, NC + i:NC + i + 1])
                        elif kind == "v":
                            last = act.activation(v[:, i, :], src, ACT.Copy)
                        elif kind == "kx":
                            for h in range(HG):
                                r = slice(h * DH, (h + 1) * DH)
                                last = act.activation(
                                    kxpad[r, :, :].rearrange("p (c h) k -> p c h k", h=HG)[:, :, h, :],
                                    psum[r, j % 4, 0:NC * S2].rearrange("p (c k) -> p c k", k=S2), ACT.Copy)
                        else:
                            last = act.activation(vx[0:S2, :], psum[0:S2, j % 4, :], ACT.Copy)
                        last.then_inc(proj_drained, 1)

                @block.gpsimd
                def _(pool):
                    reciprocal_root(pool, 0)
                    pool.wait_ge(turned, NT)
                    for t in range(NT):
                        pool.tensor_tensor(x[:, t, :], x[:, t, :], b_o[:, :], ALU.add).then_inc(resid, 1)

                @block.vector
                def _(dve):
                    link = chain_of(dve, chain_ln)
                    dve.wait_ge(loaded, 48)
                    normalise(dve, link, 0, lambda t: x[:, t, :], lambda t: x[:, t, :])
                    link(dve.tensor_scalar(floor[:, :, :], seen[:, :, :], 0.0, -TAKEN, ALU.not_equal, ALU.mult))
                    link(dve.tensor_scalar(floor[:, :, :], floor[:, :, :], 1e20, None, ALU.subtract))
                    links["n"] = link

        links = {}
        scores_full, max_ready, exp_done = sem("scores_full"), sem("max_ready"), sem("exp_done")
        rsum_ready, probs_ready = sem("rsum_ready"), sem("probs_ready")
        pT_full, pT_out_dve, pT_out_act = sem("pT_full"), sem("pT_out_dve"), sem("pT_out_act")
        attn_full, attn_out = sem("attn_full"), sem("attn_out")
        LAG = 3
        UNITS = [(g, t, p) for g in range(NC) for t in range(NT) for p in range(2)]
        PER_G = 2 * NT

        def heads():
            N = len(UNITS)
            with nc.Block() as block:
                @block.tensor
                def _(pe):
                    for n in range(N + LAG + 1):
                        if n < N:
                            g, t, p = UNITS[n]
                            if n >= 2:
                                pe.wait_ge(exp_done, 2 * (n - 1))
                            for hh in range(2):
                                mm = pe.matmul(bank[2 * (n % 2) + hh], qT[:, g, t * P:(t + 1) * P],
                                               kpad[:, HG * g + 2 * p + hh, :], start=True, stop=True)
                            mm.then_inc(scores_full, 1)
                        m = n - LAG
                        if m >= PER_G and m % PER_G == 0:
                            g = m // PER_G - 1
                            pe.wait_ge(pT_out_dve, m)
                            pe.wait_ge(pT_out_act, m)
                            if g >= 1:
                                pe.wait_ge(attn_out, g)
                            for kc in range(NT):
                                for h in range(HG):
                                    mm = pe.matmul(psum[h * DH:(h + 1) * DH, 6, :],
                                                   v[:, kc, (HG * g + h) * DH:(HG * g + h + 1) * DH],
                                                   pT[:, h, kc, :], start=(kc == 0), stop=(kc == NT - 1))
                            mm.then_inc(attn_full, 1)
                        if 0 <= m < N:
                            pe.wait_ge(probs_ready, m + 1)
                            for hh in range(2):
                                if m >= 1:
                                    pe.wait_ge(pT_out_act if hh else pT_out_dve, m)
                                for kc in range(NT):
                                    mm = pe.transpose(bank[4 + hh][:, kc * P:(kc + 1) * P],
                                                      probs[:, m % 4, hh, kc * P:(kc + 1) * P], ident[:, :])
                                mm.then_inc(pT_full, 1)

                @block.vector
                def _(dve):
                    for n in range(N + LAG):
                        if n < N:
                            dve.wait_ge(scores_full, n + 1)
                            if n >= 4:
                                dve.wait_ge(exp_done, 2 * (n - 3))
                            dve.tensor_reduce(nmax[:, n % 4, :], psum[:, 2 * (n % 2):2 * (n % 2) + 2, :], AX.X, ALU.max,
                                              negate=True).then_inc(max_ready, 1)
                        m = n - 1
                        if 0 <= m < N:
                            dve.wait_ge(exp_done, 2 * m + 2)
                            if m >= 4:
                                dve.wait_ge(probs_ready, m - 3)
                            dve.reciprocal(rsum[:, m % 4, :], psums[:, m % 4, :]).then_inc(rsum_ready, 1)
                        m = n - LAG
                        if 0 <= m < N:
                            g, t, p = UNITS[m]
                            dve.wait_ge(pT_full, 2 * m + 1)
                            if g >= 1:
                                dve.wait_ge(attn_full, g)
                            dve.tensor_copy(pT[:, 2 * p, :, t * P:(t + 1) * P],
                                            bank[4].rearrange("p (k q) -> p k q", q=P)).then_inc(pT_out_dve, 1)

                @block.scalar
                def _(act):
                    for n in range(N + LAG + 1):
                        if n < N:
                            act.wait_ge(max_ready, n + 1)
                            if n >= 4:
                                act.wait_ge(pT_full, 2 * (n - 3))
                                act.wait_ge(rsum_ready, n - 3)
                            for hh in range(2):
                                act.activation(probs[:, n % 4, hh, :], bank[2 * (n % 2) + hh], ACT.Exp,
                                               bias=nmax[:, n % 4, hh:hh + 1],
                                               accum_out=psums[:, n % 4, hh:hh + 1]).then_inc(exp_done, 1)
                        m = n - LAG
                        if 0 <= m < N:
                            g, t, p = UNITS[m]
                            act.wait_ge(pT_full, 2 * m + 2)
                            if g >= 1:
                                act.wait_ge(attn_full, g)
                            act.activation(pT[:, 2 * p + 1, :, t * P:(t + 1) * P],
                                           bank[5].rearrange("p (k q) -> p k q", q=P), ACT.Copy).then_inc(pT_out_act, 1)
                        if m >= PER_G and m % PER_G == 0:
                            g = m // PER_G - 1
                            act.wait_ge(attn_full, g + 1)
                            act.activation(yT[:, g, :], bank[6], ACT.Identity,
                                           bias=b_qkv[:, 2 * NC + g:2 * NC + g + 1]).then_inc(attn_out, 1)

                @block.gpsimd
                def _(pool):
                    for n in range(N):
                        pool.wait_ge(rsum_ready, n + 1)
                        pr = probs[:, n % 4, :, :]
                        pool.tensor_tensor(pr, pr, rsum[:, n % 4, :].rearrange("p (h a) -> p h a", a=1)
                                           .to_broadcast([P, 2, S]), ALU.mult).then_inc(probs_ready, 1)

        o_full, res1 = sem("o_full"), sem("res1")
        t_full, t_out = sem("t_full"), sem("t_out")
        qx_full, qx_out = sem("qx_full"), sem("qx_out")
        resid2 = sem("resid2")
        xs_full, xs_out = sem("xs_full"), sem("xs_out")
        xsub_done, xexp_done, xrsum_ready, xprobs_ready = (sem(n) for n in ("xsub", "xexp", "xrsum_ready", "xprobs"))
        xpT_full, xpT_out = sem("xpT_full"), sem("xpT_out")
        xa_full, xa_out = sem("xa_full"), sem("xa_out")
        xo_full, res2 = sem("xo_full"), sem("res2")
        conv_full, conv_out, stored = sem("conv_full"), sem("conv_out"), sem("stored")
        chain_x = sem("chain_x")
        XU = [(g, t) for g in range(NC) for t in range(NT)]
        XLAG = 2

        def tail(b):
            with nc.Block() as block:
                @block.tensor
                def _(pe):
                    for t in range(NT):
                        for c in range(NC):
                            mm = pe.matmul(bank[t], yT[:, c, t * P:(t + 1) * P], w_o[:, c, :],
                                           start=(c == 0), stop=(c == NC - 1))
                        mm.then_inc(o_full, 1)
                    for t in range(NT):
                        pe.wait_ge(ln_done, NT + t + 1)
                        for c in range(NC):
                            mm = pe.transpose(bank[4 + t][:, c * P:(c + 1) * P], x[:, t, c * P:(c + 1) * P], ident[:, :])
                        mm.then_inc(t_full, 1)
                    pe.wait_ge(t_out, NT)
                    for c in range(NC):
                        pe.matmul(bank[c], w_xdiag[:, 0, :], x4T[:, c, :], start=True, stop=True).then_inc(qx_full, 1)
                    N = len(XU)
                    for n in range(N + XLAG + 1):
                        if n < N:
                            g, t = XU[n]
                            pe.wait_ge(qx_out, g + 1)
                            if n >= 2:
                                pe.wait_ge(xs_out, n - 1)
                            pe.matmul(bank[4 + n % 2][:, 0:HG * S2], qxT[:, g, t * P:(t + 1) * P],
                                      kxpad[:, g * HG:(g + 1) * HG, :].rearrange("p h k -> p (h k)"),
                                      start=True, stop=True).then_inc(xs_full, 1)
                        m = n - XLAG
                        if m >= NT and m % NT == 0:
                            g = m // NT - 1
                            pe.wait_ge(xpT_out, m)
                            for h in range(HG):
                                mm = pe.matmul(psum[h * DH:(h + 1) * DH, g, :], vx[:, (g * HG + h) * DH:(g * HG + h + 1) * DH],
                                               pxT[:, g * HG + h, :], start=True, stop=True)
                            mm.then_inc(xa_full, 1)
                        if 0 <= m < N:
                            pe.wait_ge(xprobs_ready, m + 1)
                            if m >= 2:
                                pe.wait_ge(xpT_out, m - 1)
                            for h in range(HG):
                                mm = pe.transpose(bank[6 + m % 2][0:S2, h * P:(h + 1) * P], px[m % 4][:, h, :], ident[:, :])
                            mm.then_inc(xpT_full, 1)
                    pe.wait_ge(xa_out, NC)
                    pe.wait_ge(xs_out, N)
                    pe.wait_ge(xpT_out, N)
                    for t in range(NT):
                        for c in range(NC):
                            mm = pe.matmul(bank[4 + t], yxT[:, c, t * P:(t + 1) * P], w_xo[:, c, :],
                                           start=(c == 0), stop=(c == NC - 1))
                        mm.then_inc(xo_full, 1)
                    for t in range(NT):
                        pe.wait_ge(ln_done, 2 * NT + t + 1)
                        for c in range(NC):
                            mm = pe.transpose(bank[t][:, c * P:(c + 1) * P], x[:, t, c * P:(c + 1) * P], ident[:, :])
                        mm.then_inc(t_full, 1)
                    pe.wait_ge(t_out, 2 * NT)
                    for br in range(2):
                        for c in range(NC):
                            mm = pe.matmul(psum[c * DH:(c + 1) * DH, 4 + br, :], w_conv[:, br, c, :], x5T[:, c, :],
                                           start=True, stop=True)
                        mm.then_inc(conv_full, 1)

                @block.scalar
                def _(act):
                    for t in range(NT):
                        act.wait_ge(t_full, t + 1)
                        act.activation(x4T[:, :, t * P:(t + 1) * P], bank[4 + t].rearrange("p (c q) -> p c q", q=P),
                                       ACT.Copy).then_inc(t_out, 1)
                    for c in range(NC):
                        act.wait_ge(qx_full, c + 1)
                        act.activation(qxT[:, c, :], bank[c], ACT.Copy).then_inc(qx_out, 1)
                    N = len(XU)
                    for n in range(N + XLAG + 1):
                        if n < N:
                            act.wait_ge(xsub_done, n + 1)
                            act.activation(px[n % 4], px[n % 4], ACT.Exp, scale=XSCALE).then_inc(xexp_done, 1)
                        m = n - XLAG
                        if 0 <= m < N:
                            g, t = XU[m]
                            act.wait_ge(xpT_full, m + 1)
                            act.activation(pxT[0:S2, g * HG:(g + 1) * HG, t * P:(t + 1) * P],
                                           psum[0:S2, 6 + m % 2, :].rearrange("p (h q) -> p h q", q=P), ACT.Copy)\
                                .then_inc(xpT_out, 1)
                        if m >= NT and m % NT == 0:
                            g = m // NT - 1
                            act.wait_ge(xa_full, g + 1)
                            act.activation(yxT[:, g, :], bank[g], ACT.Copy).then_inc(xa_out, 1)
                    for t in range(NT):
                        act.wait_ge(t_full, NT + t + 1)
                        act.activation(x5T[:, :, t * P:(t + 1) * P], bank[t].rearrange("p (c q) -> p c q", q=P),
                                       ACT.Copy).then_inc(t_out, 1)
                    for br in range(2):
                        act.wait_ge(conv_full, br + 1)
                        act.activation(xc[:, br, :], bank[4 + br], ACT.Identity, bias=b_conv[:, br:br + 1])\
                            .then_inc(conv_out, 1)

                @block.vector
                def _(dve):
                    link = links["n"]
                    for t in range(NT):
                        dve.wait_ge(o_full, t + 1)
                        dve.tensor_tensor(x[:, t, :], bank[t], x[:, t, :], ALU.add).then_inc(res1, 1)
                    dve.wait_ge(res1, NT)
                    normalise(dve, link, 1, lambda t: x[:, t, :], lambda t: x[:, t, :])
                    xlink = chain_of(dve, chain_x)

                    def each(a):
                        return a.rearrange("p (h o) -> p h o", o=1).to_broadcast([P, HG, S2])

                    N = len(XU)
                    for n in range(N + 1):
                        if n < N:
                            g, t = XU[n]
                            dve.wait_ge(xs_full, n + 1)
                            if n >= 4:
                                dve.wait_ge(xpT_full, n - 3)
                            dve.tensor_tensor(px[n % 4], bank[4 + n % 2][:, 0:HG * S2].rearrange("p (h k) -> p h k", h=HG),
                                              floor[:, t, :].rearrange("p (o k) -> p o k", o=1).to_broadcast([P, HG, S2]),
                                              ALU.min).then_inc(xs_out, 1)
                            dve.wait_ge(xs_out, n + 1)
                            xlink(dve.tensor_reduce(xmax[:, n % 4, :], px[n % 4], AX.X, ALU.max))
                            dve.tensor_tensor(px[n % 4], px[n % 4], each(xmax[:, n % 4, :]), ALU.subtract).then_inc(xsub_done, 1)
                        m = n - 1
                        if 0 <= m < N:
                            dve.wait_ge(xexp_done, m + 1)
                            xlink(dve.tensor_reduce(xsum[:, m % 4, :], px[m % 4], AX.X, ALU.add))
                            if m >= 4:
                                dve.wait_ge(xprobs_ready, m - 3)
                            dve.reciprocal(xrsum[:, m % 4, :], xsum[:, m % 4, :]).then_inc(xrsum_ready, 1)
                    for t in range(NT):
                        dve.wait_ge(xo_full, t + 1)
                        dve.wait_ge(resid2, t + 1)
                        dve.tensor_tensor(x[:, t, :], bank[4 + t], x[:, t, :], ALU.add).then_inc(res2, 1)
                    dve.wait_ge(res2, NT)
                    normalise(dve, link, 2, lambda t: x[:, t, :], lambda t: x[:, t, :])

                @block.gpsimd
                def _(pool):
                    reciprocal_root(pool, 1)
                    N = len(XU)
                    for n in range(N):
                        pool.wait_ge(xrsum_ready, n + 1)
                        pool.tensor_tensor(px[n % 4], px[n % 4], xrsum[:, n % 4, :].rearrange("p (h o) -> p h o", o=1)
                                           .to_broadcast([P, HG, S2]), ALU.mult).then_inc(xprobs_ready, 1)
                        if n == 3:
                            pool.wait_ge(t_full, NT)
                            for t in range(NT):
                                pool.tensor_tensor(x[:, t, :], x[:, t, :], b_xo[:, :], ALU.add).then_inc(resid2, 1)
                    reciprocal_root(pool, 2)

                @block.sync
                def _(sp):
                    sp.wait_ge(ln_done, 3 * NT)
                    sp.dma_start(scr["x5"].rearrange("(b t p) n -> b p t n", p=P, t=NT)[b], x[:, :, :]).then_inc(stored, 16)
                    sp.wait_ge(t_out, 2 * NT)
                    sp.dma_start(scr["x5T"][b].rearrange("(c p) n -> p c n", p=P), x5T[:, :, :]).then_inc(stored, 16)
                    sp.wait_ge(conv_out, 2)
                    sp.dma_start(scr["xc"][b], xc[:, :, :]).then_inc(stored, 16)
                    sp.wait_ge(stored, 48)

        with nc.Fori(0, trips) as b:
            project(b)
            heads()
            tail(b)
            with nc.Block() as block:
                @block.vector
                def _(dve):
                    for s in sems:
                        dve.sem_clear(s)


def gated_layer_stage(nc, A, scr, out, cst, trips):
    ident = cst["ident"]
    with ExitStack() as ctx:
        def sb(name, shape, dt=FP32):
            return ctx.enter_context(nc.sbuf_tensor("gl_" + name, shape, dt))

        sems = []

        def sem(name):
            s = ctx.enter_context(nc.semaphore("gl_" + name))
            sems.append(s)
            return s

        psum = ctx.enter_context(nc.psum_tensor("gl_psum", [P, 8, 512], FP32))
        bank = [psum[:, i, :] for i in range(8)]

        w = sb("w", [P, NC, D])
        w_lin = sb("w_lin", [P, 2, D])
        b_lin = sb("b_lin", [P, 2, D])
        b_out = sb("b_out", [P, D])
        gamma = sb("gamma", [P, 2])
        beta = sb("beta", [P, 2])
        conv = sb("conv", [P, 2, B, S])
        bstats = sb("bstats", [P, 2, B, 6])
        bmv = sb("bmv", [P, 2, 2])
        bvare = sb("bvare", [P, 2])
        brstd = sb("brstd", [P, 2])
        bscale = sb("bscale", [P, 2])
        bshift = sb("bshift", [P, 2])
        act_b = sb("act_b", [P, 2, S])
        x = sb("x", [P, NT, D])
        xb = sb("xb", [P, NT, D])
        xT = sb("xT", [P, NC, S])
        expv = sb("expv", [P, 4, D])
        left = sb("left", [P, 4, D])
        top = sb("top", [P, 4, 8])
        nmax = sb("nmax", [P, 4])
        esum = sb("esum", [P, 4])
        rsum = sb("rsum", [P, 4])
        zo = sb("zo", [P, 2, D])
        xs = sb("xs", [P, 2, D])
        xsT = sb("xsT", [P, 2, NC, P])
        z = sb("z", [P, 2, D])
        stats = sb("stats", [P, 2, 6])
        mv = sb("mv", [P, 2, 2])
        vare = sb("vare", [P, 2])
        rstd = sb("rstd", [P, 2])

        setup_in, bn_step, bn_var, bn_rstd, bn_ready, gelu_done = (
            sem(n) for n in ("setup_in", "bn_step", "bn_var", "bn_rstd", "bn_ready", "gelu_done"))
        with nc.Block() as block:
            @block.sync
            def _(sp):
                for b in range(B):
                    sp.dma_start(conv[:, :, b, :], scr["xc"][b]).then_inc(setup_in, 16)
                sp.dma_start(w[:, :, :], A["w_ffn1"].rearrange("(c p) n -> p c n", p=P)).then_inc(setup_in, 16)
                sp.dma_start(w_lin[:, :, :], A["w_lin"]).then_inc(setup_in, 16)
                sp.dma_start(gamma[:, :], A["gamma"]).then_inc(setup_in, 16)
                sp.dma_start(beta[:, :], A["beta"]).then_inc(setup_in, 16)
                for br in range(2):
                    sp.dma_start(b_lin[:, br, :], A["b_lin"][br:br + 1, :].to_broadcast([P, D])).then_inc(setup_in, 16)
                sp.dma_start(b_out[:, :], A["b_ffn1"].rearrange("(a n) -> a n", a=1).to_broadcast([P, D]))\
                    .then_inc(setup_in, 16)
                sp.wait_ge(setup_in, 16 * (B + 7))

            @block.vector
            def _(dve):
                link = chain_of(dve, bn_step)
                dve.wait_ge(setup_in, 16 * (B + 7))
                for br in range(2):
                    for b in range(B):
                        dve.bn_stats(bstats[:, br, b, :], conv[:, br, b, :]).then_inc(bn_step, 1)
                link.skip(2 * B)
                for br in range(2):
                    dve.bn_aggr(bmv[:, br, :], bstats[:, br, :, :].rearrange("p b s -> p (b s)")).then_inc(bn_step, 1)
                link.skip(2)
                dve.tensor_scalar(bvare[:, :], bmv[:, :, 1], EPS, None, ALU.add).then_inc(bn_var, 1)
                dve.wait_ge(bn_rstd, 1)
                link(dve.tensor_tensor(bscale[:, :], brstd[:, :], gamma[:, :], ALU.mult))
                link(dve.tensor_tensor(bshift[:, :], bmv[:, :, 0], bscale[:, :], ALU.mult))
                dve.tensor_tensor(bshift[:, :], beta[:, :], bshift[:, :], ALU.subtract).then_inc(bn_ready, 1)

            @block.gpsimd
            def _(pool):
                pool.wait_ge(bn_var, 1)
                pool.tensor_tensor(brstd[:, :], bvare[:, :], cst["mhalf"][:, 0:2], ALU.pow).then_inc(bn_rstd, 1)

            @block.scalar
            def _(act):
                act.wait_ge(bn_ready, 1)
                for br in range(2):
                    part = conv[:, br, :, :].rearrange("p b s -> p (b s)")
                    act.activation(part, part, ACT.Gelu, scale=bscale[:, br:br + 1], bias=bshift[:, br:br + 1])\
                        .then_inc(gelu_done, 1)

        loaded, act_ready, xb_ready = sem("loaded"), sem("act_ready"), sem("xb_ready")
        lin_full, logit_done = sem("lin_full"), sem("logit_done")
        exp_done = sem("exp_done")
        chain = sem("chain")
        top_done, sel_done = sem("top_done"), sem("sel_done")
        full_full, zo_done = sem("full_full"), sem("zo_done")
        xs_done = sem("xs_done")
        xsT_full, xsT_out = sem("xsT_full"), sem("xsT_out")
        in_full, z_done = sem("in_full"), sem("z_done")
        zr_done = sem("zr_done")
        ln_step, ln_var, ln_rstd, ln_done = (sem(n) for n in ("ln_step", "ln_var", "ln_rstd", "ln_done"))
        stored = [sem(f"stored{i}") for i in range(2)]

        def batch(b):
            with nc.Block() as block:
                @block.sync
                def _(sp):
                    sp.dma_start(xT[:, :, :], scr["x5T"][b].rearrange("(c p) n -> p c n", p=P)).then_inc(loaded, 16)
                    sp.dma_start(x[:, :, :], scr["x5"].rearrange("(b t p) n -> b p t n", p=P, t=NT)[b]).then_inc(loaded, 16)
                    rows = out.rearrange("b (t p) n -> b t p n", p=P)
                    for t in range(NT):
                        sp.wait_ge(ln_done, t + 1)
                        sp.dma_start(rows[b, t], z[:, t % 2, :]).then_inc(stored[t % 2], 16)
                    for i in range(2):
                        sp.wait_ge(stored[i], 16 * NT // 2)

                @block.tensor
                def _(pe):
                    def lin(t):
                        for br in range(2):
                            if t >= 2:
                                pe.wait_ge(logit_done, 2 * (t - 2) + br + 1)
                            pe.matmul(bank[2 * (t % 2) + br], act_b[:, br, t * P:(t + 1) * P], w_lin[:, br, :],
                                      start=True, stop=True).then_inc(lin_full, 1)

                    def full(t):
                        if t >= 2:
                            pe.wait_ge(zo_done, t - 1)
                        for c in range(NC):
                            mm = pe.matmul(bank[4 + t % 2], xT[:, c, t * P:(t + 1) * P], w[:, c, :],
                                           start=(c == 0), stop=(c == NC - 1))
                        mm.then_inc(full_full, 1)

                    pe.wait_ge(act_ready, 1)
                    lin(0)
                    lin(1)
                    pe.wait_ge(loaded, 32)
                    full(0)
                    full(1)
                    for t in range(NT):
                        if t + 2 < NT:
                            lin(t + 2)
                        pe.wait_ge(xs_done, t + 1)
                        if t >= 1:
                            pe.wait_ge(xsT_out, t)
                        for c in range(NC):
                            mm = pe.transpose(bank[6][:, c * P:(c + 1) * P], xs[:, t % 2, c * P:(c + 1) * P], ident[:, :])
                        mm.then_inc(xsT_full, 1)
                        if t + 2 < NT:
                            full(t + 2)
                        pe.wait_ge(xsT_out, t + 1)
                        if t >= 1:
                            pe.wait_ge(z_done, t)
                        for c in range(NC):
                            mm = pe.matmul(bank[7], xsT[:, t % 2, c, :], w[:, c, :], start=(c == 0), stop=(c == NC - 1))
                        mm.then_inc(in_full, 1)

                @block.scalar
                def _(act):
                    act.activation(act_b[:, :, :], conv[:, :, bass.ds(b, 1), :].rearrange("p g o s -> p g (o s)"),
                                   ACT.Copy).then_inc(act_ready, 1)

                    def exps(t):
                        for br in range(2):
                            u = 2 * t + br
                            act.wait_ge(logit_done, u + 1)
                            act.activation(expv[:, u % 4, :], expv[:, u % 4, :], ACT.Exp, scale=-1.0,
                                           bias=nmax[:, u % 4:u % 4 + 1], accum_out=esum[:, u % 4:u % 4 + 1])\
                                .then_inc(exp_done, 1)

                    exps(0)
                    for t in range(NT):
                        if t + 1 < NT:
                            exps(t + 1)
                        act.wait_ge(xsT_full, t + 1)
                        if t >= 2:
                            act.wait_ge(in_full, t - 1)
                        act.activation(xsT[:, t % 2, :, :], bank[6].rearrange("p (c q) -> p c q", q=P), ACT.Copy)\
                            .then_inc(xsT_out, 1)

                @block.vector
                def _(dve):
                    link = chain_of(dve, chain)
                    ln = chain_of(dve, ln_step)

                    def logits(t):
                        for br in range(2):
                            u = 2 * t + br
                            dve.wait_ge(lin_full, u + 1)
                            if u >= 4:
                                dve.wait_ge(sel_done, t - 1)
                            dve.tensor_tensor_reduce(out=expv[:, u % 4, :], in0=bank[2 * (t % 2) + br], in1=b_lin[:, br, :],
                                                     scale=-1.0, scalar=-TAKEN, op0=ALU.add, op1=ALU.min,
                                                     accum_out=nmax[:, u % 4:u % 4 + 1]).then_inc(logit_done, 1)

                    def finish(t):
                        dve.wait_ge(in_full, t + 1)
                        dve.wait_ge(zr_done, t + 1)
                        if t >= 2:
                            dve.wait_ge(stored[t % 2], 16 * (t // 2))
                        dve.tensor_tensor(z[:, t % 2, :], bank[7], zo[:, t % 2, :], ALU.add).then_inc(z_done, 1)
                        dve.wait_ge(z_done, t + 1)
                        ln(dve.bn_stats(stats[:, t % 2, :], z[:, t % 2, :]))
                        ln(dve.bn_aggr(mv[:, t % 2, :], stats[:, t % 2, :]))
                        dve.tensor_scalar(vare[:, t % 2:t % 2 + 1], mv[:, t % 2, 1:2], EPS, None, ALU.add).then_inc(ln_var, 1)

                    def last(t):
                        dve.wait_ge(ln_rstd, t + 1)
                        dve.tensor_scalar(z[:, t % 2, :], z[:, t % 2, :], mv[:, t % 2, 0:1], rstd[:, t % 2:t % 2 + 1],
                                          ALU.subtract, ALU.mult).then_inc(ln_done, 1)

                    logits(0)
                    for t in range(NT):
                        if t + 1 < NT:
                            logits(t + 1)
                        us = [(2 * t + br) % 4 for br in range(2)]
                        dve.wait_ge(exp_done, 2 * t + 2)
                        for r in range(KGATE // 8):
                            for u in us:
                                dve.max(top[:, u, :], (left if r else expv)[:, u, :]).then_inc(chain, 1)
                            link.skip(2)
                            for i, u in enumerate(us):
                                ins = dve.match_replace(left[:, u, :], top[:, u, :], (left if r else expv)[:, u, :], 0.0)
                                if r < KGATE // 8 - 1:
                                    ins.then_inc(chain, 1)
                                else:
                                    ins.then_inc(top_done, 1)
                            if r < KGATE // 8 - 1:
                                link.skip(2)
                        if t >= 1:
                            finish(t - 1)
                        u0 = us[0]
                        link(dve.reciprocal(rsum[:, u0:u0 + 2], esum[:, u0:u0 + 2]))
                        dve.wait_ge(sel_done, t + 1)
                        dve.scalar_tensor_tensor(out=xs[:, t % 2, :], in0=left[:, us[1], :], scalar=rsum[:, us[1]:us[1] + 1],
                                                 in1=x[:, t, :], op0=ALU.mult, op1=ALU.mult).then_inc(xs_done, 1)
                        dve.wait_ge(full_full, t + 1)
                        if t >= 2:
                            dve.wait_ge(z_done, t - 1)
                        dve.scalar_tensor_tensor(out=zo[:, t % 2, :], in0=left[:, us[0], :], scalar=rsum[:, us[0]:us[0] + 1],
                                                 in1=bank[4 + t % 2], op0=ALU.mult, op1=ALU.mult).then_inc(zo_done, 1)
                        if t >= 1:
                            last(t - 1)
                    finish(NT - 1)
                    last(NT - 1)

                @block.gpsimd
                def _(pool):
                    pool.wait_ge(loaded, 32)
                    for t in range(NT):
                        pool.tensor_tensor(xb[:, t, :], x[:, t, :], b_out[:, :], ALU.add).then_inc(xb_ready, 1)
                    for t in range(NT):
                        pool.wait_ge(top_done, 2 * t + 2)
                        u0 = 2 * (t % 2)
                        pool.tensor_tensor(left[:, u0:u0 + 2, :], expv[:, u0:u0 + 2, :], left[:, u0:u0 + 2, :], ALU.subtract)\
                            .then_inc(sel_done, 1)
                        if t >= 1:
                            pool.wait_ge(ln_var, t)
                            pool.tensor_tensor(rstd[:, (t - 1) % 2:(t - 1) % 2 + 1], vare[:, (t - 1) % 2:(t - 1) % 2 + 1],
                                               cst["mhalf"][:, 0:1], ALU.pow).then_inc(ln_rstd, 1)
                        pool.wait_ge(zo_done, t + 1)
                        pool.wait_ge(xb_ready, NT)
                        pool.tensor_tensor(zo[:, t % 2, :], zo[:, t % 2, :], xb[:, t, :], ALU.add).then_inc(zr_done, 1)
                    pool.wait_ge(ln_var, NT)
                    pool.tensor_tensor(rstd[:, (NT - 1) % 2:(NT - 1) % 2 + 1], vare[:, (NT - 1) % 2:(NT - 1) % 2 + 1],
                                       cst["mhalf"][:, 0:1], ALU.pow).then_inc(ln_rstd, 1)

        with nc.Fori(0, trips) as b:
            batch(b)
            with nc.Block() as block:
                @block.vector
                def _(dve):
                    for s in sems:
                        dve.sem_clear(s)


def decoder_program(nc, A, out):
    scr = {}
    for name, shape in (("rows", [T + CAP, XW]), ("slots", [E * CAP + 1, 1]), ("acc", [T + CAP, D]),
                        ("x5", [T, D]), ("x5T", [B, D, S]), ("xc", [B, P, 2, S])):
        scr[name] = nc.dram_tensor("scratch_" + name, shape, FP32, kind="Internal").ap()
    with ExitStack() as ctx:
        cst = constants(nc, ctx)
        pruned_attention_stage(nc, A, scr, cst, B)
        experts_stage(nc, A, scr, cst)
        layer1_attention_stage(nc, A, scr, cst, B)
        gated_layer_stage(nc, A, scr, out, cst, B)


def kernel(**inputs):
    import numpy as _np
    import concourse.bacc as _bacc
    from concourse import mybir as _mybir
    from concourse.bass_utils import run_bass_kernel_spmd as _run

    a = {k: _np.asarray(v) for k, v in inputs.items()}

    def columns(*vectors):
        return _np.concatenate(vectors).reshape(-1, P).T

    def gates(name, axis, order=None):
        pair = [a["L1_ffn_so_" + name], a["L1_ffn_si_" + name]]
        return _np.stack([p.T if order else p for p in pair], axis)

    conv_w = gates("conv_w", 0).reshape(2, D // P, P).transpose(2, 0, 1)
    laid = {
        "x": a["x"], "xT": a["x"].transpose(0, 2, 1),
        "ctx": a["ctx_1024"], "ctxT": a["ctx_1024"].transpose(0, 2, 1),
        "mask": a["mask_Bx1xSxS2_if1"].reshape(B, S, S2),
        "w_qkv0": a["L0_attn_w_attn"].T, "b_qkv0": columns(a["L0_attn_b_attn"]),
        "w_proj0": a["L0_attn_w_proj"].T, "b_proj0": a["L0_attn_b_proj"],
        "w_router": a["L0_ffn_router_w"].T, "w_sgu": a["L0_ffn_ws_gate_up"], "w_sdown": a["L0_ffn_ws_down"],
        "w_gate": a["L0_ffn_w_gate"], "w_up": a["L0_ffn_w_up"], "w_down": a["L0_ffn_w_down"],
        "w_qkv1": _np.concatenate([a["L1_attn_W" + k].T for k in "qkv"], 1),
        "b_qkv1": columns(*(a["L1_attn_b" + k] for k in "qkv")),
        "w_o1": a["L1_attn_Wo"].T, "b_o1": a["L1_attn_bo"],
        "w_x": _np.stack([a["L1_xattn_W" + k].T for k in "qkv"]),
        "w_xo": a["L1_xattn_Wo"].T, "b_xo": a["L1_xattn_bo"],
        "conv_w": conv_w, "conv_b": gates("conv_b", 1),
        "gamma": gates("gamma", 1), "beta": gates("beta", 1),
        "w_lin": gates("lin_w", 1, order="T"), "b_lin": gates("lin_b", 0),
        "w_ffn1": a["L1_ffn_weight"], "b_ffn1": a["L1_ffn_bias"],
    }
    nc = _bacc.Bacc("TRN2", target_bir_lowering=False, num_devices=1)
    arrays, aps = {}, {}
    for name, value in laid.items():
        value = _np.ascontiguousarray(value)
        arrays[f"in_{name}"] = value
        aps[name] = nc.dram_tensor(f"in_{name}", value.shape, _mybir.dt.from_np(value.dtype), kind="ExternalInput").ap()
    out = nc.dram_tensor("out_0", (B, S, D), _mybir.dt.float32, kind="ExternalOutput").ap()
    decoder_program(nc, aps, out)
    r = _run(nc, [arrays], core_ids=[0])
    return r.results[0]["out_0"]
```

```python
import numpy as np
import concourse.bass as bass
from concourse import mybir
from contextlib import ExitStack

FP32 = mybir.dt.float32
F32R = mybir.dt.float32r
BF16 = mybir.dt.bfloat16
I32 = mybir.dt.int32
ALU = mybir.AluOpType
ACT = mybir.ActivationFunctionType
AX = mybir.AxisListType

P = 128
B, S, D = 8, 512, 512
T = B * S
NT = S // P
NC = D // P
H, DH = 16, 32
HG = P // DH
S2 = 77
E, TOPK, F = 64, 8, 384
NF = F // P
CAP = 256
NJ = CAP // P
XW = D + E
KEEP = int(S * 0.2) - 1
KGATE = 32
G = D // 4
EPS = 1e-5
QSCALE = 1.0 / float(np.sqrt(DH))
XSCALE = 1.0 / float(np.sqrt(D))
FAR = 1e30
TAKEN = -3e38
GELU_C, GELU_A = 0.7978845608028654, 0.044715


def chain_of(eng, sem):
    count = [0]

    def link(ins):
        count[0] += 1
        ins.then_inc(sem, 1)
        eng.wait_ge(sem, count[0])

    def skip(n):
        count[0] += n
        eng.wait_ge(sem, count[0])
    link.skip = skip
    return link


def pruned_attention_stage(nc, A, scr, cst, trips):
    ident, upper, ones, upper_b, ones_b = (cst[k] for k in ("ident", "upper", "ones", "upper_b", "ones_b"))
    with ExitStack() as ctx:
        def sb(name, shape, dt=FP32):
            return ctx.enter_context(nc.sbuf_tensor("l0_" + name, shape, dt))

        sems = []

        def sem(name):
            s = ctx.enter_context(nc.semaphore("l0_" + name))
            sems.append(s)
            return s

        bank = [ctx.enter_context(nc.psum_tensor(f"l0_bank{i}", [P, 512], FP32)) for i in range(8)]

        w_qkv = sb("w_qkv", [P, NC, 3 * D])
        w_proj = sb("w_proj", [P, NC, D])
        w_router = sb("w_router", [P, NC, E])
        w_sgu = sb("w_sgu", [P, NC, 2 * F])
        w_sdown = sb("w_sdown", [P, NF, D])
        b_qkv = sb("b_qkv", [P, 3 * NC])
        b_proj = sb("b_proj", [P, D])
        x = sb("x", [P, NT, D])
        xT = sb("xT", [P, NC, S])
        yT = sb("yT", [P, NC, S])
        qT = sb("qT", [P, NC, S])
        kpad = sb("kpad", [P, H, S])
        v = sb("v", [P, NT, D])
        bias = sb("bias", [P, NT, S])
        probs = sb("probs", [P, 4, 2, S])
        pT = sb("pT", [P, HG, NT, S])
        x2w = sb("x2w", [P, NT, XW])
        flat_probs = probs[:, :, :, :].rearrange("p a b s -> p (a b s)")
        gate = flat_probs[:, 0:NT * S].rearrange("p (t s) -> p t s", s=S)
        work = flat_probs[:, NT * S:NT * S + S + 8]
        top = sb("top", [P, 8])
        nmax = sb("nmax", [P, 4, 2])
        psums = sb("psums", [P, 4, 2])
        rsum = sb("rsum", [P, 4, 2])
        x1T, x2T = pT[:, 0, :, :], pT[:, 1, :, :]
        ctx_rows = sb("ctx_rows", [P, D])
        ctx_T = sb("ctx_T", [P, NC, S2])
        gl = pT[:, 2, 0, :]
        hid = pT[:, 3, 0:NF, :]
        gelu_out = sb("gelu_out", [P, S])
        stats = sb("stats", [P, NT, 6])
        mv = sb("mv", [P, NT, 2])
        vare = sb("vare", [P, NT])
        rstd = sb("rstd", [P, NT])
        expv = sb("expv", [P, NT, E])
        left = sb("left", [P, NT, E])
        mask = sb("mask", [P, NT, E])
        mask_b = sb("mask_b", [P, NT, E], BF16)
        run = sb("run", [P, NT + 1, E], BF16)
        nmx = sb("nmx", [P, NT])
        wsum = sb("wsum", [P, NT])
        m8 = sb("m8", [P, NT, 8])
        enc = sb("enc", [P, NT, E])
        slot1 = sb("slot1", [P, E])
        off = sb("off", [P, NT * 8])
        idx = sb("idx", [P, NT * 8], I32)
        tok = sb("tok", [P, NT])

        setup_in = sem("setup_in")
        setup_pool = sem("setup_pool")
        setup_slots = sem("setup_slots")
        setup_dve = sem("setup_dve")

        with nc.Block() as block:
            @block.sync
            def _(sp):
                for dst, src in ((w_qkv, A["w_qkv0"]), (w_proj, A["w_proj0"]), (w_router, A["w_router"]),
                                 (w_sgu, A["w_sgu"]), (w_sdown, A["w_sdown"])):
                    sp.dma_start(dst[:, :, :], src.rearrange("(c p) n -> p c n", p=P)).then_inc(setup_in, 16)
                sp.dma_start(b_qkv[:, :], A["b_qkv0"]).then_inc(setup_in, 16)
                sp.dma_start(b_proj[:, :], A["b_proj0"].rearrange("(a n) -> a n", a=1).to_broadcast([P, D]))\
                    .then_inc(setup_in, 16)
                sp.wait_ge(setup_pool, 4)
                sp.dma_start(scr["slots"][1:E * CAP + 1, :].rearrange("(e n) o -> e (n o)", n=CAP),
                             work[0:E, 0:CAP]).then_inc(setup_slots, 16)
                sp.dma_start(scr["slots"][0:1, :], work[0:1, 0:1]).then_inc(setup_slots, 16)
                for j in range(NJ):
                    sp.dma_start(scr["rows"][T + j * P:T + (j + 1) * P, :], x2w[:, 0, :]).then_inc(setup_slots, 16)
                    sp.dma_start(scr["acc"][T + j * P:T + (j + 1) * P, :], x2w[:, 0, 0:D]).then_inc(setup_slots, 16)
                sp.wait_ge(setup_slots, (2 + 2 * NJ) * 16)

            @block.gpsimd
            def _(pool):
                pool.iota(tok[:, :], pattern=[[P, NT]], base=-S, channel_multiplier=1,
                          allow_small_or_imprecise_dtypes=True).then_inc(setup_pool, 1)
                pool.iota(slot1[:, :], pattern=[[CAP, E]], base=1, channel_multiplier=0,
                          allow_small_or_imprecise_dtypes=True).then_inc(setup_pool, 1)
                pool.iota(work[:, 0:CAP], pattern=[[1, CAP]], base=T, channel_multiplier=0,
                          allow_small_or_imprecise_dtypes=True).then_inc(setup_pool, 1)
                pool.memset(x2w[:, 0, :], 0.0).then_inc(setup_pool, 1)

            @block.vector
            def _(dve):
                dve.memset(kpad[:, :, :], 0.0)
                dve.memset(gelu_out[:, :], 0.0)
                dve.memset(ctx_rows[:, :], 0.0)
                dve.memset(run[:, 0, :], 0.0)
                dve.memset(idx[:, :], 4 * E * CAP)
                dve.wait_ge(setup_in, 7 * 16)
                dve.tensor_scalar(b_qkv[:, 0:NC], b_qkv[:, 0:NC], QSCALE, None, ALU.mult)

        loaded = sem("loaded")
        proj_full, proj_drained = sem("proj_full"), sem("proj_drained")
        gate_full, gate_relu = sem("gate_full"), sem("gate_relu")
        gate_masked = sem("gate_masked")
        forget_full, forget_out = sem("forget_full"), sem("forget_out")
        forget_causal = sem("forget_causal")
        dropped = sem("dropped")
        bias_ready = sem("bias_ready")
        chain_p1 = sem("chain_p1")

        def width(t):
            return (t + 1) * P

        PROJ = [("q", 0), ("k", 0), ("v", 0), ("v", 1), ("v", 2), ("v", 3), ("q", 1), ("k", 1),
                ("q", 2), ("k", 2), ("q", 3), ("k", 3)]
        ROUNDS = -(-KEEP // 8)
        EXTRA = ROUNDS * 8 - KEEP
        SELECT = [(t, r, min(n, ROUNDS - r)) for t, n in enumerate((7, 5, 4, 3)) for r in range(0, ROUNDS, n)]
        GATE_STEPS = 4 + len(SELECT)
        FIRST_SELECT = 4

        LATE_PROJ = 4
        GATE_PROJ = {0: range(0, 2), 2: range(2, LATE_PROJ)}

        def project(pe, j):
            kind, i = PROJ[j]
            if j >= 2:
                pe.wait_ge(proj_drained, j - 1)
            out = bank[j % 2]
            for c in range(NC):
                if kind == "v":
                    mm = pe.matmul(out[:, :], xT[:, c, i * P:(i + 1) * P], w_qkv[:, c, 2 * D:3 * D],
                                   start=(c == 0), stop=(c == NC - 1))
                else:
                    at = i * P + (D if kind == "k" else 0)
                    mm = pe.matmul(out[:, :], w_qkv[:, c, at:at + P], xT[:, c, :],
                                   start=(c == 0), stop=(c == NC - 1))
            mm.then_inc(proj_full, 1)

        def drain_projection(act, j):
            kind, i = PROJ[j]
            act.wait_ge(proj_full, j + 1)
            src = bank[j % 2]
            if kind == "q":
                last = act.activation(qT[:, i, :], src[:, :], ACT.Identity, scale=QSCALE, bias=b_qkv[:, i:i + 1])
            elif kind == "k":
                for h in range(HG):
                    r = slice(h * DH, (h + 1) * DH)
                    last = act.activation(kpad[r, i * HG + h, :], src[r, :], ACT.Identity,
                                          bias=b_qkv[r, NC + i:NC + i + 1])
            else:
                last = act.activation(v[:, i, :], src[:, :], ACT.Copy)
            last.then_inc(proj_drained, 1)

        def late_projections(step, eng):
            for j in range(LATE_PROJ, len(PROJ)):
                step(eng, j)
                yield

        def gate_pe(pe):
            pe.wait_ge(loaded, 16)
            for step in range(GATE_STEPS):
                if step == FIRST_SELECT:
                    pe.wait_ge(forget_out, NT)
                for j in GATE_PROJ.get(step, ()):
                    project(pe, j)
                if step == 1:
                    pe.wait_ge(proj_drained, 2)
                    for t in range(NT):
                        if t >= 2:
                            pe.wait_ge(gate_relu, t - 1)
                        pe.matmul(bank[2 + t % 2][:, 0:width(t)], qT[:, 0, t * P:(t + 1) * P],
                                  kpad[:, 0, 0:width(t)], start=True, stop=True).then_inc(gate_full, 1)
                if step == 3:
                    pe.wait_ge(gate_masked, 2 * NT)
                    for t in range(NT):
                        if t >= 2:
                            pe.wait_ge(forget_out, t - 1)
                        out = bank[2 + t % 2]
                        mm = pe.matmul(out[:, 0:width(t)], upper[:, :], gate[:, t, 0:width(t)], start=True, stop=True)
                        for u in range(t):
                            mm = pe.matmul(out[:, 0:width(u)], ones[:, :], gate[:, u, 0:width(u)],
                                           start=False, stop=True, skip_group_check=True)
                        mm.then_inc(forget_full, 1)
                yield

        def gate_act(act):
            for step in range(GATE_STEPS):
                for j in GATE_PROJ.get(step, ()):
                    drain_projection(act, j)
                if step == 3:
                    for t in range(NT):
                        act.wait_ge(forget_full, t + 1)
                        act.activation(bias[:, t, 0:width(t)], bank[2 + t % 2][:, 0:width(t)], ACT.Copy,
                                       scale=-1.0).then_inc(forget_out, 1)
                yield

        def gate_pool(pool):
            for step in range(GATE_STEPS):
                if step == 1:
                    for t in range(NT):
                        pool.wait_ge(gate_relu, t + 1)
                        own = gate[:, t, t * P:(t + 1) * P]
                        pool.affine_select(out=own, in_=own, pattern=[[-1, P]], compare_op=ALU.is_gt, fill=0.0,
                                           base=0, channel_multiplier=1).then_inc(gate_masked, 1)
                        pool.wait_ge(gate_masked, 2 * t + 1)
                        pool.memset(gate[:, t, 0:1], 0.0).then_inc(gate_masked, 1)
                if step == 3:
                    for t in range(NT):
                        pool.wait_ge(forget_out, t + 1)
                        own = bias[:, t, t * P:(t + 1) * P]
                        pool.affine_select(out=own, in_=own, pattern=[[-1, P]], compare_op=ALU.is_ge, fill=-FAR,
                                           base=0, channel_multiplier=1).then_inc(forget_causal, 1)
                k = step - FIRST_SELECT - 1
                if 0 <= k and SELECT[k][1] + SELECT[k][2] == ROUNDS:
                    keep_own(pool, SELECT[k][0])
                yield
            keep_own(pool, NT - 1)

        def keep_own(pool, t):
            pool.wait_ge(dropped, t + 1)
            own = bias[:, t, t * P:(t + 1) * P]
            pool.affine_select(out=own, in_=own, pattern=[[-1, P]], compare_op=ALU.not_equal, fill=0.0,
                               base=0, channel_multiplier=1).then_inc(bias_ready, 1)

        def gate_dve(dve):
            link = chain_of(dve, chain_p1)
            for step in range(GATE_STEPS):
                if step == 1:
                    for t in range(NT):
                        dve.wait_ge(gate_full, t + 1)
                        dve.tensor_scalar(gate[:, t, 0:width(t)], bank[2 + t % 2][:, 0:width(t)], 0.0, None,
                                          ALU.max).then_inc(gate_relu, 1)
                if step >= FIRST_SELECT:
                    t, first, rounds = SELECT[step - FIRST_SELECT]
                    w = width(t)
                    if first == 0:
                        link(dve.memset(work[:, 0:EXTRA], -TAKEN))
                        dve.wait_ge(forget_causal, t + 1)
                        link(dve.tensor_copy(work[:, EXTRA:EXTRA + w], bias[:, t, 0:w]))
                    for _ in range(rounds):
                        link(dve.max(top[:, :], work[:, 0:EXTRA + w]))
                        link(dve.match_replace(work[:, 0:EXTRA + w], top[:, :], work[:, 0:EXTRA + w], TAKEN))
                    if first + rounds == ROUNDS:
                        link(dve.tensor_scalar(work[:, EXTRA:EXTRA + w], work[:, EXTRA:EXTRA + w], TAKEN / 2, -FAR,
                                               ALU.is_gt, ALU.mult))
                        dve.tensor_tensor(bias[:, t, 0:w], bias[:, t, 0:w], work[:, EXTRA:EXTRA + w],
                                          ALU.min).then_inc(dropped, 1)
                        dve.wait_ge(dropped, t + 1)
                yield

        scores_full, scores_out = sem("scores_full"), sem("scores_out")
        exp_done = sem("exp_done")
        rsum_ready = sem("rsum_ready")
        probs_ready = sem("probs_ready")
        pT_full = sem("pT_full")
        pT_out_dve, pT_out_act = sem("pT_out_dve"), sem("pT_out_act")
        attn_full, attn_out = sem("attn_full"), sem("attn_out")
        LAG = 3

        UNITS = [(g, t, p) for g in range(NC) for t in range(NT) for p in range(2)]
        PER_G = 2 * NT

        tail_in, resid = sem("tail_in"), sem("resid")

        scattered = ctx.enter_context(nc.semaphore("l0_scattered"))

        ALL_SCATTERED = 16 * NT * TOPK

        def scatter(pool, k):
            pool.indirect_dma_start(
                out=scr["slots"][:, :], out_offset=bass.IndirectOffsetOnAxis(ap=idx[:, k:k + 1], axis=0),
                in_=tok[:, k // TOPK:k // TOPK + 1], in_offset=None,
                bounds_check=E * CAP, oob_is_err=False).then_inc(scattered, 16)

        def heads(b):
            N = len(UNITS)
            with nc.Block() as block:
                @block.sync
                def _(sp):
                    sp.dma_start(x[:, :, :], A["x"][b].rearrange("(t p) n -> p t n", p=P)).then_inc(tail_in, 16)
                    sp.dma_start(ctx_rows[0:S2, :], A["ctx"][b]).then_inc(tail_in, 16)
                    sp.dma_start(ctx_T[:, :, :], A["ctxT"][b].rearrange("(c p) n -> p c n", p=P)).then_inc(tail_in, 16)
                    sp.wait_ge(tail_in, 48)

                @block.tensor
                def _(pe):
                    for n in range(N + LAG + 1):
                        if n < N:
                            g, t, p = UNITS[n]
                            if n >= 2:
                                pe.wait_ge(scores_out, 2 * (n - 1))
                            for hh in range(2):
                                mm = pe.matmul(bank[2 * (n % 2) + hh][:, 0:width(t)], qT[:, g, t * P:(t + 1) * P],
                                               kpad[:, HG * g + 2 * p + hh, 0:width(t)], start=True, stop=True)
                            mm.then_inc(scores_full, 1)
                        m = n - LAG
                        if m >= PER_G and m % PER_G == 0:
                            g = m // PER_G - 1
                            pe.wait_ge(pT_out_dve, m)
                            pe.wait_ge(pT_out_act, m)
                            if g >= 1:
                                pe.wait_ge(attn_out, g)
                            for kc in range(NT):
                                for h in range(HG):
                                    mm = pe.matmul(bank[6][h * DH:(h + 1) * DH, kc * P:S],
                                                   v[:, kc, (HG * g + h) * DH:(HG * g + h + 1) * DH],
                                                   pT[:, h, kc, kc * P:S], start=(kc == 0), stop=True,
                                                   skip_group_check=True)
                            mm.then_inc(attn_full, 1)
                        if 0 <= m < N:
                            g, t, p = UNITS[m]
                            pe.wait_ge(probs_ready, m + 1)
                            for hh in range(2):
                                if m >= 1:
                                    pe.wait_ge(pT_out_act if hh else pT_out_dve, m)
                                for kc in range(t + 1):
                                    mm = pe.transpose(bank[4 + hh][:, kc * P:(kc + 1) * P],
                                                      probs[:, m % 4, hh, kc * P:(kc + 1) * P], ident[:, :])
                                mm.then_inc(pT_full, 1)

                @block.vector
                def _(dve):
                    for n in range(N + LAG):
                        if n < N:
                            g, t, p = UNITS[n]
                            dve.wait_ge(scores_full, n + 1)
                            if n >= 4:
                                dve.wait_ge(pT_full, 2 * (n - 3))
                            for hh in range(2):
                                dve.tensor_tensor_reduce(
                                    out=probs[:, n % 4, hh, 0:width(t)], in0=bank[2 * (n % 2) + hh][:, 0:width(t)],
                                    in1=bias[:, t, 0:width(t)], scale=-1.0, scalar=-TAKEN, op0=ALU.add, op1=ALU.min,
                                    accum_out=nmax[:, n % 4, hh:hh + 1]).then_inc(scores_out, 1)
                        m = n - 1
                        if 0 <= m < N:
                            dve.wait_ge(exp_done, 2 * m + 2)
                            dve.reciprocal(rsum[:, m % 4, :], psums[:, m % 4, :]).then_inc(rsum_ready, 1)
                        m = n - LAG
                        if 0 <= m < N:
                            g, t, p = UNITS[m]
                            dve.wait_ge(pT_full, 2 * m + 1)
                            if g >= 1:
                                dve.wait_ge(attn_full, g)
                            dve.tensor_copy(pT[:, 2 * p, 0:t + 1, t * P:(t + 1) * P],
                                            bank[4][:, 0:width(t)].rearrange("p (k q) -> p k q", q=P))\
                                .then_inc(pT_out_dve, 1)

                @block.scalar
                def _(act):
                    for n in range(N + LAG + 1):
                        if n < N:
                            g, t, p = UNITS[n]
                            for hh in range(2):
                                act.wait_ge(scores_out, 2 * n + hh + 1)
                                pr = probs[:, n % 4, hh, 0:width(t)]
                                act.activation(pr, pr, ACT.Exp, scale=-1.0, bias=nmax[:, n % 4, hh:hh + 1],
                                               accum_out=psums[:, n % 4, hh:hh + 1]).then_inc(exp_done, 1)
                        m = n - LAG
                        if 0 <= m < N:
                            g, t, p = UNITS[m]
                            act.wait_ge(pT_full, 2 * m + 2)
                            if g >= 1:
                                act.wait_ge(attn_full, g)
                            act.activation(pT[:, 2 * p + 1, 0:t + 1, t * P:(t + 1) * P],
                                           bank[5][:, 0:width(t)].rearrange("p (k q) -> p k q", q=P), ACT.Copy)\
                                .then_inc(pT_out_act, 1)
                        if m >= PER_G and m % PER_G == 0:
                            g = m // PER_G - 1
                            act.wait_ge(attn_full, g + 1)
                            act.activation(yT[:, g, :], bank[6][:, :], ACT.Identity,
                                           bias=b_qkv[:, 2 * NC + g:2 * NC + g + 1]).then_inc(attn_out, 1)

                @block.gpsimd
                def _(pool):
                    for n in range(N):
                        g, t, p = UNITS[n]
                        pool.wait_ge(rsum_ready, n + 1)
                        pr = probs[:, n % 4, :, 0:width(t)]
                        pool.tensor_tensor(pr, pr, rsum[:, n % 4, :].rearrange("p (h a) -> p h a", a=1)
                                           .to_broadcast([P, 2, width(t)]), ALU.mult).then_inc(probs_ready, 1)
                    pool.wait_ge(tail_in, 48)
                    for t in range(NT):
                        pool.tensor_tensor(x[:, t, :], x[:, t, :], b_proj[:, :], ALU.add).then_inc(resid, 1)
                    pool.wait_ge(resid, NT)

        o_full, res1 = sem("o_full"), sem("res1")
        ln_var, ln_rstd = sem("ln_var"), sem("ln_rstd")
        ln_done = sem("ln_done")
        t_full, t_out = sem("t_full"), sem("t_out")
        cx_full = sem("cx_full")
        sq_done, poly_done, tanh_done, gelu_done = sem("sq_done"), sem("poly_done"), sem("tanh_done"), sem("gelu_done")
        cy_full, res2 = sem("cy_full"), sem("res2")
        route_full = sem("route_full")
        shift_done, expv_done = sem("shift_done"), sem("expv_done")
        mask_done = sem("mask_done")
        pos_full = sem("pos_full")
        w_done, idx_done = sem("w_done"), sem("idx_done")
        sg_full, stanh_done = sem("sg_full"), sem("stanh_done")
        hid_mid, hid_done = sem("hid_mid"), sem("hid_done")
        sd_full, acc_done = sem("sd_full"), sem("acc_done")
        stored = sem("stored")
        chain_p3 = sem("chain_p3")

        TAIL_STEPS = 21

        def shared_banks(f):
            return (bank[6], bank[7]) if f % 2 == 0 else (bank[2], bank[3])

        DOWN_BANKS = (2, 3, 6, 7)
        SHARED_PE, SHARED_ACT, SHARED_DVE = (14, 15, 18), (15, 16, 18), (17, 18, 19)

        def tail_pe(pe):
            for step in range(TAIL_STEPS):
                if step == 0:
                    for t in range(NT):
                        for c in range(NC):
                            mm = pe.matmul(bank[4 + t][:, :], yT[:, c, t * P:(t + 1) * P], w_proj[:, c, :],
                                           start=(c == 0), stop=(c == NC - 1))
                        mm.then_inc(o_full, 1)
                if step in (4, 13):
                    k = 0 if step == 4 else 1
                    src = x if k == 0 else x2w
                    for t in range(NT):
                        pe.wait_ge(ln_done, k * NT + t + 1)
                        for c in range(NC):
                            mm = pe.transpose(bank[4 + t][:, c * P:(c + 1) * P], src[:, t, c * P:(c + 1) * P], ident[:, :])
                        mm.then_inc(t_full, 1)
                if step == 5:
                    pe.wait_ge(t_out, NT)
                    for c in range(NC):
                        mm = pe.matmul(bank[4][0:S2, :], ctx_T[:, c, :], x1T[:, c, :], start=(c == 0), stop=(c == NC - 1))
                    mm.then_inc(cx_full, 1)
                if step == 9:
                    pe.wait_ge(gelu_done, 1)
                    for t in range(NT):
                        pe.matmul(bank[4 + t][:, :], gelu_out[:, t * P:(t + 1) * P], ctx_rows[:, :],
                                  start=True, stop=True).then_inc(cy_full, 1)
                if step == 14:
                    pe.wait_ge(t_out, 2 * NT)
                    for t in range(NT):
                        for c in range(NC):
                            mm = pe.matmul(bank[4][:, t * E:(t + 1) * E], x2T[:, c, t * P:(t + 1) * P],
                                           w_router[:, c, :], start=(c == 0), stop=(c == NC - 1))
                    mm.then_inc(route_full, 1)
                if step == 18:
                    pe.wait_ge(mask_done, NT)
                    for t in range(NT):
                        pe.matmul(bank[5][:, t * E:(t + 1) * E], upper_b[:, :], mask_b[:, t, :], start=True, stop=False)
                        mm = pe.matmul(bank[5][:, t * E:(t + 1) * E], ones_b[:, :], run[:, t, :], start=False, stop=True)
                    mm.then_inc(pos_full, 1)
                if step in SHARED_PE:
                    f = SHARED_PE.index(step)
                    if f >= 2:
                        pe.wait_ge(hid_done, f - 1)
                    for half in range(2):
                        at = half * F + f * P
                        for c in range(NC):
                            mm = pe.matmul(shared_banks(f)[half][:, :], w_sgu[:, c, at:at + P], x2T[:, c, :],
                                           start=(c == 0), stop=(c == NC - 1))
                        mm.then_inc(sg_full, 1)
                if step == 20:
                    pe.wait_ge(hid_done, NF)
                    for t in range(NT):
                        for f in range(NF):
                            mm = pe.matmul(bank[DOWN_BANKS[t]][:, :], hid[:, f, t * P:(t + 1) * P], w_sdown[:, f, :],
                                           start=(f == 0), stop=(f == NF - 1))
                        mm.then_inc(sd_full, 1)
                yield

        def tail_act(act):
            for step in range(TAIL_STEPS):
                if step in (4, 13):
                    k = 0 if step == 4 else 1
                    for t in range(NT):
                        act.wait_ge(t_full, k * NT + t + 1)
                        act.activation((x2T if k else x1T)[:, :, t * P:(t + 1) * P],
                                       bank[4 + t][:, :].rearrange("p (c q) -> p c q", q=P), ACT.Copy).then_inc(t_out, 1)
                if step == 6:
                    act.wait_ge(cx_full, 1)
                    act.activation(gl[0:S2, :], bank[4][0:S2, :], ACT.Square).then_inc(sq_done, 1)
                if step == 7:
                    act.wait_ge(poly_done, 1)
                    act.activation(gl[0:S2, :], gl[0:S2, :], ACT.Tanh, scale=GELU_C).then_inc(tanh_done, 1)
                if step == 15:
                    act.wait_ge(shift_done, 1)
                    act.activation(expv[:, :, :], expv[:, :, :], ACT.Exp).then_inc(expv_done, 1)
                if step in SHARED_ACT:
                    f = SHARED_ACT.index(step)
                    act.wait_ge(sg_full, 2 * f + 1)
                    act.activation(hid[:, f, :], shared_banks(f)[0][:, :], ACT.Tanh, scale=0.5).then_inc(stanh_done, 1)
                yield

        def tail_dve(dve, end):
            link = chain_of(dve, chain_p3)

            def rows(step):
                return (lambda t: x[:, t, :]) if step < 10 else (lambda t: x2w[:, t, 0:D])

            def over(a, n=E):
                return a.rearrange("p (t o) -> p t o", o=1).to_broadcast([P, NT, n])

            logits = bank[4][:, 0:NT * E].rearrange("p (t e) -> p t e", e=E)
            pos = bank[5][:, 0:NT * E].rearrange("p (t e) -> p t e", e=E)
            for step in range(TAIL_STEPS):
                if step == 1:
                    for t in range(NT):
                        dve.wait_ge(o_full, t + 1)
                        dve.tensor_tensor(x[:, t, :], bank[4 + t][:, :], x[:, t, :], ALU.add).then_inc(res1, 1)
                    dve.wait_ge(res1, NT)
                if step in (2, 11):
                    for t in range(NT):
                        dve.bn_stats(stats[:, t, :], rows(step)(t)).then_inc(chain_p3, 1)
                    link.skip(NT)
                    for t in range(NT):
                        dve.bn_aggr(mv[:, t, :], stats[:, t, :]).then_inc(chain_p3, 1)
                    link.skip(NT)
                    dve.tensor_scalar(vare[:, :], mv[:, :, 1], EPS, None, ALU.add).then_inc(ln_var, 1)
                if step in (3, 12):
                    k = 0 if step == 3 else 1
                    dve.wait_ge(ln_rstd, k + 1)
                    for t in range(NT):
                        dve.tensor_scalar(rows(step)(t), rows(step)(t), mv[:, t, 0:1], rstd[:, t:t + 1],
                                          ALU.subtract, ALU.mult).then_inc(ln_done, 1)
                    dve.wait_ge(ln_done, NT * (k + 1))
                if step == 7:
                    dve.wait_ge(sq_done, 1)
                    link(dve.tensor_scalar(gl[0:S2, :], gl[0:S2, :], GELU_A, 1.0, ALU.mult, ALU.add))
                    dve.tensor_tensor(gl[0:S2, :], gl[0:S2, :], bank[4][0:S2, :], ALU.mult).then_inc(poly_done, 1)
                if step == 8:
                    dve.wait_ge(tanh_done, 1)
                    dve.scalar_tensor_tensor(out=gelu_out[0:S2, :], in0=gl[0:S2, :], scalar=1.0, in1=bank[4][0:S2, :],
                                             op0=ALU.add, op1=ALU.mult).then_inc(gelu_done, 1)
                if step == 10:
                    for t in range(NT):
                        dve.wait_ge(cy_full, t + 1)
                        dve.scalar_tensor_tensor(out=x2w[:, t, 0:D], in0=bank[4 + t][:, :], scalar=0.5, in1=x[:, t, :],
                                                 op0=ALU.mult, op1=ALU.add).then_inc(res2, 1)
                    dve.wait_ge(res2, NT)
                if step == 15:
                    dve.wait_ge(route_full, 1)
                    link(dve.tensor_reduce(nmx[:, :], logits, AX.X, ALU.max))
                    dve.tensor_tensor(expv[:, :, :], logits, over(nmx[:, :]), ALU.subtract).then_inc(shift_done, 1)
                if step == 16:
                    dve.wait_ge(expv_done, 1)
                    for t in range(NT):
                        dve.max(m8[:, t, :], expv[:, t, :]).then_inc(chain_p3, 1)
                    link.skip(NT)
                    for t in range(NT):
                        dve.match_replace(left[:, t, :], m8[:, t, :], expv[:, t, :], -1.0).then_inc(chain_p3, 1)
                    link.skip(NT)
                    link(dve.tensor_scalar(mask[:, :, :], left[:, :, :], -1.0, None, ALU.is_equal))
                    link(dve.tensor_copy(mask_b[:, :, :], mask[:, :, :]))
                    for t in range(NT):
                        dve.tensor_tensor(run[:, t + 1, :], run[:, t, :], mask_b[:, t, :], ALU.add).then_inc(mask_done, 1)
                        dve.wait_ge(mask_done, t + 1)
                if step == 17:
                    link(dve.tensor_tensor(expv[:, :, :], expv[:, :, :], mask[:, :, :], ALU.mult))
                    link(dve.tensor_reduce(wsum[:, :], expv[:, :, :], AX.X, ALU.add))
                    link(dve.reciprocal(wsum[:, :], wsum[:, :]))
                    dve.tensor_tensor(x2w[:, :, D:XW], expv[:, :, :], over(wsum[:, :]), ALU.mult).then_inc(w_done, 1)
                if step == 19:
                    dve.wait_ge(scattered, end * ALL_SCATTERED + ALL_SCATTERED)
                    link(dve.tensor_scalar(tok[:, :], tok[:, :], float(S), None, ALU.add))
                    dve.wait_ge(pos_full, 1)
                    link(dve.scalar_tensor_tensor(out=left[:, :, :], in0=pos, scalar=float(CAP), in1=mask[:, :, :],
                                                  op0=ALU.is_lt, op1=ALU.mult))
                    link(dve.tensor_tensor(enc[:, :, :], pos, slot1[:, :].rearrange("p (o e) -> p o e", o=1)
                                           .to_broadcast([P, NT, E]), ALU.add))
                    link(dve.tensor_tensor(enc[:, :, :], enc[:, :, :], left[:, :, :], ALU.mult))
                    for t in range(NT):
                        dve.max(m8[:, t, :], enc[:, t, :]).then_inc(chain_p3, 1)
                    link.skip(NT)
                    flat = m8[:, :, :].rearrange("p t k -> p (t k)")
                    link(dve.tensor_scalar(off[:, :], flat, 0.5, float(4 * E * CAP), ALU.is_lt, ALU.mult))
                    dve.tensor_tensor(idx[:, :], off[:, :], flat, ALU.add).then_inc(idx_done, 1)
                    link(dve.tensor_copy(run[:, 0, :], run[:, NT, :]))
                if step in SHARED_DVE:
                    f = SHARED_DVE.index(step)
                    gate_bank, up_bank = shared_banks(f)
                    dve.wait_ge(stanh_done, f + 1)
                    dve.scalar_tensor_tensor(out=hid[:, f, :], in0=hid[:, f, :], scalar=1.0, in1=gate_bank[:, :],
                                             op0=ALU.add, op1=ALU.mult).then_inc(hid_mid, 1)
                    dve.wait_ge(sg_full, 2 * f + 2)
                    dve.wait_ge(hid_mid, f + 1)
                    dve.tensor_tensor(hid[:, f, :], hid[:, f, :], up_bank[:, :], ALU.mult).then_inc(hid_done, 1)
                if step == 20:
                    for t in range(NT):
                        dve.wait_ge(sd_full, t + 1)
                        dve.scalar_tensor_tensor(out=x[:, t, :], in0=bank[DOWN_BANKS[t]][:, :], scalar=0.5,
                                                 in1=x2w[:, t, 0:D], op0=ALU.mult, op1=ALU.add).then_inc(acc_done, 1)
                yield

        def tail_pool(pool):
            for step in range(TAIL_STEPS):
                if step in (2, 11):
                    pool.wait_ge(ln_var, 1 if step == 2 else 2)
                    pool.tensor_tensor(rstd[:, :], vare[:, :], cst["mhalf"][:, 0:NT], ALU.pow).then_inc(ln_rstd, 1)
                if 4 <= step < 12:
                    for k in range((step - 4) * NT, (step - 3) * NT):
                        scatter(pool, k)
                yield

        def tail_stores(sp, b):
            sp.wait_ge(w_done, 1)
            sp.dma_start(scr["rows"][0:T, :].rearrange("(b t p) n -> b p t n", p=P, t=NT)[b], x2w[:, :, :])\
                .then_inc(stored, 16)
            sp.wait_ge(acc_done, NT)
            sp.dma_start(scr["acc"][0:T, :].rearrange("(b t p) n -> b p t n", p=P, t=NT)[b], x[:, :, :])\
                .then_inc(stored, 16)
            sp.wait_ge(stored, 32)

        ORDER = "tggggtttppgtptggttptptgtptgtptgtgtttggttggttgtgt"

        def in_order(tail, gate, proj=None):
            programs = {"t": tail, "g": gate, "p": proj}
            for which in ORDER:
                if programs[which] is not None:
                    next(programs[which], None)
            for program in programs.values():
                if program is not None:
                    for _ in program:
                        pass

        def between_heads(end, start):
            with nc.Block() as block:
                @block.sync
                def _(sp):
                    if start is not None:
                        sp.dma_start(xT[:, :, :], A["xT"][start].rearrange("(c p) n -> p c n", p=P)).then_inc(loaded, 16)
                        sp.wait_ge(loaded, 16)
                    if end is not None:
                        tail_stores(sp, end)

                @block.tensor
                def _(pe):
                    in_order(None if end is None else tail_pe(pe), None if start is None else gate_pe(pe),
                             None if start is None else late_projections(project, pe))

                @block.scalar
                def _(act):
                    in_order(None if end is None else tail_act(act), None if start is None else gate_act(act),
                             None if start is None else late_projections(drain_projection, act))

                @block.vector
                def _(dve):
                    in_order(None if end is None else tail_dve(dve, end), None if start is None else gate_dve(dve))

                @block.gpsimd
                def _(pool):
                    in_order(None if end is None else tail_pool(pool), None if start is None else gate_pool(pool))

        def clear():
            with nc.Block() as block:
                @block.vector
                def _(dve):
                    for s in sems:
                        dve.sem_clear(s)

        between_heads(None, 0)
        heads(0)
        clear()
        with nc.Fori(0, trips - 1) as b:
            between_heads(b, b + 1)
            heads(b + 1)
            clear()
        between_heads(trips - 1, None)
        with nc.Block() as block:
            @block.gpsimd
            def _(pool):
                for k in range(NT * TOPK):
                    scatter(pool, k)
                pool.wait_ge(scattered, (trips + 1) * ALL_SCATTERED)
        clear()


def constants(nc, ctx):
    def sb(name, shape, dt=FP32):
        return ctx.enter_context(nc.sbuf_tensor("cst_" + name, shape, dt))
    cst = {"ident": sb("ident", [P, P]), "upper": sb("upper", [P, P]), "ones": sb("ones", [P, P]),
           "upper_b": sb("upper_b", [P, P], BF16), "ones_b": sb("ones_b", [P, P], BF16), "mhalf": sb("mhalf", [P, NT]),
           "groups": sb("groups", [P, DH])}
    made = ctx.enter_context(nc.semaphore("constants_made"))
    with nc.Block() as block:
        @block.gpsimd
        def _(pool):
            pool.memset(cst["ones"][:, :], 1.0).then_inc(made, 1)
            pool.memset(cst["ones_b"][:, :], 1.0).then_inc(made, 1)
            pool.memset(cst["mhalf"][:, :], -0.5).then_inc(made, 1)
            pool.wait_ge(made, 3)
            for name, src, op in (("ident", "ones", ALU.is_equal), ("upper", "ones", ALU.is_gt),
                                  ("upper_b", "ones_b", ALU.is_gt)):
                pool.affine_select(out=cst[name][:, :], in_=cst[src][:, :], pattern=[[1, P]], compare_op=op,
                                   fill=0.0, base=0, channel_multiplier=-1).then_inc(made, 1)
            pool.wait_ge(made, 6)
    return cst


def experts_stage(nc, A, scr, cst):
    ident = cst["ident"]
    with ExitStack() as ctx:
        def sb(name, shape, dt=FP32):
            return ctx.enter_context(nc.sbuf_tensor("moe_" + name, shape, dt))

        def sem(name):
            return ctx.enter_context(nc.semaphore("moe_" + name))

        bank = [ctx.enter_context(nc.psum_tensor(f"moe_bank{i}", [P, 512], FP32)) for i in range(8)]
        NI = E // 2
        lists = sb("lists", [P, P])
        listsT = sb("listsT", [P, E * NJ])
        w_gu = [sb(f"w_gu{s}", [P, NC, 2 * F]) for s in range(2)]
        w_dn = [sb(f"w_dn{s}", [P, NF, D]) for s in range(2)]
        rows = [sb(f"rows{s}", [P, NJ, XW]) for s in range(2)]
        rowsT = [sb(f"rowsT{s}", [P, NC, CAP]) for s in range(2)]
        hid = [sb(f"hid{s}", [P, NF, CAP]) for s in range(2)]
        y = [sb(f"y{s}", [P, NJ, D]) for s in range(2)]
        gidx = [sb(f"gidx{s}", [P, NJ], I32) for s in range(2)]
        sidx = [sb(f"sidx{s}", [P, NJ], I32) for s in range(2)]
        wcur = [sb(f"wcur{s}", [P, NJ]) for s in range(2)]

        lists_in, lists_t, lists_out = sem("lists_in"), sem("lists_t"), sem("lists_out")
        gu_in = [sem(f"gu_in{s}") for s in range(2)]
        dn_in = [sem(f"dn_in{s}") for s in range(2)]
        gidx_ready, sidx_ready = sem("gidx_ready"), sem("sidx_ready")
        gathered = [sem(f"gathered{s}") for s in range(2)]
        t_full = sem("t_full")
        t_act, t_dve = sem("t_act"), sem("t_dve")
        w_taken = sem("w_taken")
        gu_full = sem("gu_full")
        tanh_done, hid_mid, hid_done = sem("tanh_done"), sem("hid_mid"), sem("hid_done")
        dn_full = sem("dn_full")
        y_done = sem("y_done")
        may_move = sem("may_move")
        added = sem("added")

        with nc.Block() as block:
            @block.sync
            def _(sp):
                sp.dma_start(lists[:, :], scr["slots"][1:E * CAP + 1, :].rearrange("(r n) o -> r (n o)", n=P))\
                    .then_inc(lists_in, 16)
                sp.wait_ge(lists_in, 16)

            @block.tensor
            def _(pe):
                pe.wait_ge(lists_in, 16)
                pe.transpose(bank[0][:, 0:P], lists[:, :], ident[:, :]).then_inc(lists_t, 1)

            @block.vector
            def _(dve):
                dve.wait_ge(lists_t, 1)
                dve.tensor_copy(listsT[:, :], bank[0][:, 0:P]).then_inc(lists_out, 1)
                dve.wait_ge(lists_out, 1)

        def over_pairs(eng, step):
            for s in range(2):
                step(s, s, 0, True, False)
            with eng.Fori(1, NI - 1) as i:
                for s in range(2):
                    step(i * 2 + s, s, i, False, False)
            for s in range(2):
                step(E - 2 + s, s, NI - 1, False, True)

        with nc.Block() as block:
            @block.sync
            def _(sp):
                def step(e, s, i, first, last):
                    if not first:
                        sp.wait_ge(gu_full, e * NF - NF)
                    sp.dma_start(w_gu[s][:, :, 0:F], A["w_gate"][e].rearrange("(c p) n -> p c n", p=P)).then_inc(gu_in[s], 16)
                    sp.dma_start(w_gu[s][:, :, F:2 * F], A["w_up"][e].rearrange("(c p) n -> p c n", p=P)).then_inc(gu_in[s], 16)
                    if not first:
                        sp.wait_ge(dn_full, e * NJ - NJ)
                    sp.dma_start(w_dn[s][:, :, :], A["w_down"][e].rearrange("(c p) n -> p c n", p=P)).then_inc(dn_in[s], 16)
                over_pairs(sp, step)

            @block.tensor
            def _(pe):
                def transposes(e, s, i, start=False):
                    pe.wait_ge(gathered[s], i * 32 + 32)
                    for j in range(NJ):
                        if not start:
                            pe.wait_ge(t_dve if j else t_act, e)
                        for c in range(NC):
                            mm = pe.transpose(bank[j][:, c * P:(c + 1) * P], rows[s][:, j, c * P:(c + 1) * P], ident[:, :])
                        mm.then_inc(t_full, 1)

                def down(e, s, i, start=False):
                    pe.wait_ge(dn_in[s], i * 16 + 16)
                    pe.wait_ge(hid_done, e * NF + NF)
                    for j in range(NJ):
                        if not start:
                            pe.wait_ge(y_done, e * NJ - NJ + j + 1)
                        for f in range(NF):
                            mm = pe.matmul(bank[5 + j][:, :], hid[s][:, f, j * P:(j + 1) * P], w_dn[s][:, f, :],
                                           start=(f == 0), stop=(f == NF - 1))
                        mm.then_inc(dn_full, 1)

                def step(e, s, i, first, last):
                    pe.wait_ge(gu_in[s], i * 32 + 32)
                    pe.wait_ge(t_act, e + 1)
                    pe.wait_ge(t_dve, e + 1)
                    for f in range(NF):
                        if not (first and s == 0):
                            pe.wait_ge(hid_done, e * NF - NF + f + 1)
                        for half in range(2):
                            for c in range(NC):
                                at = half * F + f * P
                                mm = pe.matmul(bank[2 + f][:, half * CAP:(half + 1) * CAP], w_gu[s][:, c, at:at + P],
                                               rowsT[s][:, c, :], start=(c == 0), stop=(c == NC - 1))
                        mm.then_inc(gu_full, 1)
                    if not (last and s == 1):
                        transposes(e + 1, 1 - s, i + s)
                    if not (first and s == 0):
                        down(e - 1, 1 - s, i + s - 1, start=(first and s == 1))

                transposes(0, 0, 0, start=True)
                over_pairs(pe, step)
                down(E - 1, 1, NI - 1)

            @block.scalar
            def _(act):
                def turn(e, s, first):
                    act.wait_ge(t_full, e * NJ + 1)
                    if not first:
                        act.wait_ge(gu_full, e * NF - NF)
                    act.activation(rowsT[s][:, :, 0:P], bank[0][:, :].rearrange("p (c q) -> p c q", q=P), ACT.Copy)\
                        .then_inc(t_act, 1)

                def out(e, s, first):
                    for j in range(NJ):
                        act.wait_ge(dn_full, e * NJ + j + 1)
                        if not first:
                            act.wait_ge(added, e * 32 - 32)
                        act.activation(y[s][:, j, :], bank[5 + j][:, :], ACT.Copy, scale=wcur[s][:, j:j + 1])\
                            .then_inc(y_done, 1)

                def step(e, s, i, first, last):
                    for f in range(NF):
                        act.wait_ge(gu_full, e * NF + f + 1)
                        if not first:
                            act.wait_ge(dn_full, e * NJ - NJ)
                        act.activation(hid[s][:, f, :], bank[2 + f][:, 0:CAP], ACT.Tanh, scale=0.5).then_inc(tanh_done, 1)
                    if not (last and s == 1):
                        turn(e + 1, 1 - s, first and s == 0)
                    if not (first and s == 0):
                        act.wait_ge(w_taken, e)
                        out(e - 1, 1 - s, (first and s == 1))

                turn(0, 0, True)
                over_pairs(act, step)
                out(E - 1, 1, False)

            @block.vector
            def _(dve):
                def prepare(e, s, i, first):
                    dve.wait_ge(t_full, e * NJ + 2)
                    if not first:
                        dve.wait_ge(gu_full, e * NF - NF)
                    dve.tensor_copy(rowsT[s][:, :, P:2 * P], bank[1][:, :].rearrange("p (c q) -> p c q", q=P))\
                        .then_inc(t_dve, 1)
                    if not first:
                        dve.wait_ge(y_done, e * NJ - NJ)
                        dve.wait_ge(added, e * 32 - 32)
                    dve.tensor_scalar(wcur[s][:, :], rows[s][:, :, bass.ds(e + D, 1)].rearrange("p j o -> p (j o)"),
                                      0.5, None, ALU.mult).then_inc(w_taken, 1)
                    dve.tensor_copy(sidx[s][:, :], listsT[:, bass.ds(e * NJ, NJ)]).then_inc(sidx_ready, 1)

                def gather_list(e, s):
                    dve.tensor_copy(gidx[s][:, :], listsT[:, bass.ds(e * NJ, NJ)]).then_inc(gidx_ready, 1)

                def step(e, s, i, first, last):
                    for f in range(NF):
                        dve.wait_ge(tanh_done, e * NF + f + 1)
                        dve.scalar_tensor_tensor(out=hid[s][:, f, :], in0=hid[s][:, f, :], scalar=1.0,
                                                 in1=bank[2 + f][:, 0:CAP], op0=ALU.add, op1=ALU.mult).then_inc(hid_mid, 1)
                        dve.wait_ge(hid_mid, e * NF + f + 1)
                        dve.tensor_tensor(hid[s][:, f, :], hid[s][:, f, :], bank[2 + f][:, CAP:2 * CAP], ALU.mult)\
                            .then_inc(hid_done, 1)
                    if not last:
                        dve.wait_ge(gathered[s], i * 32 + 32)
                        gather_list(e + 2, s)
                    if not (last and s == 1):
                        prepare(e + 1, 1 - s, i + s, first and s == 0)

                gather_list(0, 0)
                gather_list(1, 1)
                prepare(0, 0, 0, True)
                over_pairs(dve, step)

            @block.gpsimd
            def _(pool):
                def gather(e, s):
                    pool.wait_ge(gidx_ready, e + 1)
                    pool.sem_inc(may_move, 1)
                    for j in range(NJ):
                        pool.indirect_dma_start(
                            out=rows[s][:, j, :], out_offset=None, in_=scr["rows"][:, :],
                            in_offset=bass.IndirectOffsetOnAxis(ap=gidx[s][:, j:j + 1], axis=0)).then_inc(gathered[s], 16)

                def step(e, s, i, first, last):
                    if not last:
                        pool.wait_ge(t_full, e * NJ + NJ)
                        pool.wait_ge(w_taken, e + 1)
                        gather(e + 2, s)
                    if not (first and s == 0):
                        pool.wait_ge(added, e * 32)
                    pool.wait_ge(y_done, e * NJ + NJ)
                    pool.wait_ge(sidx_ready, e + 1)
                    pool.sem_inc(may_move, 1)
                    for j in range(NJ):
                        pool.indirect_dma_start(
                            out=scr["acc"][:, :], out_offset=bass.IndirectOffsetOnAxis(ap=sidx[s][:, j:j + 1], axis=0),
                            in_=y[s][:, j, :], in_offset=None, compute_op=ALU.add).then_inc(added, 16)

                gather(0, 0)
                gather(1, 1)
                over_pairs(pool, step)
                pool.wait_ge(added, E * 32)


RING = 3


def layer1_attention_stage(nc, A, scr, cst, trips):
    ident = cst["ident"]
    with ExitStack() as ctx:
        def sb(name, shape, dt=FP32):
            return ctx.enter_context(nc.sbuf_tensor("l1_" + name, shape, dt))

        sems = []

        def sem(name):
            s = ctx.enter_context(nc.semaphore("l1_" + name))
            sems.append(s)
            return s

        psum = ctx.enter_context(nc.psum_tensor("l1_psum", [P, 8, 512], FP32))
        bank = [psum[:, i, :] for i in range(8)]

        w_qkv = sb("w_qkv", [P, NC, 3 * D])
        w_o = sb("w_o", [P, NC, D])
        w_xo = sb("w_xo", [P, NC, D])
        w_xdiag = sb("w_xdiag", [P, 3, P])
        w_conv = sb("w_conv", [P, 2, NC, DH])
        wcol = sb("wcol", [P, 2, NC])
        b_conv = sb("b_conv", [P, 2])
        b_qkv = sb("b_qkv", [P, 3 * NC])
        b_o = sb("b_o", [P, D])
        b_xo = sb("b_xo", [P, D])
        x_new = sb("x_new", [P, NT, D])
        x = sb("x", [P, NT, D])
        xT = sb("xT", [P, NC, S])
        q_parts = [sb("q_high", [P, NC, S]), sb("q_low", [P, NC, S])]
        k_parts = [sb("k_high", [P, NC, S]), sb("k_low", [P, NC, S])]
        q_stack = sb("q_stack", [P, RING, 2, S])
        k_stack = sb("k_stack", [P, RING, 2, S])
        v = sb("v", [P, NT, D])
        yT = xT
        probs = sb("probs", [P, 4, 2, S])
        pT = sb("pT", [P, HG, NT, S])
        ctx_T = sb("ctx_T", [P, NC, S2])
        kxpad = sb("kxpad", [P, H, S2])
        vx = sb("vx", [P, D])
        seen = sb("seen", [P, NT, S2], I32)
        floor = sb("floor", [P, NT, S2])
        pxT = [pT[:, i, :, :] for i in range(2)]
        x4T, qxT, x5T, xc = pT[:, 2, :, :], pT[:, 3, :, :], pT[:, 2, :, :], pT[:, 3, 0:2, :]
        px = [probs[:, i, 0, 0:HG * S2].rearrange("p (h k) -> p h k", h=HG) for i in range(4)]
        yxT = probs[:, :, 1, :]
        nmax = sb("nmax", [P, 4, 2])
        psums = sb("psums", [P, 4, 2])
        rsum = sb("rsum", [P, 4, 2])
        xmax = sb("xmax", [P, 4, HG])
        xsum = sb("xsum", [P, 4, HG])
        xrsum = sb("xrsum", [P, 4, HG])

        setup_in, setup_zero, setup_conv = sem("setup_in"), sem("setup_zero"), sem("setup_conv")
        with nc.Block() as block:
            @block.sync
            def _(sp):
                for dst, src in ((w_qkv, A["w_qkv1"]), (w_o, A["w_o1"]), (w_xo, A["w_xo"])):
                    sp.dma_start(dst[:, :, :], src.rearrange("(c p) n -> p c n", p=P)).then_inc(setup_in, 16)
                sp.dma_start(b_qkv[:, :], A["b_qkv1"]).then_inc(setup_in, 16)
                for dst, src in ((b_o, A["b_o1"]), (b_xo, A["b_xo"])):
                    sp.dma_start(dst[:, :], src.rearrange("(a n) -> a n", a=1).to_broadcast([P, D])).then_inc(setup_in, 16)
                sp.dma_start(wcol[:, :, :], A["conv_w"]).then_inc(setup_in, 16)
                sp.dma_start(b_conv[:, :], A["conv_b"]).then_inc(setup_in, 16)
                sp.wait_ge(setup_zero, 1)
                for i in range(3):
                    for h in range(HG):
                        sp.dma_start(w_xdiag[h * DH:(h + 1) * DH, i, h * DH:(h + 1) * DH], A["w_x"][i])\
                            .then_inc(setup_in, 16)
                sp.wait_ge(setup_in, (8 + 3 * HG) * 16)

            @block.vector
            def _(dve):
                dve.memset(w_xdiag[:, :, :], 0.0).then_inc(setup_zero, 1)
                dve.memset(kxpad[:, :, :], 0.0)
                dve.memset(vx[:, :], 0.0)
                dve.wait_ge(setup_in, (8 + 3 * HG) * 16)
                dve.tensor_scalar(b_qkv[:, 0:NC], b_qkv[:, 0:NC], QSCALE, None, ALU.mult)
                dve.tensor_scalar(w_qkv[:, :, 0:D], w_qkv[:, :, 0:D], QSCALE, None, ALU.mult)
                dve.wait_ge(setup_conv, 2)
                for br in range(2):
                    for c in range(NC):
                        dve.tensor_scalar(w_conv[:, br, c, :], cst["groups"][:, :], wcol[:, br, c:c + 1], None, ALU.mult)

            @block.gpsimd
            def _(pool):
                pool.affine_select(out=cst["groups"][:, :], in_=cst["ones"][:, 0:DH], pattern=[[-4, DH]],
                                   compare_op=ALU.is_ge, fill=0.0, base=0, channel_multiplier=1).then_inc(setup_conv, 1)
                pool.wait_ge(setup_conv, 1)
                pool.affine_select(out=cst["groups"][:, :], in_=cst["groups"][:, :], pattern=[[4, DH]],
                                   compare_op=ALU.is_ge, fill=0.0, base=3, channel_multiplier=-1).then_inc(setup_conv, 1)

        class Norm:
            def __init__(self, name):
                self.stats, self.mv = sb(name + "_stats", [P, NT, 6]), sb(name + "_mv", [P, NT, 2])
                self.vare, self.rstd = sb(name + "_vare", [P, NT]), sb(name + "_rstd", [P, NT])
                self.var, self.root, self.done = sem(name + "_var"), sem(name + "_root"), sem(name + "_done")
                self.chain = sem(name + "_chain")

            def statistics(self, dve, link, rows):
                for t in range(NT):
                    dve.bn_stats(self.stats[:, t, :], rows[:, t, :]).then_inc(self.chain, 1)
                link.skip(NT)
                for t in range(NT):
                    dve.bn_aggr(self.mv[:, t, :], self.stats[:, t, :]).then_inc(self.chain, 1)
                link.skip(NT)
                dve.tensor_scalar(self.vare[:, :], self.mv[:, :, 1], EPS, None, ALU.add).then_inc(self.var, 1)

            def reciprocal_root(self, pool, k):
                pool.wait_ge(self.var, k + 1)
                pool.tensor_tensor(self.rstd[:, :], self.vare[:, :], cst["mhalf"][:, 0:NT], ALU.pow)\
                    .then_inc(self.root, 1)

            def normalise(self, dve, k, rows):
                dve.wait_ge(self.root, k + 1)
                for t in range(NT):
                    dve.tensor_scalar(rows[:, t, :], rows[:, t, :], self.mv[:, t, 0:1], self.rstd[:, t:t + 1],
                                      ALU.subtract, ALU.mult).then_inc(self.done, 1)
                dve.wait_ge(self.done, NT * (k + 1))

        norm_new, norm = Norm("norm_new"), Norm("norm")

        loaded = sem("loaded")
        turned, turned_out = sem("turned"), sem("turned_out")
        proj_full = sem("proj_full")
        PROJ = [("q", 0), ("k", 0), ("q", 1), ("k", 1), ("v", 0), ("v", 1), ("v", 2), ("v", 3),
                ("q", 2), ("k", 2), ("q", 3), ("k", 3)]
        high_done = sem("high_done")
        low_done = sem("low_done")
        v_done = sem("v_done")

        def parts_of(j):
            return sum(kind != "v" for kind, _ in PROJ[:j + 1])

        def wait_drained(eng, j):
            if PROJ[j][0] == "v":
                eng.wait_ge(v_done, j + 1 - parts_of(j))
            else:
                eng.wait_ge(low_done, parts_of(j))

        START_STEPS = 4 + len(PROJ)

        def start_pe(pe):
            for step in range(START_STEPS):
                if step in (2, 3):
                    for t in (2 * step - 4, 2 * step - 3):
                        pe.wait_ge(norm_new.done, t + 1)
                        if t >= 2:
                            pe.wait_ge(turned_out, t - 1)
                        for c in range(NC):
                            mm = pe.transpose(bank[t % 2][:, c * P:(c + 1) * P], x_new[:, t, c * P:(c + 1) * P], ident[:, :])
                        mm.then_inc(turned, 1)
                if step >= 4:
                    j = step - 4
                    kind, i = PROJ[j]
                    if j == 0:
                        pe.wait_ge(turned_out, NT)
                    if j >= 2:
                        wait_drained(pe, j - 2)
                    for c in range(NC):
                        if kind == "v":
                            mm = pe.matmul(bank[j % 2], xT[:, c, i * P:(i + 1) * P], w_qkv[:, c, 2 * D:3 * D],
                                           start=(c == 0), stop=(c == NC - 1))
                        else:
                            at = i * P + (D if kind == "k" else 0)
                            mm = pe.matmul(bank[j % 2], w_qkv[:, c, at:at + P], xT[:, c, :],
                                           start=(c == 0), stop=(c == NC - 1))
                    mm.then_inc(proj_full, 1)
                yield

        def start_act(act):
            for step in range(START_STEPS):
                if step in (2, 3):
                    for t in (2 * step - 4, 2 * step - 3):
                        act.wait_ge(turned, t + 1)
                        act.activation(xT[:, :, t * P:(t + 1) * P], bank[t % 2].rearrange("p (c q) -> p c q", q=P),
                                       ACT.Copy).then_inc(turned_out, 1)
                if step >= 4:
                    j = step - 4
                    kind, i = PROJ[j]
                    act.wait_ge(proj_full, j + 1)
                    src = bank[j % 2]
                    if kind == "v":
                        act.activation(v[:, i, :], src, ACT.Copy).then_inc(v_done, 1)
                    else:
                        at = i + (NC if kind == "k" else 0)
                        high = (k_parts if kind == "k" else q_parts)[0]
                        act.activation(high[:, i, :].bitcast(F32R), src, ACT.Identity, bias=b_qkv[:, at:at + 1])\
                            .then_inc(high_done, 1)
                yield

        def start_dve(dve):
            link = chain_of(dve, norm_new.chain)
            dve.wait_ge(loaded, 16)
            norm_new.statistics(dve, link, x_new)
            yield
            norm_new.normalise(dve, 0, x_new)
            for step in range(1, START_STEPS):
                yield
                j = step - 4
                if j >= 0 and PROJ[j][0] != "v":
                    kind, i = PROJ[j]
                    at = i + (NC if kind == "k" else 0)
                    high, low = k_parts if kind == "k" else q_parts
                    dve.wait_ge(high_done, parts_of(j))
                    dve.scalar_tensor_tensor(out=low[:, i, :].bitcast(F32R), in0=bank[j % 2], scalar=b_qkv[:, at:at + 1],
                                             in1=high[:, i, :], op0=ALU.add, op1=ALU.subtract).then_inc(low_done, 1)

        def start_pool(pool):
            norm_new.reciprocal_root(pool, 0)
            yield

        stack_in = [sem(f"stack_in{i}") for i in range(RING)]
        PAIRS = 2 * NC

        def stack_pair(sp, u):
            for hh in range(2):
                r = slice((2 * (u % 2) + hh) * DH, (2 * (u % 2) + hh + 1) * DH)
                for place in range(4):
                    to = slice(place * DH, (place + 1) * DH)
                    for stack, part in ((q_stack, q_parts[place // 2]), (k_stack, k_parts[place % 2])):
                        sp.dma_start(stack[to, u % RING, hh, :], part[r, u // 2, :]).then_inc(stack_in[u % RING], 16)

        tail_in, resid = sem("tail_in"), sem("resid")
        scores_full, max_ready, exp_done = sem("scores_full"), sem("max_ready"), sem("exp_done")
        rsum_ready, probs_ready = sem("rsum_ready"), sem("probs_ready")
        pT_full, pT_out_dve, pT_out_act = sem("pT_full"), sem("pT_out_dve"), sem("pT_out_act")
        attn_full, attn_out = sem("attn_full"), sem("attn_out")
        LAG = 3
        UNITS = [(g, t, p) for g in range(NC) for p in range(2) for t in range(NT)]
        PER_G = 2 * NT

        def heads(b):
            N = len(UNITS)
            with nc.Block() as block:
                @block.sync
                def _(sp):
                    sp.dma_start(ctx_T[:, :, :], A["ctxT"][b].rearrange("(c p) n -> p c n", p=P)).then_inc(tail_in, 16)
                    sp.dma_start(seen[:, :, :], A["mask"][b].rearrange("(t p) n -> p t n", p=P)).then_inc(tail_in, 16)
                    for u in range(RING, PAIRS):
                        sp.wait_ge(scores_full, (u - RING + 1) * NT)
                        stack_pair(sp, u)
                    sp.wait_ge(tail_in, 32)
                    for i in range(RING):
                        sp.wait_ge(stack_in[i], len(range(i, PAIRS, RING)) * 16 * 16)

                @block.tensor
                def _(pe):
                    for n in range(N + LAG + 1):
                        if n < N:
                            g, t, p = UNITS[n]
                            u = 2 * g + p
                            pe.wait_ge(stack_in[u % RING], (u // RING + 1) * 16 * 16)
                            if n >= 2:
                                pe.wait_ge(exp_done, 2 * (n - 1))
                            for hh in range(2):
                                mm = pe.matmul(bank[2 * (n % 2) + hh],
                                               q_stack[:, u % RING, hh, t * P:(t + 1) * P].bitcast(F32R),
                                               k_stack[:, u % RING, hh, :].bitcast(F32R), start=True, stop=True)
                            mm.then_inc(scores_full, 1)
                        m = n - LAG
                        if m >= PER_G and m % PER_G == 0:
                            g = m // PER_G - 1
                            pe.wait_ge(pT_out_dve, m)
                            pe.wait_ge(pT_out_act, m)
                            if g >= 1:
                                pe.wait_ge(attn_out, g)
                            for kc in range(NT):
                                for h in range(HG):
                                    mm = pe.matmul(psum[h * DH:(h + 1) * DH, 6, :],
                                                   v[:, kc, (HG * g + h) * DH:(HG * g + h + 1) * DH],
                                                   pT[:, h, kc, :], start=(kc == 0), stop=(kc == NT - 1))
                            mm.then_inc(attn_full, 1)
                        if 0 <= m < N:
                            pe.wait_ge(probs_ready, m + 1)
                            for hh in range(2):
                                if m >= 1:
                                    pe.wait_ge(pT_out_act if hh else pT_out_dve, m)
                                for kc in range(NT):
                                    mm = pe.transpose(bank[4 + hh][:, kc * P:(kc + 1) * P],
                                                      probs[:, m % 4, hh, kc * P:(kc + 1) * P], ident[:, :])
                                mm.then_inc(pT_full, 1)

                @block.vector
                def _(dve):
                    for n in range(N + LAG):
                        if n < N:
                            dve.wait_ge(scores_full, n + 1)
                            if n >= 4:
                                dve.wait_ge(exp_done, 2 * (n - 3))
                            dve.tensor_reduce(nmax[:, n % 4, :], psum[:, 2 * (n % 2):2 * (n % 2) + 2, :], AX.X, ALU.max,
                                              negate=True).then_inc(max_ready, 1)
                        m = n - 1
                        if 0 <= m < N:
                            dve.wait_ge(exp_done, 2 * m + 2)
                            if m >= 4:
                                dve.wait_ge(probs_ready, m - 3)
                            dve.reciprocal(rsum[:, m % 4, :], psums[:, m % 4, :]).then_inc(rsum_ready, 1)
                        m = n - LAG
                        if 0 <= m < N:
                            g, t, p = UNITS[m]
                            dve.wait_ge(pT_full, 2 * m + 1)
                            if g >= 1:
                                dve.wait_ge(attn_full, g)
                            dve.tensor_copy(pT[:, 2 * p, :, t * P:(t + 1) * P],
                                            bank[4].rearrange("p (k q) -> p k q", q=P)).then_inc(pT_out_dve, 1)

                @block.scalar
                def _(act):
                    for n in range(N + LAG + 1):
                        if n < N:
                            act.wait_ge(max_ready, n + 1)
                            if n >= 4:
                                act.wait_ge(pT_full, 2 * (n - 3))
                                act.wait_ge(rsum_ready, n - 3)
                            for hh in range(2):
                                act.activation(probs[:, n % 4, hh, :], bank[2 * (n % 2) + hh], ACT.Exp,
                                               bias=nmax[:, n % 4, hh:hh + 1],
                                               accum_out=psums[:, n % 4, hh:hh + 1]).then_inc(exp_done, 1)
                        m = n - LAG
                        if 0 <= m < N:
                            g, t, p = UNITS[m]
                            act.wait_ge(pT_full, 2 * m + 2)
                            if g >= 1:
                                act.wait_ge(attn_full, g)
                            act.activation(pT[:, 2 * p + 1, :, t * P:(t + 1) * P],
                                           bank[5].rearrange("p (k q) -> p k q", q=P), ACT.Copy).then_inc(pT_out_act, 1)
                        if m >= PER_G and m % PER_G == 0:
                            g = m // PER_G - 1
                            act.wait_ge(attn_full, g + 1)
                            act.activation(yT[:, g, :], bank[6], ACT.Identity,
                                           bias=b_qkv[:, 2 * NC + g:2 * NC + g + 1]).then_inc(attn_out, 1)

                @block.gpsimd
                def _(pool):
                    for n in range(N):
                        pool.wait_ge(rsum_ready, n + 1)
                        pr = probs[:, n % 4, :, :]
                        pool.tensor_tensor(pr, pr, rsum[:, n % 4, :].rearrange("p (h a) -> p h a", a=1)
                                           .to_broadcast([P, 2, S]), ALU.mult).then_inc(probs_ready, 1)
                    for t in range(NT):
                        pool.tensor_tensor(x[:, t, :], x_new[:, t, :], b_o[:, :], ALU.add).then_inc(resid, 1)
                    pool.wait_ge(resid, NT)

        kx_full, kx_out = sem("kx_full"), sem("kx_out")
        floor_done = sem("floor_done")
        o_full, res1 = sem("o_full"), sem("res1")
        t_full, t_out = sem("t_full"), sem("t_out")
        qx_full, qx_out = sem("qx_full"), sem("qx_out")
        resid2 = sem("resid2")
        xs_full, xs_out = sem("xs_full"), sem("xs_out")
        xsub_done, xexp_done, xrsum_ready, xprobs_ready = (sem(n) for n in ("xsub", "xexp", "xrsum_ready", "xprobs"))
        xpT_full, xpT_out = sem("xpT_full"), sem("xpT_out")
        xa_full, xa_out = sem("xa_full"), sem("xa_out")
        xo_full, res2 = sem("xo_full"), sem("res2")
        conv_full, conv_out, stored = sem("conv_full"), sem("conv_out"), sem("stored")
        chain_x = sem("chain_x")
        XU = [(g, t) for g in range(NC) for t in range(NT)]
        XLAG = 2
        NX = len(XU)

        FIRST_UNIT = 6
        AFTER = FIRST_UNIT + NX + XLAG + 1
        TAIL_STEPS = AFTER + 6

        def transposes(pe, k):
            for t in range(NT):
                pe.wait_ge(norm.done, k * NT + t + 1)
                for c in range(NC):
                    mm = pe.transpose(bank[4 + t][:, c * P:(c + 1) * P], x[:, t, c * P:(c + 1) * P], ident[:, :])
                mm.then_inc(t_full, 1)

        def transposes_out(act, k, dst):
            for t in range(NT):
                act.wait_ge(t_full, k * NT + t + 1)
                act.activation(dst[:, :, t * P:(t + 1) * P], bank[4 + t].rearrange("p (c q) -> p c q", q=P),
                               ACT.Copy).then_inc(t_out, 1)

        def tail_pe(pe):
            for step in range(TAIL_STEPS):
                n = step - FIRST_UNIT
                m = n - XLAG
                if step == 0:
                    for t in range(NT):
                        for c in range(NC):
                            mm = pe.matmul(bank[4 + t], yT[:, c, t * P:(t + 1) * P], w_o[:, c, :],
                                           start=(c == 0), stop=(c == NC - 1))
                        mm.then_inc(o_full, 1)
                    for c in range(NC):
                        mm = pe.matmul(bank[2][:, c * S2:(c + 1) * S2], w_xdiag[:, 1, :], ctx_T[:, c, :],
                                       start=True, stop=True)
                    mm.then_inc(kx_full, 1)
                    for c in range(NC):
                        mm = pe.matmul(bank[3][0:S2, c * P:(c + 1) * P], ctx_T[:, c, :], w_xdiag[:, 2, :],
                                       start=True, stop=True)
                    mm.then_inc(kx_full, 1)
                if step == 4:
                    transposes(pe, 0)
                if step == 5:
                    pe.wait_ge(t_out, NT)
                    for c in range(NC):
                        pe.matmul(bank[4 + c], w_xdiag[:, 0, :], x4T[:, c, :], start=True, stop=True).then_inc(qx_full, 1)
                if 0 <= n < NX:
                    g, t = XU[n]
                    if n == 0:
                        pe.wait_ge(kx_out, 2)
                        pe.wait_ge(qx_out, NC)
                    if n >= 2:
                        pe.wait_ge(xs_out, n - 1)
                    pe.matmul(bank[2 + n % 2][:, 0:HG * S2], qxT[:, g, t * P:(t + 1) * P],
                              kxpad[:, g * HG:(g + 1) * HG, :].rearrange("p h k -> p (h k)"),
                              start=True, stop=True).then_inc(xs_full, 1)
                if NT <= m <= NX and m % NT == 0:
                    g = m // NT - 1
                    pe.wait_ge(xpT_out, m)
                    if g >= 2:
                        pe.wait_ge(xa_out, g - 1)
                    for h in range(HG):
                        mm = pe.matmul(psum[h * DH:(h + 1) * DH, 4 + g % 2, :], vx[:, (g * HG + h) * DH:(g * HG + h + 1) * DH],
                                       pxT[g % 2][:, h, :], start=True, stop=True)
                    mm.then_inc(xa_full, 1)
                if 0 <= m < NX:
                    pe.wait_ge(xprobs_ready, m + 1)
                    if m >= 2:
                        pe.wait_ge(xpT_out, m - 1)
                    for h in range(HG):
                        mm = pe.transpose(bank[6 + m % 2][0:S2, h * P:(h + 1) * P], px[m % 4][:, h, :], ident[:, :])
                    mm.then_inc(xpT_full, 1)
                if step == AFTER:
                    pe.wait_ge(xa_out, NC)
                    pe.wait_ge(xs_out, NX)
                    for t in range(NT):
                        for c in range(NC):
                            mm = pe.matmul(bank[4 + t], yxT[:, c, t * P:(t + 1) * P], w_xo[:, c, :],
                                           start=(c == 0), stop=(c == NC - 1))
                        mm.then_inc(xo_full, 1)
                if step == AFTER + 4:
                    transposes(pe, 1)
                if step == AFTER + 5:
                    pe.wait_ge(t_out, 2 * NT)
                    for br in range(2):
                        for c in range(NC):
                            mm = pe.matmul(psum[c * DH:(c + 1) * DH, 2 + br, :], w_conv[:, br, c, :], x5T[:, c, :],
                                           start=True, stop=True)
                        mm.then_inc(conv_full, 1)
                yield

        def tail_act(act):
            for step in range(TAIL_STEPS):
                n = step - FIRST_UNIT
                m = n - XLAG
                if step == 0:
                    act.wait_ge(kx_full, 1)
                    for h in range(HG):
                        r = slice(h * DH, (h + 1) * DH)
                        last = act.activation(kxpad[r, :, :].rearrange("p (c h) k -> p c h k", h=HG)[:, :, h, :],
                                              psum[r, 2, 0:NC * S2].rearrange("p (c k) -> p c k", k=S2), ACT.Copy)
                    last.then_inc(kx_out, 1)
                    act.wait_ge(kx_full, 2)
                    act.activation(vx[0:S2, :], psum[0:S2, 3, :], ACT.Copy).then_inc(kx_out, 1)
                if step == 4:
                    transposes_out(act, 0, x4T)
                if step == 5:
                    for c in range(NC):
                        act.wait_ge(qx_full, c + 1)
                        act.activation(qxT[:, c, :], bank[4 + c], ACT.Copy).then_inc(qx_out, 1)
                if 0 <= n < NX:
                    act.wait_ge(xsub_done, n + 1)
                    act.activation(px[n % 4], px[n % 4], ACT.Exp, scale=XSCALE).then_inc(xexp_done, 1)
                if 0 <= m < NX:
                    g, t = XU[m]
                    act.wait_ge(xpT_full, m + 1)
                    act.activation(pxT[g % 2][0:S2, :, t * P:(t + 1) * P],
                                   psum[0:S2, 6 + m % 2, :].rearrange("p (h q) -> p h q", q=P), ACT.Copy)\
                        .then_inc(xpT_out, 1)
                if NT <= m <= NX and m % NT == 0:
                    g = m // NT - 1
                    act.wait_ge(xa_full, g + 1)
                    act.activation(yxT[:, g, :], bank[4 + g % 2], ACT.Copy).then_inc(xa_out, 1)
                if step == AFTER + 4:
                    transposes_out(act, 1, x5T)
                if step == AFTER + 5:
                    for br in range(2):
                        act.wait_ge(conv_full, br + 1)
                        act.activation(xc[:, br, :], bank[2 + br], ACT.Identity, bias=b_conv[:, br:br + 1])\
                            .then_inc(conv_out, 1)
                yield

        def tail_dve(dve):
            link = chain_of(dve, norm.chain)
            xlink = chain_of(dve, chain_x)

            def each(a):
                return a.rearrange("p (h o) -> p h o", o=1).to_broadcast([P, HG, S2])

            for step in range(TAIL_STEPS):
                n = step - FIRST_UNIT
                m = n - 1
                if step == 0:
                    xlink(dve.tensor_scalar(floor[:, :, :], seen[:, :, :], 0.0, -TAKEN, ALU.not_equal, ALU.mult))
                    xlink(dve.tensor_scalar(floor[:, :, :], floor[:, :, :], 1e20, None, ALU.subtract))
                if step == 1:
                    for t in range(NT):
                        dve.wait_ge(o_full, t + 1)
                        dve.tensor_tensor(x[:, t, :], bank[4 + t], x[:, t, :], ALU.add).then_inc(res1, 1)
                    dve.wait_ge(res1, NT)
                if step == 2:
                    norm.statistics(dve, link, x)
                if step == 3:
                    norm.normalise(dve, 0, x)
                if 0 <= n < NX:
                    g, t = XU[n]
                    dve.wait_ge(xs_full, n + 1)
                    if n >= 4:
                        dve.wait_ge(xpT_full, n - 3)
                    dve.tensor_tensor(px[n % 4], bank[2 + n % 2][:, 0:HG * S2].rearrange("p (h k) -> p h k", h=HG),
                                      floor[:, t, :].rearrange("p (o k) -> p o k", o=1).to_broadcast([P, HG, S2]),
                                      ALU.min).then_inc(xs_out, 1)
                    dve.wait_ge(xs_out, n + 1)
                    xlink(dve.tensor_reduce(xmax[:, n % 4, :], px[n % 4], AX.X, ALU.max))
                    dve.tensor_tensor(px[n % 4], px[n % 4], each(xmax[:, n % 4, :]), ALU.subtract).then_inc(xsub_done, 1)
                if 0 <= m < NX:
                    dve.wait_ge(xexp_done, m + 1)
                    xlink(dve.tensor_reduce(xsum[:, m % 4, :], px[m % 4], AX.X, ALU.add))
                    if m >= 4:
                        dve.wait_ge(xprobs_ready, m - 3)
                    dve.reciprocal(xrsum[:, m % 4, :], xsum[:, m % 4, :]).then_inc(xrsum_ready, 1)
                if step == AFTER + 1:
                    for t in range(NT):
                        dve.wait_ge(xo_full, t + 1)
                        dve.wait_ge(resid2, t + 1)
                        dve.tensor_tensor(x[:, t, :], bank[4 + t], x[:, t, :], ALU.add).then_inc(res2, 1)
                    dve.wait_ge(res2, NT)
                if step == AFTER + 2:
                    norm.statistics(dve, link, x)
                if step == AFTER + 3:
                    norm.normalise(dve, 1, x)
                yield

        def tail_pool(pool):
            for step in range(TAIL_STEPS):
                m = step - FIRST_UNIT - 1
                if step == 2:
                    norm.reciprocal_root(pool, 0)
                if 0 <= m < NX:
                    pool.wait_ge(xrsum_ready, m + 1)
                    pool.tensor_tensor(px[m % 4], px[m % 4], xrsum[:, m % 4, :].rearrange("p (h o) -> p h o", o=1)
                                       .to_broadcast([P, HG, S2]), ALU.mult).then_inc(xprobs_ready, 1)
                if 3 <= m < 3 + NT:
                    t = m - 3
                    pool.wait_ge(t_full, NT)
                    pool.tensor_tensor(x[:, t, :], x[:, t, :], b_xo[:, :], ALU.add).then_inc(resid2, 1)
                if step == AFTER + 2:
                    norm.reciprocal_root(pool, 1)
                yield

        def tail_stores(sp, b):
            sp.wait_ge(norm.done, 2 * NT)
            sp.dma_start(scr["x5"].rearrange("(b t p) n -> b p t n", p=P, t=NT)[b], x[:, :, :]).then_inc(stored, 16)
            sp.wait_ge(t_out, 2 * NT)
            sp.dma_start(scr["x5T"][b].rearrange("(c p) n -> p c n", p=P), x5T).then_inc(stored, 16)
            sp.wait_ge(conv_out, 2)
            sp.dma_start(scr["xc"][b], xc).then_inc(stored, 16)
            sp.wait_ge(stored, 48)

        ORDER = "ttttsttttttstttttttttstststssttssttsttttsssstss"

        def in_order(tail, start):
            programs = {"t": tail, "s": start}
            for which in ORDER:
                if programs[which] is not None:
                    next(programs[which], None)
            for program in programs.values():
                if program is not None:
                    for _ in program:
                        pass

        def between_heads(end, start):
            with nc.Block() as block:
                @block.sync
                def _(sp):
                    if start is not None:
                        sp.dma_start(x_new[:, :, :], scr["acc"][0:T, :].rearrange("(b t p) n -> b p t n", p=P, t=NT)[start])\
                            .then_inc(loaded, 16)
                        for u in range(RING):
                            wait_drained(sp, PROJ.index(("k", u // 2)))
                            stack_pair(sp, u)
                    if end is not None:
                        tail_stores(sp, end)

                @block.tensor
                def _(pe):
                    in_order(None if end is None else tail_pe(pe), None if start is None else start_pe(pe))

                @block.scalar
                def _(act):
                    in_order(None if end is None else tail_act(act), None if start is None else start_act(act))

                @block.vector
                def _(dve):
                    in_order(None if end is None else tail_dve(dve), None if start is None else start_dve(dve))

                @block.gpsimd
                def _(pool):
                    in_order(None if end is None else tail_pool(pool), None if start is None else start_pool(pool))

        def clear():
            with nc.Block() as block:
                @block.vector
                def _(dve):
                    for s in sems:
                        dve.sem_clear(s)

        between_heads(None, 0)
        heads(0)
        clear()
        with nc.Fori(0, trips - 1) as b:
            between_heads(b, b + 1)
            heads(b + 1)
            clear()
        between_heads(trips - 1, None)
        clear()


def gated_layer_stage(nc, A, scr, out, cst, trips):
    ident = cst["ident"]
    with ExitStack() as ctx:
        def sb(name, shape, dt=FP32):
            return ctx.enter_context(nc.sbuf_tensor("gl_" + name, shape, dt))

        sems = []

        def sem(name):
            s = ctx.enter_context(nc.semaphore("gl_" + name))
            sems.append(s)
            return s

        psum = ctx.enter_context(nc.psum_tensor("gl_psum", [P, 8, 512], FP32))
        bank = [psum[:, i, :] for i in range(8)]

        w = sb("w", [P, NC, D])
        w_lin = sb("w_lin", [P, 2, D])
        b_lin = sb("b_lin", [P, 2, D])
        b_out = sb("b_out", [P, D])
        gamma = sb("gamma", [P, 2])
        beta = sb("beta", [P, 2])
        conv = sb("conv", [P, 2, B, S])
        bstats = sb("bstats", [P, 2, B, 6])
        bmv = sb("bmv", [P, 2, 2])
        bvare = sb("bvare", [P, 2])
        brstd = sb("brstd", [P, 2])
        bscale = sb("bscale", [P, 2])
        bshift = sb("bshift", [P, 2])
        act_b = sb("act_b", [P, 2, S])
        x = sb("x", [P, NT, D])
        xb = sb("xb", [P, NT, D])
        xT = sb("xT", [P, NC, S])
        expv = sb("expv", [P, 4, D])
        left = sb("left", [P, 4, D])
        top = sb("top", [P, 4, 8])
        nmax = sb("nmax", [P, 4])
        esum = sb("esum", [P, 4])
        rsum = sb("rsum", [P, 4])
        zo = sb("zo", [P, 2, D])
        xs = sb("xs", [P, 2, D])
        xsT = sb("xsT", [P, 2, NC, P])
        z = sb("z", [P, 2, D])
        stats = sb("stats", [P, 2, 6])
        mv = sb("mv", [P, 2, 2])
        vare = sb("vare", [P, 2])
        rstd = sb("rstd", [P, 2])

        setup_in, bn_step, bn_var, bn_rstd, bn_ready, gelu_done = (
            sem(n) for n in ("setup_in", "bn_step", "bn_var", "bn_rstd", "bn_ready", "gelu_done"))
        with nc.Block() as block:
            @block.sync
            def _(sp):
                for b in range(B):
                    sp.dma_start(conv[:, :, b, :], scr["xc"][b]).then_inc(setup_in, 16)
                sp.dma_start(w[:, :, :], A["w_ffn1"].rearrange("(c p) n -> p c n", p=P)).then_inc(setup_in, 16)
                sp.dma_start(w_lin[:, :, :], A["w_lin"]).then_inc(setup_in, 16)
                sp.dma_start(gamma[:, :], A["gamma"]).then_inc(setup_in, 16)
                sp.dma_start(beta[:, :], A["beta"]).then_inc(setup_in, 16)
                for br in range(2):
                    sp.dma_start(b_lin[:, br, :], A["b_lin"][br:br + 1, :].to_broadcast([P, D])).then_inc(setup_in, 16)
                sp.dma_start(b_out[:, :], A["b_ffn1"].rearrange("(a n) -> a n", a=1).to_broadcast([P, D]))\
                    .then_inc(setup_in, 16)
                sp.wait_ge(setup_in, 16 * (B + 7))

            @block.vector
            def _(dve):
                link = chain_of(dve, bn_step)
                dve.wait_ge(setup_in, 16 * (B + 7))
                for br in range(2):
                    for b in range(B):
                        dve.bn_stats(bstats[:, br, b, :], conv[:, br, b, :]).then_inc(bn_step, 1)
                link.skip(2 * B)
                for br in range(2):
                    dve.bn_aggr(bmv[:, br, :], bstats[:, br, :, :].rearrange("p b s -> p (b s)")).then_inc(bn_step, 1)
                link.skip(2)
                dve.tensor_scalar(bvare[:, :], bmv[:, :, 1], EPS, None, ALU.add).then_inc(bn_var, 1)
                dve.wait_ge(bn_rstd, 1)
                link(dve.tensor_tensor(bscale[:, :], brstd[:, :], gamma[:, :], ALU.mult))
                link(dve.tensor_tensor(bshift[:, :], bmv[:, :, 0], bscale[:, :], ALU.mult))
                dve.tensor_tensor(bshift[:, :], beta[:, :], bshift[:, :], ALU.subtract).then_inc(bn_ready, 1)

            @block.gpsimd
            def _(pool):
                pool.wait_ge(bn_var, 1)
                pool.tensor_tensor(brstd[:, :], bvare[:, :], cst["mhalf"][:, 0:2], ALU.pow).then_inc(bn_rstd, 1)

            @block.scalar
            def _(act):
                act.wait_ge(bn_ready, 1)
                for br in range(2):
                    part = conv[:, br, :, :].rearrange("p b s -> p (b s)")
                    act.activation(part, part, ACT.Gelu, scale=bscale[:, br:br + 1], bias=bshift[:, br:br + 1])\
                        .then_inc(gelu_done, 1)

        loaded, act_ready, xb_ready = sem("loaded"), sem("act_ready"), sem("xb_ready")
        lin_full, logit_done = sem("lin_full"), sem("logit_done")
        exp_done = sem("exp_done")
        chain = sem("chain")
        top_done, sel_done = sem("top_done"), sem("sel_done")
        full_full, zo_done = sem("full_full"), sem("zo_done")
        xs_done = sem("xs_done")
        xsT_full, xsT_out = sem("xsT_full"), sem("xsT_out")
        in_full, z_done = sem("in_full"), sem("z_done")
        zr_done = sem("zr_done")
        ln_step, ln_var, ln_rstd, ln_done = (sem(n) for n in ("ln_step", "ln_var", "ln_rstd", "ln_done"))
        stored = [sem(f"stored{i}") for i in range(2)]

        def batch(b):
            with nc.Block() as block:
                @block.sync
                def _(sp):
                    sp.dma_start(xT[:, :, :], scr["x5T"][b].rearrange("(c p) n -> p c n", p=P)).then_inc(loaded, 16)
                    sp.dma_start(x[:, :, :], scr["x5"].rearrange("(b t p) n -> b p t n", p=P, t=NT)[b]).then_inc(loaded, 16)
                    rows = out.rearrange("b (t p) n -> b t p n", p=P)
                    for t in range(NT):
                        sp.wait_ge(ln_done, t + 1)
                        sp.dma_start(rows[b, t], z[:, t % 2, :]).then_inc(stored[t % 2], 16)
                    for i in range(2):
                        sp.wait_ge(stored[i], 16 * NT // 2)

                @block.tensor
                def _(pe):
                    def lin(t):
                        for br in range(2):
                            if t >= 2:
                                pe.wait_ge(logit_done, 2 * (t - 2) + br + 1)
                            pe.matmul(bank[2 * (t % 2) + br], act_b[:, br, t * P:(t + 1) * P], w_lin[:, br, :],
                                      start=True, stop=True).then_inc(lin_full, 1)

                    def full(t):
                        if t >= 2:
                            pe.wait_ge(zo_done, t - 1)
                        for c in range(NC):
                            mm = pe.matmul(bank[4 + t % 2], xT[:, c, t * P:(t + 1) * P], w[:, c, :],
                                           start=(c == 0), stop=(c == NC - 1))
                        mm.then_inc(full_full, 1)

                    pe.wait_ge(act_ready, 1)
                    lin(0)
                    lin(1)
                    pe.wait_ge(loaded, 32)
                    full(0)
                    full(1)
                    for t in range(NT):
                        if t + 2 < NT:
                            lin(t + 2)
                        pe.wait_ge(xs_done, t + 1)
                        if t >= 1:
                            pe.wait_ge(xsT_out, t)
                        for c in range(NC):
                            mm = pe.transpose(bank[6][:, c * P:(c + 1) * P], xs[:, t % 2, c * P:(c + 1) * P], ident[:, :])
                        mm.then_inc(xsT_full, 1)
                        if t + 2 < NT:
                            full(t + 2)
                        pe.wait_ge(xsT_out, t + 1)
                        if t >= 1:
                            pe.wait_ge(z_done, t)
                        for c in range(NC):
                            mm = pe.matmul(bank[7], xsT[:, t % 2, c, :], w[:, c, :], start=(c == 0), stop=(c == NC - 1))
                        mm.then_inc(in_full, 1)

                @block.scalar
                def _(act):
                    act.activation(act_b[:, :, :], conv[:, :, bass.ds(b, 1), :].rearrange("p g o s -> p g (o s)"),
                                   ACT.Copy).then_inc(act_ready, 1)

                    def exps(t):
                        for br in range(2):
                            u = 2 * t + br
                            act.wait_ge(logit_done, u + 1)
                            act.activation(expv[:, u % 4, :], expv[:, u % 4, :], ACT.Exp, scale=-1.0,
                                           bias=nmax[:, u % 4:u % 4 + 1], accum_out=esum[:, u % 4:u % 4 + 1])\
                                .then_inc(exp_done, 1)

                    exps(0)
                    for t in range(NT):
                        if t + 1 < NT:
                            exps(t + 1)
                        act.wait_ge(xsT_full, t + 1)
                        if t >= 2:
                            act.wait_ge(in_full, t - 1)
                        act.activation(xsT[:, t % 2, :, :], bank[6].rearrange("p (c q) -> p c q", q=P), ACT.Copy)\
                            .then_inc(xsT_out, 1)

                @block.vector
                def _(dve):
                    link = chain_of(dve, chain)
                    ln = chain_of(dve, ln_step)

                    def logits(t):
                        for br in range(2):
                            u = 2 * t + br
                            dve.wait_ge(lin_full, u + 1)
                            if u >= 4:
                                dve.wait_ge(sel_done, t - 1)
                            dve.tensor_tensor_reduce(out=expv[:, u % 4, :], in0=bank[2 * (t % 2) + br], in1=b_lin[:, br, :],
                                                     scale=-1.0, scalar=-TAKEN, op0=ALU.add, op1=ALU.min,
                                                     accum_out=nmax[:, u % 4:u % 4 + 1]).then_inc(logit_done, 1)

                    def finish(t):
                        dve.wait_ge(in_full, t + 1)
                        dve.wait_ge(zr_done, t + 1)
                        if t >= 2:
                            dve.wait_ge(stored[t % 2], 16 * (t // 2))
                        dve.tensor_tensor(z[:, t % 2, :], bank[7], zo[:, t % 2, :], ALU.add).then_inc(z_done, 1)
                        dve.wait_ge(z_done, t + 1)
                        ln(dve.bn_stats(stats[:, t % 2, :], z[:, t % 2, :]))
                        ln(dve.bn_aggr(mv[:, t % 2, :], stats[:, t % 2, :]))
                        dve.tensor_scalar(vare[:, t % 2:t % 2 + 1], mv[:, t % 2, 1:2], EPS, None, ALU.add).then_inc(ln_var, 1)

                    def last(t):
                        dve.wait_ge(ln_rstd, t + 1)
                        dve.tensor_scalar(z[:, t % 2, :], z[:, t % 2, :], mv[:, t % 2, 0:1], rstd[:, t % 2:t % 2 + 1],
                                          ALU.subtract, ALU.mult).then_inc(ln_done, 1)

                    logits(0)
                    for t in range(NT):
                        if t + 1 < NT:
                            logits(t + 1)
                        us = [(2 * t + br) % 4 for br in range(2)]
                        dve.wait_ge(exp_done, 2 * t + 2)
                        for r in range(KGATE // 8):
                            for u in us:
                                dve.max(top[:, u, :], (left if r else expv)[:, u, :]).then_inc(chain, 1)
                            link.skip(2)
                            for i, u in enumerate(us):
                                ins = dve.match_replace(left[:, u, :], top[:, u, :], (left if r else expv)[:, u, :], 0.0)
                                if r < KGATE // 8 - 1:
                                    ins.then_inc(chain, 1)
                                else:
                                    ins.then_inc(top_done, 1)
                            if r < KGATE // 8 - 1:
                                link.skip(2)
                        if t >= 1:
                            finish(t - 1)
                        u0 = us[0]
                        link(dve.reciprocal(rsum[:, u0:u0 + 2], esum[:, u0:u0 + 2]))
                        dve.wait_ge(sel_done, t + 1)
                        dve.scalar_tensor_tensor(out=xs[:, t % 2, :], in0=left[:, us[1], :], scalar=rsum[:, us[1]:us[1] + 1],
                                                 in1=x[:, t, :], op0=ALU.mult, op1=ALU.mult).then_inc(xs_done, 1)
                        dve.wait_ge(full_full, t + 1)
                        if t >= 2:
                            dve.wait_ge(z_done, t - 1)
                        dve.scalar_tensor_tensor(out=zo[:, t % 2, :], in0=left[:, us[0], :], scalar=rsum[:, us[0]:us[0] + 1],
                                                 in1=bank[4 + t % 2], op0=ALU.mult, op1=ALU.mult).then_inc(zo_done, 1)
                        if t >= 1:
                            last(t - 1)
                    finish(NT - 1)
                    last(NT - 1)

                @block.gpsimd
                def _(pool):
                    pool.wait_ge(loaded, 32)
                    for t in range(NT):
                        pool.tensor_tensor(xb[:, t, :], x[:, t, :], b_out[:, :], ALU.add).then_inc(xb_ready, 1)
                    for t in range(NT):
                        pool.wait_ge(top_done, 2 * t + 2)
                        u0 = 2 * (t % 2)
                        pool.tensor_tensor(left[:, u0:u0 + 2, :], expv[:, u0:u0 + 2, :], left[:, u0:u0 + 2, :], ALU.subtract)\
                            .then_inc(sel_done, 1)
                        if t >= 1:
                            pool.wait_ge(ln_var, t)
                            pool.tensor_tensor(rstd[:, (t - 1) % 2:(t - 1) % 2 + 1], vare[:, (t - 1) % 2:(t - 1) % 2 + 1],
                                               cst["mhalf"][:, 0:1], ALU.pow).then_inc(ln_rstd, 1)
                        pool.wait_ge(zo_done, t + 1)
                        pool.wait_ge(xb_ready, NT)
                        pool.tensor_tensor(zo[:, t % 2, :], zo[:, t % 2, :], xb[:, t, :], ALU.add).then_inc(zr_done, 1)
                    pool.wait_ge(ln_var, NT)
                    pool.tensor_tensor(rstd[:, (NT - 1) % 2:(NT - 1) % 2 + 1], vare[:, (NT - 1) % 2:(NT - 1) % 2 + 1],
                                       cst["mhalf"][:, 0:1], ALU.pow).then_inc(ln_rstd, 1)

        with nc.Fori(0, trips) as b:
            batch(b)
            with nc.Block() as block:
                @block.vector
                def _(dve):
                    for s in sems:
                        dve.sem_clear(s)


def decoder_program(nc, A, out):
    scr = {}
    for name, shape in (("rows", [T + CAP, XW]), ("slots", [E * CAP + 1, 1]), ("acc", [T + CAP, D]),
                        ("x5", [T, D]), ("x5T", [B, D, S]), ("xc", [B, P, 2, S])):
        scr[name] = nc.dram_tensor("scratch_" + name, shape, FP32, kind="Internal").ap()
    with ExitStack() as ctx:
        cst = constants(nc, ctx)
        pruned_attention_stage(nc, A, scr, cst, B)
        experts_stage(nc, A, scr, cst)
        layer1_attention_stage(nc, A, scr, cst, B)
        gated_layer_stage(nc, A, scr, out, cst, B)


def kernel(**inputs):
    import numpy as _np
    import concourse.bacc as _bacc
    from concourse import mybir as _mybir
    from concourse.bass_utils import run_bass_kernel_spmd as _run

    a = {k: _np.asarray(v) for k, v in inputs.items()}

    def columns(*vectors):
        return _np.concatenate(vectors).reshape(-1, P).T

    def gates(name, axis, order=None):
        pair = [a["L1_ffn_so_" + name], a["L1_ffn_si_" + name]]
        return _np.stack([p.T if order else p for p in pair], axis)

    conv_w = gates("conv_w", 0).reshape(2, D // P, P).transpose(2, 0, 1)
    laid = {
        "x": a["x"], "xT": a["x"].transpose(0, 2, 1),
        "ctx": a["ctx_1024"], "ctxT": a["ctx_1024"].transpose(0, 2, 1),
        "mask": a["mask_Bx1xSxS2_if1"].reshape(B, S, S2),
        "w_qkv0": a["L0_attn_w_attn"].T, "b_qkv0": columns(a["L0_attn_b_attn"]),
        "w_proj0": a["L0_attn_w_proj"].T, "b_proj0": a["L0_attn_b_proj"],
        "w_router": a["L0_ffn_router_w"].T, "w_sgu": a["L0_ffn_ws_gate_up"], "w_sdown": a["L0_ffn_ws_down"],
        "w_gate": a["L0_ffn_w_gate"], "w_up": a["L0_ffn_w_up"], "w_down": a["L0_ffn_w_down"],
        "w_qkv1": _np.concatenate([a["L1_attn_W" + k].T for k in "qkv"], 1),
        "b_qkv1": columns(*(a["L1_attn_b" + k] for k in "qkv")),
        "w_o1": a["L1_attn_Wo"].T, "b_o1": a["L1_attn_bo"],
        "w_x": _np.stack([a["L1_xattn_W" + k].T for k in "qkv"]),
        "w_xo": a["L1_xattn_Wo"].T, "b_xo": a["L1_xattn_bo"],
        "conv_w": conv_w, "conv_b": gates("conv_b", 1),
        "gamma": gates("gamma", 1), "beta": gates("beta", 1),
        "w_lin": gates("lin_w", 1, order="T"), "b_lin": gates("lin_b", 0),
        "w_ffn1": a["L1_ffn_weight"], "b_ffn1": a["L1_ffn_bias"],
    }
    nc = _bacc.Bacc("TRN2", target_bir_lowering=False, num_devices=1)
    arrays, aps = {}, {}
    for name, value in laid.items():
        value = _np.ascontiguousarray(value)
        arrays[f"in_{name}"] = value
        aps[name] = nc.dram_tensor(f"in_{name}", value.shape, _mybir.dt.from_np(value.dtype), kind="ExternalInput").ap()
    out = nc.dram_tensor("out_0", (B, S, D), _mybir.dt.float32, kind="ExternalOutput").ap()
    decoder_program(nc, aps, out)
    r = _run(nc, [arrays], core_ids=[0])
    return r.results[0]["out_0"]
```

```python
import numpy as np
import concourse.bass as bass
from concourse import mybir
from contextlib import ExitStack

FP32 = mybir.dt.float32
F32R = mybir.dt.float32r
BF16 = mybir.dt.bfloat16
I32 = mybir.dt.int32
ALU = mybir.AluOpType
ACT = mybir.ActivationFunctionType
AX = mybir.AxisListType

P = 128
B, S, D = 8, 512, 512
T = B * S
NT = S // P
NC = D // P
H, DH = 16, 32
HG = P // DH
S2 = 77
E, TOPK, F = 64, 8, 384
NF = F // P
CAP = 256
NJ = CAP // P
XW = D + E
KEEP = int(S * 0.2) - 1
KGATE = 32
G = D // 4
EPS = 1e-5
QSCALE = 1.0 / float(np.sqrt(DH))
XSCALE = 1.0 / float(np.sqrt(D))
FAR = 1e30
TAKEN = -3e38
GELU_C, GELU_A = 0.7978845608028654, 0.044715


def chain_of(eng, sem):
    count = [0]

    def link(ins):
        count[0] += 1
        ins.then_inc(sem, 1)
        eng.wait_ge(sem, count[0])

    def skip(n):
        count[0] += n
        eng.wait_ge(sem, count[0])
    link.skip = skip
    return link


def pruned_attention_stage(nc, A, scr, cst, trips):
    ident, upper, ones, upper_b, ones_b = (cst[k] for k in ("ident", "upper", "ones", "upper_b", "ones_b"))
    with ExitStack() as ctx:
        def sb(name, shape, dt=FP32):
            return ctx.enter_context(nc.sbuf_tensor("l0_" + name, shape, dt))

        sems = []

        def sem(name):
            s = ctx.enter_context(nc.semaphore("l0_" + name))
            sems.append(s)
            return s

        bank = [ctx.enter_context(nc.psum_tensor(f"l0_bank{i}", [P, 512], FP32)) for i in range(8)]

        w_qkv = sb("w_qkv", [P, NC, 3 * D])
        w_proj = sb("w_proj", [P, NC, D])
        w_router = sb("w_router", [P, NC, E])
        w_sgu = sb("w_sgu", [P, NC, 2 * F])
        w_sdown = sb("w_sdown", [P, NF, D])
        b_qkv = sb("b_qkv", [P, 3 * NC])
        b_proj = sb("b_proj", [P, D])
        x = sb("x", [P, NT, D])
        xT = sb("xT", [P, NC, S])
        yT = sb("yT", [P, NC, S])
        qT = sb("qT", [P, NC, S])
        kpad = sb("kpad", [P, H, S])
        v = sb("v", [P, NT, D])
        bias = sb("bias", [P, NT, S])
        probs = sb("probs", [P, 4, 2, S])
        pT = sb("pT", [P, HG, NT, S])
        x2w = sb("x2w", [P, NT, XW])
        flat_probs = probs[:, :, :, :].rearrange("p a b s -> p (a b s)")
        gate = flat_probs[:, 0:NT * S].rearrange("p (t s) -> p t s", s=S)
        work = flat_probs[:, NT * S:NT * S + S + 8]
        top = sb("top", [P, 8])
        nmax = sb("nmax", [P, 4, 2])
        psums = sb("psums", [P, 4, 2])
        rsum = sb("rsum", [P, 4, 2])
        x1T, x2T = pT[:, 0, :, :], pT[:, 1, :, :]
        ctx_rows = sb("ctx_rows", [P, D])
        ctx_T = sb("ctx_T", [P, NC, S2])
        gl = pT[:, 2, 0, :]
        hid = pT[:, 3, 0:NF, :]
        gelu_out = sb("gelu_out", [P, S])
        stats = sb("stats", [P, NT, 6])
        mv = sb("mv", [P, NT, 2])
        vare = sb("vare", [P, NT])
        rstd = sb("rstd", [P, NT])
        expv = sb("expv", [P, NT, E])
        left = sb("left", [P, NT, E])
        mask = sb("mask", [P, NT, E])
        mask_b = sb("mask_b", [P, NT, E], BF16)
        run = sb("run", [P, NT + 1, E], BF16)
        nmx = sb("nmx", [P, NT])
        wsum = sb("wsum", [P, NT])
        m8 = sb("m8", [P, NT, 8])
        enc = sb("enc", [P, NT, E])
        slot1 = sb("slot1", [P, E])
        off = sb("off", [P, NT * 8])
        idx = sb("idx", [P, NT * 8], I32)
        tok = sb("tok", [P, NT])

        setup_in = sem("setup_in")
        late_in = sem("late_in")
        setup_pool = sem("setup_pool")
        setup_slots = sem("setup_slots")
        setup_dve = sem("setup_dve")

        with nc.Block() as block:
            @block.sync
            def _(sp):
                sp.dma_start(w_qkv[:, :, :], A["w_qkv0"].rearrange("(c p) n -> p c n", p=P)).then_inc(setup_in, 16)
                sp.dma_start(b_qkv[:, :], A["b_qkv0"]).then_inc(setup_in, 16)
                sp.dma_start(b_proj[:, :], A["b_proj0"].rearrange("(a n) -> a n", a=1).to_broadcast([P, D]))\
                    .then_inc(setup_in, 16)
                sp.wait_ge(setup_pool, 4)
                sp.dma_start(scr["slots"][1:E * CAP + 1, :].rearrange("(e n) o -> e (n o)", n=CAP),
                             work[0:E, 0:CAP]).then_inc(setup_slots, 16)
                sp.dma_start(scr["slots"][0:1, :], work[0:1, 0:1]).then_inc(setup_slots, 16)
                for j in range(NJ):
                    sp.dma_start(scr["rows"][T + j * P:T + (j + 1) * P, :], x2w[:, 0, :]).then_inc(setup_slots, 16)
                    sp.dma_start(scr["acc"][T + j * P:T + (j + 1) * P, :], x2w[:, 0, 0:D]).then_inc(setup_slots, 16)
                sp.wait_ge(setup_slots, (2 + 2 * NJ) * 16)

            @block.gpsimd
            def _(pool):
                pool.iota(tok[:, :], pattern=[[P, NT]], base=-S, channel_multiplier=1,
                          allow_small_or_imprecise_dtypes=True).then_inc(setup_pool, 1)
                pool.iota(slot1[:, :], pattern=[[CAP, E]], base=1, channel_multiplier=0,
                          allow_small_or_imprecise_dtypes=True).then_inc(setup_pool, 1)
                pool.iota(work[:, 0:CAP], pattern=[[1, CAP]], base=T, channel_multiplier=0,
                          allow_small_or_imprecise_dtypes=True).then_inc(setup_pool, 1)
                pool.memset(x2w[:, 0, :], 0.0).then_inc(setup_pool, 1)

            @block.vector
            def _(dve):
                dve.memset(kpad[:, :, :], 0.0)
                dve.memset(gelu_out[:, :], 0.0)
                dve.memset(ctx_rows[:, :], 0.0)
                dve.memset(run[:, 0, :], 0.0)
                dve.memset(idx[:, :], 4 * E * CAP)
                dve.wait_ge(setup_in, 3 * 16)
                dve.tensor_scalar(b_qkv[:, 0:NC], b_qkv[:, 0:NC], QSCALE, None, ALU.mult)

        loaded = sem("loaded")
        proj_full, proj_drained = sem("proj_full"), sem("proj_drained")
        gate_full, gate_relu = sem("gate_full"), sem("gate_relu")
        gate_masked = sem("gate_masked")
        forget_full, forget_out = sem("forget_full"), sem("forget_out")
        forget_causal = sem("forget_causal")
        dropped = sem("dropped")
        bias_ready = sem("bias_ready")
        chain_p1 = sem("chain_p1")

        def width(t):
            return (t + 1) * P

        PROJ = [("q", 0), ("k", 0), ("v", 0), ("v", 1), ("v", 2), ("v", 3), ("q", 1), ("k", 1),
                ("q", 2), ("k", 2), ("q", 3), ("k", 3)]
        ROUNDS = -(-KEEP // 8)
        EXTRA = ROUNDS * 8 - KEEP
        SELECT = [(t, r, min(n, ROUNDS - r)) for t, n in enumerate((7, 5, 4, 3)) for r in range(0, ROUNDS, n)]
        GATE_STEPS = 4 + len(SELECT)
        FIRST_SELECT = 4

        LATE_PROJ = 4
        GATE_PROJ = {0: range(0, 2), 2: range(2, LATE_PROJ)}

        def project(pe, j):
            kind, i = PROJ[j]
            if j >= 2:
                pe.wait_ge(proj_drained, j - 1)
            out = bank[j % 2]
            for c in range(NC):
                if kind == "v":
                    mm = pe.matmul(out[:, :], xT[:, c, i * P:(i + 1) * P], w_qkv[:, c, 2 * D:3 * D],
                                   start=(c == 0), stop=(c == NC - 1))
                else:
                    at = i * P + (D if kind == "k" else 0)
                    mm = pe.matmul(out[:, :], w_qkv[:, c, at:at + P], xT[:, c, :],
                                   start=(c == 0), stop=(c == NC - 1))
            mm.then_inc(proj_full, 1)

        def drain_projection(act, j):
            kind, i = PROJ[j]
            act.wait_ge(proj_full, j + 1)
            src = bank[j % 2]
            if kind == "q":
                last = act.activation(qT[:, i, :], src[:, :], ACT.Identity, scale=QSCALE, bias=b_qkv[:, i:i + 1])
            elif kind == "k":
                for h in range(HG):
                    r = slice(h * DH, (h + 1) * DH)
                    last = act.activation(kpad[r, i * HG + h, :], src[r, :], ACT.Identity,
                                          bias=b_qkv[r, NC + i:NC + i + 1])
            else:
                last = act.activation(v[:, i, :], src[:, :], ACT.Copy)
            last.then_inc(proj_drained, 1)

        def late_projections(step, eng):
            for j in range(LATE_PROJ, len(PROJ)):
                step(eng, j)
                yield

        def gate_pe(pe):
            pe.wait_ge(loaded, 16)
            for step in range(GATE_STEPS):
                if step == FIRST_SELECT:
                    pe.wait_ge(forget_out, NT)
                for j in GATE_PROJ.get(step, ()):
                    project(pe, j)
                if step == 1:
                    pe.wait_ge(proj_drained, 2)
                    for t in range(NT):
                        if t >= 2:
                            pe.wait_ge(gate_relu, t - 1)
                        pe.matmul(bank[2 + t % 2][:, 0:width(t)], qT[:, 0, t * P:(t + 1) * P],
                                  kpad[:, 0, 0:width(t)], start=True, stop=True).then_inc(gate_full, 1)
                if step == 3:
                    pe.wait_ge(gate_masked, 2 * NT)
                    for t in range(NT):
                        if t >= 2:
                            pe.wait_ge(forget_out, t - 1)
                        out = bank[2 + t % 2]
                        mm = pe.matmul(out[:, 0:width(t)], upper[:, :], gate[:, t, 0:width(t)], start=True, stop=True)
                        for u in range(t):
                            mm = pe.matmul(out[:, 0:width(u)], ones[:, :], gate[:, u, 0:width(u)],
                                           start=False, stop=True, skip_group_check=True)
                        mm.then_inc(forget_full, 1)
                yield

        def gate_act(act):
            for step in range(GATE_STEPS):
                for j in GATE_PROJ.get(step, ()):
                    drain_projection(act, j)
                if step == 3:
                    for t in range(NT):
                        act.wait_ge(forget_full, t + 1)
                        act.activation(bias[:, t, 0:width(t)], bank[2 + t % 2][:, 0:width(t)], ACT.Copy,
                                       scale=-1.0).then_inc(forget_out, 1)
                yield

        def gate_pool(pool):
            for step in range(GATE_STEPS):
                if step == 1:
                    for t in range(NT):
                        pool.wait_ge(gate_relu, t + 1)
                        own = gate[:, t, t * P:(t + 1) * P]
                        pool.affine_select(out=own, in_=own, pattern=[[-1, P]], compare_op=ALU.is_gt, fill=0.0,
                                           base=0, channel_multiplier=1).then_inc(gate_masked, 1)
                        pool.wait_ge(gate_masked, 2 * t + 1)
                        pool.memset(gate[:, t, 0:1], 0.0).then_inc(gate_masked, 1)
                if step == 3:
                    for t in range(NT):
                        pool.wait_ge(forget_out, t + 1)
                        own = bias[:, t, t * P:(t + 1) * P]
                        pool.affine_select(out=own, in_=own, pattern=[[-1, P]], compare_op=ALU.is_ge, fill=-FAR,
                                           base=0, channel_multiplier=1).then_inc(forget_causal, 1)
                k = step - FIRST_SELECT - 1
                if 0 <= k and SELECT[k][1] + SELECT[k][2] == ROUNDS:
                    keep_own(pool, SELECT[k][0])
                yield
            keep_own(pool, NT - 1)

        def keep_own(pool, t):
            pool.wait_ge(dropped, t + 1)
            own = bias[:, t, t * P:(t + 1) * P]
            pool.affine_select(out=own, in_=own, pattern=[[-1, P]], compare_op=ALU.not_equal, fill=0.0,
                               base=0, channel_multiplier=1).then_inc(bias_ready, 1)

        def gate_dve(dve):
            link = chain_of(dve, chain_p1)
            for step in range(GATE_STEPS):
                if step == 1:
                    for t in range(NT):
                        dve.wait_ge(gate_full, t + 1)
                        dve.tensor_scalar(gate[:, t, 0:width(t)], bank[2 + t % 2][:, 0:width(t)], 0.0, None,
                                          ALU.max).then_inc(gate_relu, 1)
                if step >= FIRST_SELECT:
                    t, first, rounds = SELECT[step - FIRST_SELECT]
                    w = width(t)
                    if first == 0:
                        link(dve.memset(work[:, 0:EXTRA], -TAKEN))
                        dve.wait_ge(forget_causal, t + 1)
                        link(dve.tensor_copy(work[:, EXTRA:EXTRA + w], bias[:, t, 0:w]))
                    for _ in range(rounds):
                        link(dve.max(top[:, :], work[:, 0:EXTRA + w]))
                        link(dve.match_replace(work[:, 0:EXTRA + w], top[:, :], work[:, 0:EXTRA + w], TAKEN))
                    if first + rounds == ROUNDS:
                        link(dve.tensor_scalar(work[:, EXTRA:EXTRA + w], work[:, EXTRA:EXTRA + w], TAKEN / 2, -FAR,
                                               ALU.is_gt, ALU.mult))
                        dve.tensor_tensor(bias[:, t, 0:w], bias[:, t, 0:w], work[:, EXTRA:EXTRA + w],
                                          ALU.min).then_inc(dropped, 1)
                        dve.wait_ge(dropped, t + 1)
                yield

        scores_full, scores_out = sem("scores_full"), sem("scores_out")
        exp_done = sem("exp_done")
        rsum_ready = sem("rsum_ready")
        probs_ready = sem("probs_ready")
        pT_full = sem("pT_full")
        pT_out_dve, pT_out_act = sem("pT_out_dve"), sem("pT_out_act")
        attn_full, attn_out = sem("attn_full"), sem("attn_out")
        LAG = 3

        UNITS = [(g, t, p) for g in range(NC) for t in range(NT) for p in range(2)]
        PER_G = 2 * NT

        tail_in, resid = sem("tail_in"), sem("resid")

        scattered = nc.alloc_semaphore("l0_scattered")

        ALL_SCATTERED = 16 * NT * TOPK

        def scatter(pool, k):
            pool.indirect_dma_start(
                out=scr["slots"][:, :], out_offset=bass.IndirectOffsetOnAxis(ap=idx[:, k:k + 1], axis=0),
                in_=tok[:, k // TOPK:k // TOPK + 1], in_offset=None,
                bounds_check=E * CAP, oob_is_err=False).then_inc(scattered, 16)

        def heads(b, first=False):
            N = len(UNITS)
            with nc.Block() as block:
                @block.sync
                def _(sp):
                    sp.dma_start(x[:, :, :], A["x"][b].rearrange("(t p) n -> p t n", p=P)).then_inc(tail_in, 16)
                    sp.dma_start(ctx_rows[0:S2, :], A["ctx"][b]).then_inc(tail_in, 16)
                    sp.dma_start(ctx_T[:, :, :], A["ctxT"][b].rearrange("(c p) n -> p c n", p=P)).then_inc(tail_in, 16)
                    if first:
                        sp.wait_ge(late_in, len(LATE) * 16)
                    sp.wait_ge(tail_in, 48)

                @block.tensor
                def _(pe):
                    for n in range(N + LAG + NT):
                        if n < N:
                            g, t, p = UNITS[n]
                            if n >= 2:
                                pe.wait_ge(scores_out, 2 * (n - 1))
                            for hh in range(2):
                                mm = pe.matmul(bank[2 * (n % 2) + hh][:, 0:width(t)], qT[:, g, t * P:(t + 1) * P],
                                               kpad[:, HG * g + 2 * p + hh, 0:width(t)], start=True, stop=True)
                            mm.then_inc(scores_full, 1)
                        m = n - LAG
                        if m >= PER_G and m % PER_G < NT:
                            g, kc = m // PER_G - 1, m % PER_G
                            if kc == 0:
                                pe.wait_ge(pT_out_dve, m)
                                pe.wait_ge(pT_out_act, m)
                                if g >= 1:
                                    pe.wait_ge(attn_out, g)
                            for h in range(HG):
                                mm = pe.matmul(bank[6][h * DH:(h + 1) * DH, kc * P:S],
                                               v[:, kc, (HG * g + h) * DH:(HG * g + h + 1) * DH],
                                               pT[:, h, kc, kc * P:S], start=(kc == 0), stop=True,
                                               skip_group_check=True)
                            mm.then_inc(attn_full, 1)
                        if 0 <= m < N:
                            g, t, p = UNITS[m]
                            pe.wait_ge(probs_ready, m + 1)
                            for hh in range(2):
                                if m >= 1:
                                    pe.wait_ge(pT_out_act if hh else pT_out_dve, m)
                                for kc in range(t + 1):
                                    mm = pe.transpose(bank[4 + hh][:, kc * P:(kc + 1) * P],
                                                      probs[:, m % 4, hh, kc * P:(kc + 1) * P], ident[:, :])
                                mm.then_inc(pT_full, 1)

                @block.vector
                def _(dve):
                    for n in range(N + LAG):
                        if n < N:
                            g, t, p = UNITS[n]
                            dve.wait_ge(scores_full, n + 1)
                            if n >= 4:
                                dve.wait_ge(pT_full, 2 * (n - 3))
                            for hh in range(2):
                                dve.tensor_tensor_reduce(
                                    out=probs[:, n % 4, hh, 0:width(t)], in0=bank[2 * (n % 2) + hh][:, 0:width(t)],
                                    in1=bias[:, t, 0:width(t)], scale=-1.0, scalar=-TAKEN, op0=ALU.add, op1=ALU.min,
                                    accum_out=nmax[:, n % 4, hh:hh + 1]).then_inc(scores_out, 1)
                        m = n - 1
                        if 0 <= m < N:
                            dve.wait_ge(exp_done, 2 * m + 2)
                            dve.reciprocal(rsum[:, m % 4, :], psums[:, m % 4, :]).then_inc(rsum_ready, 1)
                        m = n - LAG
                        if 0 <= m < N:
                            g, t, p = UNITS[m]
                            dve.wait_ge(pT_full, 2 * m + 1)
                            if g >= 1:
                                dve.wait_ge(attn_full, (g - 1) * NT + t + 1)
                            dve.tensor_copy(pT[:, 2 * p, 0:t + 1, t * P:(t + 1) * P],
                                            bank[4][:, 0:width(t)].rearrange("p (k q) -> p k q", q=P))\
                                .then_inc(pT_out_dve, 1)

                @block.scalar
                def _(act):
                    for n in range(N + LAG + NT + 1):
                        if n < N:
                            g, t, p = UNITS[n]
                            for hh in range(2):
                                act.wait_ge(scores_out, 2 * n + hh + 1)
                                pr = probs[:, n % 4, hh, 0:width(t)]
                                act.activation(pr, pr, ACT.Exp, scale=-1.0, bias=nmax[:, n % 4, hh:hh + 1],
                                               accum_out=psums[:, n % 4, hh:hh + 1]).then_inc(exp_done, 1)
                        m = n - LAG
                        if 0 <= m < N:
                            g, t, p = UNITS[m]
                            act.wait_ge(pT_full, 2 * m + 2)
                            if g >= 1:
                                act.wait_ge(attn_full, (g - 1) * NT + t + 1)
                            act.activation(pT[:, 2 * p + 1, 0:t + 1, t * P:(t + 1) * P],
                                           bank[5][:, 0:width(t)].rearrange("p (k q) -> p k q", q=P), ACT.Copy)\
                                .then_inc(pT_out_act, 1)
                        if m >= PER_G and m % PER_G == NT:
                            g = m // PER_G - 1
                            act.wait_ge(attn_full, (g + 1) * NT)
                            act.activation(yT[:, g, :], bank[6][:, :], ACT.Identity,
                                           bias=b_qkv[:, 2 * NC + g:2 * NC + g + 1]).then_inc(attn_out, 1)

                @block.gpsimd
                def _(pool):
                    for n in range(N):
                        g, t, p = UNITS[n]
                        pool.wait_ge(rsum_ready, n + 1)
                        pr = probs[:, n % 4, :, 0:width(t)]
                        pool.tensor_tensor(pr, pr, rsum[:, n % 4, :].rearrange("p (h a) -> p h a", a=1)
                                           .to_broadcast([P, 2, width(t)]), ALU.mult).then_inc(probs_ready, 1)
                    pool.wait_ge(tail_in, 48)
                    for t in range(NT):
                        pool.tensor_tensor(x[:, t, :], x[:, t, :], b_proj[:, :], ALU.add).then_inc(resid, 1)
                    pool.wait_ge(resid, NT)

        o_full, res1 = sem("o_full"), sem("res1")
        ln_var, ln_rstd = sem("ln_var"), sem("ln_rstd")
        ln_done = sem("ln_done")
        t_full, t_out = sem("t_full"), sem("t_out")
        cx_full = sem("cx_full")
        sq_done, poly_done, tanh_done, gelu_done = sem("sq_done"), sem("poly_done"), sem("tanh_done"), sem("gelu_done")
        cy_full, res2 = sem("cy_full"), sem("res2")
        route_full = sem("route_full")
        shift_done, expv_done = sem("shift_done"), sem("expv_done")
        mask_done = sem("mask_done")
        pos_full = sem("pos_full")
        w_done, idx_done = sem("w_done"), sem("idx_done")
        sg_full, stanh_done = sem("sg_full"), sem("stanh_done")
        hid_mid, hid_done = sem("hid_mid"), sem("hid_done")
        sd_full, acc_done = sem("sd_full"), sem("acc_done")
        stored = sem("stored")
        chain_p3 = sem("chain_p3")

        TAIL_STEPS = 21

        def shared_banks(f):
            return (bank[6], bank[7]) if f % 2 == 0 else (bank[2], bank[3])

        DOWN_BANKS = (2, 3, 6, 7)
        SHARED_PE, SHARED_ACT, SHARED_DVE = (14, 15, 18), (15, 16, 18), (17, 18, 19)

        def tail_pe(pe):
            for step in range(TAIL_STEPS):
                if step == 0:
                    for t in range(NT):
                        for c in range(NC):
                            mm = pe.matmul(bank[4 + t][:, :], yT[:, c, t * P:(t + 1) * P], w_proj[:, c, :],
                                           start=(c == 0), stop=(c == NC - 1))
                        mm.then_inc(o_full, 1)
                if step in (4, 13):
                    k = 0 if step == 4 else 1
                    src = x if k == 0 else x2w
                    for t in range(NT):
                        pe.wait_ge(ln_done, k * NT + t + 1)
                        for c in range(NC):
                            mm = pe.transpose(bank[4 + t][:, c * P:(c + 1) * P], src[:, t, c * P:(c + 1) * P], ident[:, :])
                        mm.then_inc(t_full, 1)
                if step == 5:
                    pe.wait_ge(t_out, NT)
                    for c in range(NC):
                        mm = pe.matmul(bank[4][0:S2, :], ctx_T[:, c, :], x1T[:, c, :], start=(c == 0), stop=(c == NC - 1))
                    mm.then_inc(cx_full, 1)
                if step == 9:
                    pe.wait_ge(gelu_done, 1)
                    for t in range(NT):
                        pe.matmul(bank[4 + t][:, :], gelu_out[:, t * P:(t + 1) * P], ctx_rows[:, :],
                                  start=True, stop=True).then_inc(cy_full, 1)
                if step == 14:
                    pe.wait_ge(t_out, 2 * NT)
                    for t in range(NT):
                        for c in range(NC):
                            mm = pe.matmul(bank[4][:, t * E:(t + 1) * E], x2T[:, c, t * P:(t + 1) * P],
                                           w_router[:, c, :], start=(c == 0), stop=(c == NC - 1))
                    mm.then_inc(route_full, 1)
                if step == 18:
                    pe.wait_ge(mask_done, NT)
                    for t in range(NT):
                        pe.matmul(bank[5][:, t * E:(t + 1) * E], upper_b[:, :], mask_b[:, t, :], start=True, stop=False)
                        mm = pe.matmul(bank[5][:, t * E:(t + 1) * E], ones_b[:, :], run[:, t, :], start=False, stop=True)
                    mm.then_inc(pos_full, 1)
                if step in SHARED_PE:
                    f = SHARED_PE.index(step)
                    if f >= 2:
                        pe.wait_ge(hid_done, f - 1)
                    for half in range(2):
                        at = half * F + f * P
                        for c in range(NC):
                            mm = pe.matmul(shared_banks(f)[half][:, :], w_sgu[:, c, at:at + P], x2T[:, c, :],
                                           start=(c == 0), stop=(c == NC - 1))
                        mm.then_inc(sg_full, 1)
                if step == 20:
                    pe.wait_ge(hid_done, NF)
                    for t in range(NT):
                        for f in range(NF):
                            mm = pe.matmul(bank[DOWN_BANKS[t]][:, :], hid[:, f, t * P:(t + 1) * P], w_sdown[:, f, :],
                                           start=(f == 0), stop=(f == NF - 1))
                        mm.then_inc(sd_full, 1)
                yield

        def tail_act(act):
            for step in range(TAIL_STEPS):
                if step in (4, 13):
                    k = 0 if step == 4 else 1
                    for t in range(NT):
                        act.wait_ge(t_full, k * NT + t + 1)
                        act.activation((x2T if k else x1T)[:, :, t * P:(t + 1) * P],
                                       bank[4 + t][:, :].rearrange("p (c q) -> p c q", q=P), ACT.Copy).then_inc(t_out, 1)
                if step == 6:
                    act.wait_ge(cx_full, 1)
                    act.activation(gl[0:S2, :], bank[4][0:S2, :], ACT.Square).then_inc(sq_done, 1)
                if step == 7:
                    act.wait_ge(poly_done, 1)
                    act.activation(gl[0:S2, :], gl[0:S2, :], ACT.Tanh, scale=GELU_C).then_inc(tanh_done, 1)
                if step == 15:
                    act.wait_ge(shift_done, 1)
                    act.activation(expv[:, :, :], expv[:, :, :], ACT.Exp).then_inc(expv_done, 1)
                if step in SHARED_ACT:
                    f = SHARED_ACT.index(step)
                    act.wait_ge(sg_full, 2 * f + 1)
                    act.activation(hid[:, f, :], shared_banks(f)[0][:, :], ACT.Tanh, scale=0.5).then_inc(stanh_done, 1)
                yield

        def tail_dve(dve, end):
            link = chain_of(dve, chain_p3)

            def rows(step):
                return (lambda t: x[:, t, :]) if step < 10 else (lambda t: x2w[:, t, 0:D])

            def over(a, n=E):
                return a.rearrange("p (t o) -> p t o", o=1).to_broadcast([P, NT, n])

            logits = bank[4][:, 0:NT * E].rearrange("p (t e) -> p t e", e=E)
            pos = bank[5][:, 0:NT * E].rearrange("p (t e) -> p t e", e=E)
            for step in range(TAIL_STEPS):
                if step == 1:
                    for t in range(NT):
                        dve.wait_ge(o_full, t + 1)
                        dve.tensor_tensor(x[:, t, :], bank[4 + t][:, :], x[:, t, :], ALU.add).then_inc(res1, 1)
                    dve.wait_ge(res1, NT)
                if step in (2, 11):
                    for t in range(NT):
                        dve.bn_stats(stats[:, t, :], rows(step)(t)).then_inc(chain_p3, 1)
                    link.skip(NT)
                    for t in range(NT):
                        dve.bn_aggr(mv[:, t, :], stats[:, t, :]).then_inc(chain_p3, 1)
                    link.skip(NT)
                    dve.tensor_scalar(vare[:, :], mv[:, :, 1], EPS, None, ALU.add).then_inc(ln_var, 1)
                if step in (3, 12):
                    k = 0 if step == 3 else 1
                    dve.wait_ge(ln_rstd, k + 1)
                    for t in range(NT):
                        dve.tensor_scalar(rows(step)(t), rows(step)(t), mv[:, t, 0:1], rstd[:, t:t + 1],
                                          ALU.subtract, ALU.mult).then_inc(ln_done, 1)
                    dve.wait_ge(ln_done, NT * (k + 1))
                if step == 7:
                    dve.wait_ge(sq_done, 1)
                    link(dve.tensor_scalar(gl[0:S2, :], gl[0:S2, :], GELU_A, 1.0, ALU.mult, ALU.add))
                    dve.tensor_tensor(gl[0:S2, :], gl[0:S2, :], bank[4][0:S2, :], ALU.mult).then_inc(poly_done, 1)
                if step == 8:
                    dve.wait_ge(tanh_done, 1)
                    dve.scalar_tensor_tensor(out=gelu_out[0:S2, :], in0=gl[0:S2, :], scalar=1.0, in1=bank[4][0:S2, :],
                                             op0=ALU.add, op1=ALU.mult).then_inc(gelu_done, 1)
                if step == 10:
                    for t in range(NT):
                        dve.wait_ge(cy_full, t + 1)
                        dve.scalar_tensor_tensor(out=x2w[:, t, 0:D], in0=bank[4 + t][:, :], scalar=0.5, in1=x[:, t, :],
                                                 op0=ALU.mult, op1=ALU.add).then_inc(res2, 1)
                    dve.wait_ge(res2, NT)
                if step == 15:
                    dve.wait_ge(route_full, 1)
                    link(dve.tensor_reduce(nmx[:, :], logits, AX.X, ALU.max))
                    dve.tensor_tensor(expv[:, :, :], logits, over(nmx[:, :]), ALU.subtract).then_inc(shift_done, 1)
                if step == 16:
                    dve.wait_ge(expv_done, 1)
                    for t in range(NT):
                        dve.max(m8[:, t, :], expv[:, t, :]).then_inc(chain_p3, 1)
                    link.skip(NT)
                    for t in range(NT):
                        dve.match_replace(left[:, t, :], m8[:, t, :], expv[:, t, :], -1.0).then_inc(chain_p3, 1)
                    link.skip(NT)
                    link(dve.tensor_scalar(mask[:, :, :], left[:, :, :], -1.0, None, ALU.is_equal))
                    link(dve.tensor_copy(mask_b[:, :, :], mask[:, :, :]))
                    for t in range(NT):
                        dve.tensor_tensor(run[:, t + 1, :], run[:, t, :], mask_b[:, t, :], ALU.add).then_inc(mask_done, 1)
                        dve.wait_ge(mask_done, t + 1)
                if step == 17:
                    link(dve.tensor_tensor(expv[:, :, :], expv[:, :, :], mask[:, :, :], ALU.mult))
                    link(dve.tensor_reduce(wsum[:, :], expv[:, :, :], AX.X, ALU.add))
                    link(dve.reciprocal(wsum[:, :], wsum[:, :]))
                    dve.tensor_tensor(x2w[:, :, D:XW], expv[:, :, :], over(wsum[:, :]), ALU.mult).then_inc(w_done, 1)
                if step == 19:
                    dve.wait_ge(scattered, end * ALL_SCATTERED + ALL_SCATTERED)
                    link(dve.tensor_scalar(tok[:, :], tok[:, :], float(S), None, ALU.add))
                    dve.wait_ge(pos_full, 1)
                    link(dve.scalar_tensor_tensor(out=left[:, :, :], in0=pos, scalar=float(CAP), in1=mask[:, :, :],
                                                  op0=ALU.is_lt, op1=ALU.mult))
                    link(dve.tensor_tensor(enc[:, :, :], pos, slot1[:, :].rearrange("p (o e) -> p o e", o=1)
                                           .to_broadcast([P, NT, E]), ALU.add))
                    link(dve.tensor_tensor(enc[:, :, :], enc[:, :, :], left[:, :, :], ALU.mult))
                    for t in range(NT):
                        dve.max(m8[:, t, :], enc[:, t, :]).then_inc(chain_p3, 1)
                    link.skip(NT)
                    flat = m8[:, :, :].rearrange("p t k -> p (t k)")
                    link(dve.tensor_scalar(off[:, :], flat, 0.5, float(4 * E * CAP), ALU.is_lt, ALU.mult))
                    dve.tensor_tensor(idx[:, :], off[:, :], flat, ALU.add).then_inc(idx_done, 1)
                    link(dve.tensor_copy(run[:, 0, :], run[:, NT, :]))
                if step in SHARED_DVE:
                    f = SHARED_DVE.index(step)
                    gate_bank, up_bank = shared_banks(f)
                    dve.wait_ge(stanh_done, f + 1)
                    dve.scalar_tensor_tensor(out=hid[:, f, :], in0=hid[:, f, :], scalar=1.0, in1=gate_bank[:, :],
                                             op0=ALU.add, op1=ALU.mult).then_inc(hid_mid, 1)
                    dve.wait_ge(sg_full, 2 * f + 2)
                    dve.wait_ge(hid_mid, f + 1)
                    dve.tensor_tensor(hid[:, f, :], hid[:, f, :], up_bank[:, :], ALU.mult).then_inc(hid_done, 1)
                if step == 20:
                    for t in range(NT):
                        dve.wait_ge(sd_full, t + 1)
                        dve.scalar_tensor_tensor(out=x[:, t, :], in0=bank[DOWN_BANKS[t]][:, :], scalar=0.5,
                                                 in1=x2w[:, t, 0:D], op0=ALU.mult, op1=ALU.add).then_inc(acc_done, 1)
                yield

        def tail_pool(pool, last):
            for step in range(TAIL_STEPS):
                if step in (2, 11):
                    pool.wait_ge(ln_var, 1 if step == 2 else 2)
                    pool.tensor_tensor(rstd[:, :], vare[:, :], cst["mhalf"][:, 0:NT], ALU.pow).then_inc(ln_rstd, 1)
                if 4 <= step < 12:
                    for k in range((step - 4) * NT, (step - 3) * NT):
                        scatter(pool, k)
                yield
            if last:
                pool.wait_ge(idx_done, 1)
                for k in range(NT * TOPK):
                    scatter(pool, k)
                pool.wait_ge(scattered, (trips + 1) * ALL_SCATTERED)

        def tail_stores(sp, b):
            sp.wait_ge(w_done, 1)
            sp.dma_start(scr["rows"][0:T, :].rearrange("(b t p) n -> b p t n", p=P, t=NT)[b], x2w[:, :, :])\
                .then_inc(stored, 16)
            sp.wait_ge(acc_done, NT)
            sp.dma_start(scr["acc"][0:T, :].rearrange("(b t p) n -> b p t n", p=P, t=NT)[b], x[:, :, :])\
                .then_inc(stored, 16)
            sp.wait_ge(stored, 32)

        ORDER = "tggggttppgttptggtttgptptptgtptgtgttttgtgggttgtgt"

        def in_order(tail, gate, proj=None):
            programs = {"t": tail, "g": gate, "p": proj}
            for which in ORDER:
                if programs[which] is not None:
                    next(programs[which], None)
            for program in programs.values():
                if program is not None:
                    for _ in program:
                        pass

        LATE = ((w_proj, "w_proj0"), (w_router, "w_router"), (w_sgu, "w_sgu"), (w_sdown, "w_sdown"))

        def between_heads(end, start):
            with nc.Block() as block:
                @block.sync
                def _(sp):
                    if start is not None:
                        sp.dma_start(xT[:, :, :], A["xT"][start].rearrange("(c p) n -> p c n", p=P)).then_inc(loaded, 16)
                        sp.wait_ge(loaded, 16)
                    if end is None:
                        for dst, name in LATE:
                            sp.dma_start(dst[:, :, :], A[name].rearrange("(c p) n -> p c n", p=P)).then_inc(late_in, 16)
                    if end is not None:
                        tail_stores(sp, end)

                @block.tensor
                def _(pe):
                    in_order(None if end is None else tail_pe(pe), None if start is None else gate_pe(pe),
                             None if start is None else late_projections(project, pe))

                @block.scalar
                def _(act):
                    in_order(None if end is None else tail_act(act), None if start is None else gate_act(act),
                             None if start is None else late_projections(drain_projection, act))

                @block.vector
                def _(dve):
                    in_order(None if end is None else tail_dve(dve, end), None if start is None else gate_dve(dve))

                @block.gpsimd
                def _(pool):
                    in_order(None if end is None else tail_pool(pool, start is None), None if start is None else gate_pool(pool))

        def clear():
            with nc.Block() as block:
                @block.vector
                def _(dve):
                    for s in sems:
                        dve.sem_clear(s)

        between_heads(None, 0)
        heads(0, first=True)
        clear()
        with nc.Fori(0, trips - 1) as b:
            between_heads(b, b + 1)
            heads(b + 1)
            clear()
        between_heads(trips - 1, None)
        clear()


def constants(nc, ctx):
    def sb(name, shape, dt=FP32):
        return ctx.enter_context(nc.sbuf_tensor("cst_" + name, shape, dt))
    cst = {"ident": sb("ident", [P, P]), "upper": sb("upper", [P, P]), "ones": sb("ones", [P, P]),
           "upper_b": sb("upper_b", [P, P], BF16), "ones_b": sb("ones_b", [P, P], BF16), "mhalf": sb("mhalf", [P, NT]),
           "groups": sb("groups", [P, DH])}
    made = ctx.enter_context(nc.semaphore("constants_made"))
    with nc.Block() as block:
        @block.gpsimd
        def _(pool):
            pool.memset(cst["ones"][:, :], 1.0).then_inc(made, 1)
            pool.memset(cst["ones_b"][:, :], 1.0).then_inc(made, 1)
            pool.memset(cst["mhalf"][:, :], -0.5).then_inc(made, 1)
            pool.wait_ge(made, 3)
            for name, src, op in (("ident", "ones", ALU.is_equal), ("upper", "ones", ALU.is_gt),
                                  ("upper_b", "ones_b", ALU.is_gt)):
                pool.affine_select(out=cst[name][:, :], in_=cst[src][:, :], pattern=[[1, P]], compare_op=op,
                                   fill=0.0, base=0, channel_multiplier=-1).then_inc(made, 1)
            pool.wait_ge(made, 6)
    return cst


def experts_stage(nc, A, scr, cst):
    ident = cst["ident"]
    with ExitStack() as ctx:
        def sb(name, shape, dt=FP32):
            return ctx.enter_context(nc.sbuf_tensor("moe_" + name, shape, dt))

        sems = []

        def sem(name):
            s = ctx.enter_context(nc.semaphore("moe_" + name))
            sems.append(s)
            return s

        bank = [ctx.enter_context(nc.psum_tensor(f"moe_bank{i}", [P, 512], FP32)) for i in range(8)]
        NI = E // 2
        lists = sb("lists", [P, P])
        listsT = sb("listsT", [P, E * NJ])
        w_gu = [sb(f"w_gu{s}", [P, NC, 2 * F]) for s in range(2)]
        w_dn = [sb(f"w_dn{s}", [P, NF, D]) for s in range(2)]
        gu_parts = [[sb(f"gu_part{s}{part}", [P, NC, 2 * F]) for part in range(2)] for s in range(2)]
        dn_parts = [[sb(f"dn_part{s}{part}", [P, NF, D]) for part in range(2)] for s in range(2)]
        rowsT_parts = [[sb(f"rowsT_part{s}{part}", [P, NC, CAP]) for part in range(2)] for s in range(2)]
        hid_parts = [[sb(f"hid_part{s}{part}", [P, NF, CAP]) for part in range(2)] for s in range(2)]
        rows = [sb(f"rows{s}", [P, NJ, XW]) for s in range(2)]
        hid = [sb(f"hid{s}", [P, NF, CAP]) for s in range(2)]
        y = [sb(f"y{s}", [P, NJ, D]) for s in range(2)]
        gidx = [sb(f"gidx{s}", [P, NJ], I32) for s in range(2)]
        sidx = [sb(f"sidx{s}", [P, NJ], I32) for s in range(2)]
        wcur = [sb(f"wcur{s}", [P, NJ]) for s in range(2)]

        lists_in, lists_t, lists_out = sem("lists_in"), sem("lists_t"), sem("lists_out")
        gu_in = [sem(f"gu_in{s}") for s in range(2)]
        dn_in = [sem(f"dn_in{s}") for s in range(2)]
        gidx_ready, sidx_ready = sem("gidx_ready"), sem("sidx_ready")
        gathered = [nc.alloc_semaphore(f"moe_gathered{s}") for s in range(2)]
        t_full = sem("t_full")
        t_high, t_low = sem("t_high"), sem("t_low")
        gu_high, gu_low = sem("gu_high"), sem("gu_low")
        dn_high, dn_low = sem("dn_high"), sem("dn_low")
        w_taken = sem("w_taken")
        gu_full = sem("gu_full")
        tanh_done, hid_mid, hid_done = sem("tanh_done"), sem("hid_mid"), sem("hid_done")
        hid_high, hid_low = sem("hid_high"), sem("hid_low")
        dn_full = sem("dn_full")
        y_done = sem("y_done")
        may_move = sem("may_move")
        added = nc.alloc_semaphore("moe_added")

        with nc.Block() as block:
            @block.sync
            def _(sp):
                sp.dma_start(lists[:, :], scr["slots"][1:E * CAP + 1, :].rearrange("(r n) o -> r (n o)", n=P))\
                    .then_inc(lists_in, 16)
                sp.wait_ge(lists_in, 16)

            @block.tensor
            def _(pe):
                pe.wait_ge(lists_in, 16)
                pe.transpose(bank[0][:, 0:P], lists[:, :], ident[:, :]).then_inc(lists_t, 1)

            @block.vector
            def _(dve):
                dve.wait_ge(lists_t, 1)
                dve.tensor_copy(listsT[:, :], bank[0][:, 0:P]).then_inc(lists_out, 1)
                dve.wait_ge(lists_out, 1)

        def over_pairs(eng, step):
            for s in range(2):
                step(s, s, 0, True, False)
            with eng.Fori(1, NI - 1) as i:
                for s in range(2):
                    step(i * 2 + s, s, i, False, False)
            for s in range(2):
                step(E - 2 + s, s, NI - 1, False, True)

        with nc.Block() as block:
            @block.sync
            def _(sp):
                def step(e, s, i, first, last):
                    if not first:
                        sp.wait_ge(gu_low, e * 2 - 2)
                    sp.dma_start(w_gu[s][:, :, 0:F], A["w_gate"][e].rearrange("(c p) n -> p c n", p=P)).then_inc(gu_in[s], 16)
                    sp.dma_start(w_gu[s][:, :, F:2 * F], A["w_up"][e].rearrange("(c p) n -> p c n", p=P)).then_inc(gu_in[s], 16)
                    if not first:
                        sp.wait_ge(dn_low, e - 1)
                    sp.dma_start(w_dn[s][:, :, :], A["w_down"][e].rearrange("(c p) n -> p c n", p=P)).then_inc(dn_in[s], 16)
                over_pairs(sp, step)

            @block.tensor
            def _(pe):
                TERMS = ((0, 0), (0, 1), (1, 0))

                def product(out, left, right, first, last):
                    for k, (a, b) in enumerate(TERMS):
                        mm = pe.matmul(out, left(a).bitcast(F32R), right(b).bitcast(F32R),
                                       start=(first and k == 0), stop=(last and k == len(TERMS) - 1))
                    return mm

                def transposes(e, s, i, start=False):
                    pe.wait_ge(gathered[s], i * 32 + 32)
                    for j in range(NJ):
                        if not start:
                            pe.wait_ge(t_low, e * NJ - NJ + j + 1)
                        for c in range(NC):
                            mm = pe.transpose(bank[j][:, c * P:(c + 1) * P], rows[s][:, j, c * P:(c + 1) * P], ident[:, :])
                        mm.then_inc(t_full, 1)

                def down(e, s, start=False):
                    pe.wait_ge(dn_low, e + 1)
                    pe.wait_ge(hid_low, e * NF + NF)
                    for j in range(NJ):
                        if not start:
                            pe.wait_ge(y_done, e * NJ - NJ + j + 1)
                        for f in range(NF):
                            mm = product(bank[5 + j][:, :], lambda a: hid_parts[s][a][:, f, j * P:(j + 1) * P],
                                         lambda b: dn_parts[s][b][:, f, :], f == 0, f == NF - 1)
                        mm.then_inc(dn_full, 1)

                def step(e, s, i, first, last):
                    pe.wait_ge(gu_low, e * 2 + 2)
                    pe.wait_ge(t_low, e * NJ + NJ)
                    for f in range(NF):
                        if not (first and s == 0):
                            pe.wait_ge(hid_done, e * NF - NF + f + 1)
                        for half in range(2):
                            at = half * F + f * P
                            for c in range(NC):
                                mm = product(bank[2 + f][:, half * CAP:(half + 1) * CAP],
                                             lambda a: gu_parts[s][a][:, c, at:at + P],
                                             lambda b: rowsT_parts[s][b][:, c, :], c == 0, c == NC - 1)
                        mm.then_inc(gu_full, 1)
                    if not (last and s == 1):
                        transposes(e + 1, 1 - s, i + s)
                    if not (first and s == 0):
                        down(e - 1, 1 - s, start=(first and s == 1))

                transposes(0, 0, 0, start=True)
                over_pairs(pe, step)
                down(E - 1, 1)

            def halves(t, k):
                return t[:, k * (NC // 2):(k + 1) * (NC // 2), :]

            @block.scalar
            def _(act):
                def turn(e, s, first):
                    for j in range(NJ):
                        act.wait_ge(t_full, e * NJ + j + 1)
                        if not first:
                            act.wait_ge(gu_full, e * NF - NF)
                        act.activation(rowsT_parts[s][0][:, :, j * P:(j + 1) * P].bitcast(F32R),
                                       bank[j][:, :].rearrange("p (c q) -> p c q", q=P), ACT.Copy).then_inc(t_high, 1)

                def out(e, s, first):
                    for j in range(NJ):
                        act.wait_ge(dn_full, e * NJ + j + 1)
                        if not first:
                            act.wait_ge(added, e * 32 - 32)
                        act.activation(y[s][:, j, :], bank[5 + j][:, :], ACT.Copy, scale=wcur[s][:, j:j + 1])\
                            .then_inc(y_done, 1)

                def split_gu(s, i, k):
                    act.wait_ge(gu_in[s], i * 32 + 32)
                    act.activation(halves(gu_parts[s][0], k).bitcast(F32R), halves(w_gu[s], k), ACT.Copy)\
                        .then_inc(gu_high, 1)

                def step(e, s, i, first, last):
                    for f in range(NF):
                        act.wait_ge(gu_full, e * NF + f + 1)
                        if not first:
                            act.wait_ge(hid_low, e * NF - NF)
                        act.activation(hid[s][:, f, :], bank[2 + f][:, 0:CAP], ACT.Tanh, scale=0.5).then_inc(tanh_done, 1)
                        if f < 2 and not (last and s == 1):
                            split_gu(1 - s, i + s, f)
                    act.wait_ge(dn_in[s], i * 16 + 16)
                    if not first:
                        act.wait_ge(dn_full, e * NJ - NJ)
                    act.activation(dn_parts[s][0][:, :, :].bitcast(F32R), w_dn[s][:, :, :], ACT.Copy).then_inc(dn_high, 1)
                    for f in range(NF):
                        act.wait_ge(hid_done, e * NF + f + 1)
                        act.activation(hid_parts[s][0][:, f, :].bitcast(F32R), hid[s][:, f, :], ACT.Copy)\
                            .then_inc(hid_high, 1)
                    if not (last and s == 1):
                        turn(e + 1, 1 - s, first and s == 0)
                    if not (first and s == 0):
                        act.wait_ge(w_taken, e)
                        out(e - 1, 1 - s, (first and s == 1))

                for k in range(2):
                    split_gu(0, 0, k)
                turn(0, 0, True)
                over_pairs(act, step)
                out(E - 1, 1, False)

            @block.vector
            def _(dve):
                def low(part, whole):
                    high, rest = part
                    return dve.tensor_tensor(rest.bitcast(F32R), whole, high, ALU.subtract)

                def split_gu(e, s, k):
                    dve.wait_ge(gu_high, e * 2 + k + 1)
                    low([halves(part, k) for part in gu_parts[s]], halves(w_gu[s], k)).then_inc(gu_low, 1)

                def turn(e, s):
                    for j in range(NJ):
                        dve.wait_ge(t_high, e * NJ + j + 1)
                        low([part[:, :, j * P:(j + 1) * P] for part in rowsT_parts[s]],
                            bank[j][:, :].rearrange("p (c q) -> p c q", q=P)).then_inc(t_low, 1)

                def take_weights(e, s, first):
                    if not first:
                        dve.wait_ge(y_done, e * NJ - NJ)
                    dve.tensor_scalar(wcur[s][:, :], rows[s][:, :, bass.ds(e + D, 1)].rearrange("p j o -> p (j o)"),
                                      0.5, None, ALU.mult).then_inc(w_taken, 1)

                def scatter_list(e, s, first):
                    if not first:
                        dve.wait_ge(added, e * 32 - 32)
                    dve.tensor_copy(sidx[s][:, :], listsT[:, bass.ds(e * NJ, NJ)]).then_inc(sidx_ready, 1)

                def gather_list(e, s):
                    dve.tensor_copy(gidx[s][:, :], listsT[:, bass.ds(e * NJ, NJ)]).then_inc(gidx_ready, 1)

                def step(e, s, i, first, last):
                    for f in range(NF):
                        dve.wait_ge(tanh_done, e * NF + f + 1)
                        dve.scalar_tensor_tensor(out=hid[s][:, f, :], in0=hid[s][:, f, :], scalar=1.0,
                                                 in1=bank[2 + f][:, 0:CAP], op0=ALU.add, op1=ALU.mult).then_inc(hid_mid, 1)
                        dve.wait_ge(hid_mid, e * NF + f + 1)
                        dve.tensor_tensor(hid[s][:, f, :], hid[s][:, f, :], bank[2 + f][:, CAP:2 * CAP], ALU.mult)\
                            .then_inc(hid_done, 1)
                        if f < 2 and not (last and s == 1):
                            split_gu(e + 1, 1 - s, f)
                    scatter_list(e, s, first)
                    if not last:
                        dve.wait_ge(gathered[s], i * 32 + 32)
                        gather_list(e + 2, s)
                    if not (last and s == 1):
                        turn(e + 1, 1 - s)
                    dve.wait_ge(dn_high, e + 1)
                    low([part[:, :, :] for part in dn_parts[s]], w_dn[s][:, :, :]).then_inc(dn_low, 1)
                    if not (last and s == 1):
                        take_weights(e + 1, 1 - s, first and s == 0)

                gather_list(0, 0)
                gather_list(1, 1)
                for k in range(2):
                    split_gu(0, 0, k)
                turn(0, 0)
                take_weights(0, 0, True)
                over_pairs(dve, step)

            @block.gpsimd
            def _(pool):
                def gather(e, s):
                    pool.wait_ge(gidx_ready, e + 1)
                    pool.sem_inc(may_move, 1)
                    for j in range(NJ):
                        pool.indirect_dma_start(
                            out=rows[s][:, j, :], out_offset=None, in_=scr["rows"][:, :],
                            in_offset=bass.IndirectOffsetOnAxis(ap=gidx[s][:, j:j + 1], axis=0)).then_inc(gathered[s], 16)

                def next_rows(e, s):
                    pool.wait_ge(t_full, e * NJ - NJ)
                    pool.wait_ge(w_taken, e - 1)
                    gather(e, s)

                def step(e, s, start=False, more=True):
                    for f in range(NF):
                        pool.wait_ge(hid_high, e * NF + f + 1)
                        pool.tensor_tensor(hid_parts[s][1][:, f, :].bitcast(F32R), hid[s][:, f, :],
                                           hid_parts[s][0][:, f, :], ALU.subtract).then_inc(hid_low, 1)
                    if more:
                        next_rows(e + 3, 1 - s)
                    if not start:
                        pool.wait_ge(added, e * 32)
                    pool.wait_ge(y_done, e * NJ + NJ)
                    pool.wait_ge(sidx_ready, e + 1)
                    pool.sem_inc(may_move, 1)
                    for j in range(NJ):
                        pool.indirect_dma_start(
                            out=scr["acc"][:, :], out_offset=bass.IndirectOffsetOnAxis(ap=sidx[s][:, j:j + 1], axis=0),
                            in_=y[s][:, j, :], in_offset=None, compute_op=ALU.add).then_inc(added, 16)

                gather(0, 0)
                gather(1, 1)
                next_rows(2, 0)
                step(0, 0, start=True)
                step(1, 1)
                with pool.Fori(1, NI - 2) as i:
                    for s in range(2):
                        step(i * 2 + s, s)
                for e in range(E - 4, E):
                    step(e, e % 2, more=(e + 3 < E))
                pool.wait_ge(added, E * 32)

        with nc.Block() as block:
            @block.vector
            def _(dve):
                for s in sems:
                    dve.sem_clear(s)


RING = 3
DEEP = 5


def layer1_attention_stage(nc, A, scr, cst, trips):
    ident = cst["ident"]
    with ExitStack() as ctx:
        def sb(name, shape, dt=FP32):
            return ctx.enter_context(nc.sbuf_tensor("l1_" + name, shape, dt))

        sems = []

        def sem(name):
            s = ctx.enter_context(nc.semaphore("l1_" + name))
            sems.append(s)
            return s

        psum = ctx.enter_context(nc.psum_tensor("l1_psum", [P, 8, 512], FP32))
        bank = [psum[:, i, :] for i in range(8)]

        w_qkv = sb("w_qkv", [P, NC, 3 * D])
        w_o = sb("w_o", [P, NC, D])
        w_xo = sb("w_xo", [P, NC, D])
        w_xdiag = sb("w_xdiag", [P, 3, P])
        w_conv = sb("w_conv", [P, 2, NC, DH])
        wcol = sb("wcol", [P, 2, NC])
        b_conv = sb("b_conv", [P, 2])
        b_qkv = sb("b_qkv", [P, 3 * NC])
        b_o = sb("b_o", [P, D])
        b_xo = sb("b_xo", [P, D])
        x_new = sb("x_new", [P, NT, D])
        x = sb("x", [P, NT, D])
        xT = sb("xT", [P, NC, S])
        q_parts = [sb("q_high", [P, NC, S]), sb("q_low", [P, NC, S])]
        k_parts = [sb("k_high", [P, NC, S]), sb("k_low", [P, NC, S])]
        q_stack = sb("q_stack", [P, RING, 2, S])
        k_stack = sb("k_stack", [P, RING, 2, S])
        v = sb("v", [P, NT, D])
        yT = xT
        probs = sb("probs", [P, DEEP, 2, S])
        pT = sb("pT", [P, 6, NT, S])
        ctx_T = sb("ctx_T", [P, NC, S2])
        pxT = [pT[:, i, :, :] for i in range(2)]
        x4T, qxT, x5T, xc = pT[:, 2, :, :], pT[:, 3, :, :], pT[:, 2, :, :], pT[:, 3, 0:2, :]
        kxpad = pT[:, 4, :, :].rearrange("p t s -> p (t s)")[:, 0:H * S2].rearrange("p (h k) -> p h k", k=S2)
        vx = pT[:, 5, 0, :]
        seen = pT[:, 5, 2, 0:NT * S2].bitcast(I32).rearrange("p (t k) -> p t k", k=S2)
        floor = pT[:, 5, 1, 0:NT * S2].rearrange("p (t k) -> p t k", k=S2)
        px = [probs[:, i, 0, 0:HG * S2].rearrange("p (h k) -> p h k", h=HG) for i in range(4)]
        yxT = probs[:, 0:NC, 1, :]
        nmax = sb("nmax", [P, DEEP, 2])
        psums = sb("psums", [P, DEEP, 2])
        rsum = sb("rsum", [P, DEEP, 2])
        xmax = sb("xmax", [P, 4, HG])
        xsum = sb("xsum", [P, 4, HG])
        xrsum = sb("xrsum", [P, 4, HG])

        setup_in, setup_conv = sem("setup_in"), sem("setup_conv")
        late_in = sem("late_in")
        with nc.Block() as block:
            @block.sync
            def _(sp):
                sp.dma_start(w_qkv[:, :, :], A["w_qkv1"].rearrange("(c p) n -> p c n", p=P)).then_inc(setup_in, 16)
                sp.dma_start(b_qkv[:, :], A["b_qkv1"]).then_inc(setup_in, 16)
                for dst, src in ((b_o, A["b_o1"]), (b_xo, A["b_xo"])):
                    sp.dma_start(dst[:, :], src.rearrange("(a n) -> a n", a=1).to_broadcast([P, D])).then_inc(setup_in, 16)
                sp.dma_start(wcol[:, :, :], A["conv_w"]).then_inc(setup_in, 16)
                sp.dma_start(b_conv[:, :], A["conv_b"]).then_inc(setup_in, 16)
                sp.wait_ge(setup_in, 6 * 16)

            @block.vector
            def _(dve):
                dve.memset(w_xdiag[:, :, :], 0.0)
                dve.wait_ge(setup_in, 6 * 16)
                dve.tensor_scalar(b_qkv[:, 0:NC], b_qkv[:, 0:NC], QSCALE, None, ALU.mult)
                dve.tensor_scalar(w_qkv[:, :, 0:D], w_qkv[:, :, 0:D], QSCALE, None, ALU.mult)
                dve.wait_ge(setup_conv, 2)
                for br in range(2):
                    for c in range(NC):
                        dve.tensor_scalar(w_conv[:, br, c, :], cst["groups"][:, :], wcol[:, br, c:c + 1], None, ALU.mult)

            @block.gpsimd
            def _(pool):
                pool.affine_select(out=cst["groups"][:, :], in_=cst["ones"][:, 0:DH], pattern=[[-4, DH]],
                                   compare_op=ALU.is_ge, fill=0.0, base=0, channel_multiplier=1).then_inc(setup_conv, 1)
                pool.wait_ge(setup_conv, 1)
                pool.affine_select(out=cst["groups"][:, :], in_=cst["groups"][:, :], pattern=[[4, DH]],
                                   compare_op=ALU.is_ge, fill=0.0, base=3, channel_multiplier=-1).then_inc(setup_conv, 1)

        class Norm:
            def __init__(self, name):
                self.stats, self.mv = sb(name + "_stats", [P, NT, 6]), sb(name + "_mv", [P, NT, 2])
                self.vare, self.rstd = sb(name + "_vare", [P, NT]), sb(name + "_rstd", [P, NT])
                self.var, self.root, self.done = sem(name + "_var"), sem(name + "_root"), sem(name + "_done")
                self.chain = sem(name + "_chain")

            def statistics(self, dve, link, rows):
                for t in range(NT):
                    dve.bn_stats(self.stats[:, t, :], rows[:, t, :]).then_inc(self.chain, 1)
                link.skip(NT)
                for t in range(NT):
                    dve.bn_aggr(self.mv[:, t, :], self.stats[:, t, :]).then_inc(self.chain, 1)
                link.skip(NT)
                dve.tensor_scalar(self.vare[:, :], self.mv[:, :, 1], EPS, None, ALU.add).then_inc(self.var, 1)

            def reciprocal_root(self, pool, k):
                pool.wait_ge(self.var, k + 1)
                pool.tensor_tensor(self.rstd[:, :], self.vare[:, :], cst["mhalf"][:, 0:NT], ALU.pow)\
                    .then_inc(self.root, 1)

            def normalise(self, dve, k, rows):
                dve.wait_ge(self.root, k + 1)
                for t in range(NT):
                    dve.tensor_scalar(rows[:, t, :], rows[:, t, :], self.mv[:, t, 0:1], self.rstd[:, t:t + 1],
                                      ALU.subtract, ALU.mult).then_inc(self.done, 1)
                dve.wait_ge(self.done, NT * (k + 1))

        norm_new, norm = Norm("norm_new"), Norm("norm")

        loaded = sem("loaded")
        turned, turned_out = sem("turned"), sem("turned_out")
        proj_full = sem("proj_full")
        PROJ = [("q", 0), ("k", 0), ("q", 1), ("k", 1), ("v", 0), ("v", 1), ("v", 2), ("v", 3),
                ("q", 2), ("k", 2), ("q", 3), ("k", 3)]
        high_done = sem("high_done")
        low_done = sem("low_done")
        v_done = sem("v_done")

        def parts_of(j):
            return sum(kind != "v" for kind, _ in PROJ[:j + 1])

        def wait_drained(eng, j):
            if PROJ[j][0] == "v":
                eng.wait_ge(v_done, j + 1 - parts_of(j))
            else:
                eng.wait_ge(low_done, parts_of(j))

        EARLY = 8
        LATE_BANK = 7

        def proj_bank(j):
            return j % 2 if j < EARLY else LATE_BANK

        def project(pe, j, chunks=range(NC)):
            kind, i = PROJ[j]
            for c in chunks:
                if kind == "v":
                    mm = pe.matmul(bank[proj_bank(j)], xT[:, c, i * P:(i + 1) * P], w_qkv[:, c, 2 * D:3 * D],
                                   start=(c == 0), stop=(c == NC - 1))
                else:
                    at = i * P + (D if kind == "k" else 0)
                    mm = pe.matmul(bank[proj_bank(j)], w_qkv[:, c, at:at + P], xT[:, c, :],
                                   start=(c == 0), stop=(c == NC - 1))
                if c == NC - 1:
                    mm.then_inc(proj_full, 1)

        def take_high(act, j):
            kind, i = PROJ[j]
            at = i + (NC if kind == "k" else 0)
            high = (k_parts if kind == "k" else q_parts)[0]
            act.wait_ge(proj_full, j + 1)
            act.activation(high[:, i, :].bitcast(F32R), bank[proj_bank(j)], ACT.Identity, bias=b_qkv[:, at:at + 1])\
                .then_inc(high_done, 1)

        def take_low(dve, j):
            kind, i = PROJ[j]
            at = i + (NC if kind == "k" else 0)
            high, low = k_parts if kind == "k" else q_parts
            dve.wait_ge(high_done, parts_of(j))
            dve.scalar_tensor_tensor(out=low[:, i, :].bitcast(F32R), in0=bank[proj_bank(j)], scalar=b_qkv[:, at:at + 1],
                                     in1=high[:, i, :], op0=ALU.add, op1=ALU.subtract).then_inc(low_done, 1)

        START_STEPS = 4 + EARLY

        def start_pe(pe):
            for step in range(START_STEPS):
                if step in (2, 3):
                    for t in (2 * step - 4, 2 * step - 3):
                        pe.wait_ge(norm_new.done, t + 1)
                        if t >= 2:
                            pe.wait_ge(turned_out, t - 1)
                        for c in range(NC):
                            mm = pe.transpose(bank[t % 2][:, c * P:(c + 1) * P], x_new[:, t, c * P:(c + 1) * P], ident[:, :])
                        mm.then_inc(turned, 1)
                if step >= 4:
                    j = step - 4
                    if j == 0:
                        pe.wait_ge(turned_out, NT)
                    if j >= 2:
                        wait_drained(pe, j - 2)
                    project(pe, j)
                yield

        def start_act(act):
            for step in range(START_STEPS):
                if step in (2, 3):
                    for t in (2 * step - 4, 2 * step - 3):
                        act.wait_ge(turned, t + 1)
                        act.activation(xT[:, :, t * P:(t + 1) * P], bank[t % 2].rearrange("p (c q) -> p c q", q=P),
                                       ACT.Copy).then_inc(turned_out, 1)
                if step >= 4:
                    j = step - 4
                    kind, i = PROJ[j]
                    if kind == "v":
                        act.wait_ge(proj_full, j + 1)
                        act.activation(v[:, i, :], bank[proj_bank(j)], ACT.Copy).then_inc(v_done, 1)
                    else:
                        take_high(act, j)
                yield

        def start_dve(dve):
            link = chain_of(dve, norm_new.chain)
            dve.wait_ge(loaded, 16)
            norm_new.statistics(dve, link, x_new)
            yield
            norm_new.normalise(dve, 0, x_new)
            for step in range(1, START_STEPS):
                yield
                j = step - 4
                if j >= 0 and PROJ[j][0] != "v":
                    take_low(dve, j)

        def start_pool(pool):
            norm_new.reciprocal_root(pool, 0)
            yield

        stack_in = [sem(f"stack_in{i}") for i in range(RING)]
        PAIRS = 2 * NC

        def stack_pair(sp, u):
            for hh in range(2):
                r = slice((2 * (u % 2) + hh) * DH, (2 * (u % 2) + hh + 1) * DH)
                for place in range(4):
                    to = slice(place * DH, (place + 1) * DH)
                    for stack, part in ((q_stack, q_parts[place // 2]), (k_stack, k_parts[place % 2])):
                        sp.dma_start(stack[to, u % RING, hh, :], part[r, u // 2, :]).then_inc(stack_in[u % RING], 16)

        tail_in, resid = sem("tail_in"), sem("resid")
        scores_full, max_ready, exp_done = sem("scores_full"), sem("max_ready"), sem("exp_done")
        rsum_ready, probs_ready = sem("rsum_ready"), sem("probs_ready")
        pT_full, pT_out_dve, pT_out_act = sem("pT_full"), sem("pT_out_dve"), sem("pT_out_act")
        attn_full, attn_out = sem("attn_full"), sem("attn_out")
        LAG = 3
        UNITS = [(g, t, p) for g in range(NC) for p in range(2) for t in range(NT)]
        PER_G = 2 * NT

        def heads(b, first=False):
            N = len(UNITS)
            with nc.Block() as block:
                @block.sync
                def _(sp):
                    sp.dma_start(ctx_T[:, :, :], A["ctxT"][b].rearrange("(c p) n -> p c n", p=P)).then_inc(tail_in, 16)
                    for u in range(RING, PAIRS):
                        sp.wait_ge(scores_full, (u - RING + 1) * NT)
                        wait_drained(sp, PROJ.index(("k", u // 2)))
                        stack_pair(sp, u)
                    sp.wait_ge(tail_in, 16)
                    if first:
                        sp.wait_ge(late_in, LATE_LOADS * 16)
                    for i in range(RING):
                        sp.wait_ge(stack_in[i], len(range(i, PAIRS, RING)) * 16 * 16)

                @block.tensor
                def _(pe):
                    for n in range(N + LAG + NT):
                        if n < N:
                            g, t, p = UNITS[n]
                            u = 2 * g + p
                            pe.wait_ge(stack_in[u % RING], (u // RING + 1) * 16 * 16)
                            if n >= 2:
                                pe.wait_ge(exp_done, 2 * (n - 1))
                            for hh in range(2):
                                mm = pe.matmul(bank[2 * (n % 2) + hh],
                                               q_stack[:, u % RING, hh, t * P:(t + 1) * P].bitcast(F32R),
                                               k_stack[:, u % RING, hh, :].bitcast(F32R), start=True, stop=True)
                            mm.then_inc(scores_full, 1)
                            if n % 3 < 2 and EARLY + n // 3 < len(PROJ):
                                j = EARLY + n // 3
                                if n % 3 == 0 and n > 0:
                                    wait_drained(pe, j - 1)
                                project(pe, j, range(2 * (n % 3), 2 * (n % 3) + 2))
                        m = n - LAG
                        if m >= PER_G and m % PER_G < NT:
                            g, kc = m // PER_G - 1, m % PER_G
                            if kc == 0:
                                pe.wait_ge(pT_out_dve, m)
                                pe.wait_ge(pT_out_act, m)
                                if g >= 1:
                                    pe.wait_ge(attn_out, g)
                            for h in range(HG):
                                mm = pe.matmul(psum[h * DH:(h + 1) * DH, 6, :],
                                               v[:, kc, (HG * g + h) * DH:(HG * g + h + 1) * DH],
                                               pT[:, (HG * g + h) % 6, kc, :], start=(kc == 0), stop=(kc == NT - 1))
                            mm.then_inc(attn_full, 1)
                        if 0 <= m < N:
                            pe.wait_ge(probs_ready, m + 1)
                            for hh in range(2):
                                if m >= 1:
                                    pe.wait_ge(pT_out_act if hh else pT_out_dve, m)
                                for kc in range(NT):
                                    mm = pe.transpose(bank[4 + hh][:, kc * P:(kc + 1) * P],
                                                      probs[:, m % DEEP, hh, kc * P:(kc + 1) * P], ident[:, :])
                                mm.then_inc(pT_full, 1)

                @block.vector
                def _(dve):
                    for n in range(N + LAG):
                        if n < N:
                            dve.wait_ge(scores_full, n + 1)
                            if n >= DEEP:
                                dve.wait_ge(exp_done, 2 * (n - DEEP + 1))
                            dve.tensor_reduce(nmax[:, n % DEEP, :], psum[:, 2 * (n % 2):2 * (n % 2) + 2, :], AX.X, ALU.max,
                                              negate=True).then_inc(max_ready, 1)
                        m = n - 1
                        if 0 <= m < N:
                            dve.wait_ge(exp_done, 2 * m + 2)
                            if m >= DEEP:
                                dve.wait_ge(probs_ready, m - DEEP + 1)
                            dve.reciprocal(rsum[:, m % DEEP, :], psums[:, m % DEEP, :]).then_inc(rsum_ready, 1)
                        m = n - LAG
                        if 0 <= m < N:
                            g, t, p = UNITS[m]
                            dve.wait_ge(pT_full, 2 * m + 1)
                            u = 2 * g + p
                            if u >= 3:
                                dve.wait_ge(attn_full, ((u - 3) // 2 + 1) * NT)
                            dve.tensor_copy(pT[:, 2 * u % 6, :, t * P:(t + 1) * P],
                                            bank[4].rearrange("p (k q) -> p k q", q=P)).then_inc(pT_out_dve, 1)
                        if n % 3 == 2 and EARLY + n // 3 < len(PROJ):
                            take_low(dve, EARLY + n // 3)

                @block.scalar
                def _(act):
                    for n in range(N + LAG + NT + 1):
                        if n < N:
                            act.wait_ge(max_ready, n + 1)
                            if n >= DEEP:
                                act.wait_ge(pT_full, 2 * (n - DEEP + 1))
                                act.wait_ge(rsum_ready, n - DEEP + 1)
                            for hh in range(2):
                                act.activation(probs[:, n % DEEP, hh, :], bank[2 * (n % 2) + hh], ACT.Exp,
                                               bias=nmax[:, n % DEEP, hh:hh + 1],
                                               accum_out=psums[:, n % DEEP, hh:hh + 1]).then_inc(exp_done, 1)
                        m = n - LAG
                        if 0 <= m < N:
                            g, t, p = UNITS[m]
                            act.wait_ge(pT_full, 2 * m + 2)
                            u = 2 * g + p
                            if u >= 3:
                                act.wait_ge(attn_full, ((u - 3) // 2 + 1) * NT)
                            act.activation(pT[:, 2 * u % 6 + 1, :, t * P:(t + 1) * P],
                                           bank[5].rearrange("p (k q) -> p k q", q=P), ACT.Copy).then_inc(pT_out_act, 1)
                        if n % 3 == 1 and EARLY + n // 3 < len(PROJ):
                            take_high(act, EARLY + n // 3)
                        if m >= PER_G and m % PER_G == NT:
                            g = m // PER_G - 1
                            act.wait_ge(attn_full, (g + 1) * NT)
                            act.activation(yT[:, g, :], bank[6], ACT.Identity,
                                           bias=b_qkv[:, 2 * NC + g:2 * NC + g + 1]).then_inc(attn_out, 1)

                @block.gpsimd
                def _(pool):
                    for n in range(N):
                        pool.wait_ge(rsum_ready, n + 1)
                        pr = probs[:, n % DEEP, :, :]
                        pool.tensor_tensor(pr, pr, rsum[:, n % DEEP, :].rearrange("p (h a) -> p h a", a=1)
                                           .to_broadcast([P, 2, S]), ALU.mult).then_inc(probs_ready, 1)
                    for t in range(NT):
                        pool.tensor_tensor(x[:, t, :], x_new[:, t, :], b_o[:, :], ALU.add).then_inc(resid, 1)
                    pool.wait_ge(resid, NT)

        kx_full, kx_out = sem("kx_full"), sem("kx_out")
        seen_in = sem("seen_in")
        kx_zero = sem("kx_zero")
        o_full, res1 = sem("o_full"), sem("res1")
        t_full, t_out = sem("t_full"), sem("t_out")
        qx_full, qx_out = sem("qx_full"), sem("qx_out")
        resid2 = sem("resid2")
        xs_full, xs_out = sem("xs_full"), sem("xs_out")
        xsub_done, xexp_done, xrsum_ready, xprobs_ready = (sem(n) for n in ("xsub", "xexp", "xrsum_ready", "xprobs"))
        xpT_full, xpT_out = sem("xpT_full"), sem("xpT_out")
        xa_full, xa_out = sem("xa_full"), sem("xa_out")
        xo_full, res2 = sem("xo_full"), sem("res2")
        conv_full, conv_out, stored = sem("conv_full"), sem("conv_out"), sem("stored")
        chain_x = sem("chain_x")
        XU = [(g, t) for g in range(NC) for t in range(NT)]
        XLAG = 2
        NX = len(XU)

        FIRST_UNIT = 6
        AFTER = FIRST_UNIT + NX + XLAG + 1
        TAIL_STEPS = AFTER + 6

        def transposes(pe, k):
            for t in range(NT):
                pe.wait_ge(norm.done, k * NT + t + 1)
                for c in range(NC):
                    mm = pe.transpose(bank[4 + t][:, c * P:(c + 1) * P], x[:, t, c * P:(c + 1) * P], ident[:, :])
                mm.then_inc(t_full, 1)

        def transposes_out(act, k, dst):
            for t in range(NT):
                act.wait_ge(t_full, k * NT + t + 1)
                act.activation(dst[:, :, t * P:(t + 1) * P], bank[4 + t].rearrange("p (c q) -> p c q", q=P),
                               ACT.Copy).then_inc(t_out, 1)

        def tail_pe(pe):
            for step in range(TAIL_STEPS):
                n = step - FIRST_UNIT
                m = n - XLAG
                if step == 0:
                    for t in range(NT):
                        for c in range(NC):
                            mm = pe.matmul(bank[4 + t], yT[:, c, t * P:(t + 1) * P], w_o[:, c, :],
                                           start=(c == 0), stop=(c == NC - 1))
                        mm.then_inc(o_full, 1)
                    for c in range(NC):
                        mm = pe.matmul(bank[2][:, c * S2:(c + 1) * S2], w_xdiag[:, 1, :], ctx_T[:, c, :],
                                       start=True, stop=True)
                    mm.then_inc(kx_full, 1)
                    for c in range(NC):
                        mm = pe.matmul(bank[3][0:S2, c * P:(c + 1) * P], ctx_T[:, c, :], w_xdiag[:, 2, :],
                                       start=True, stop=True)
                    mm.then_inc(kx_full, 1)
                if step == 4:
                    transposes(pe, 0)
                if step == 5:
                    pe.wait_ge(t_out, NT)
                    for c in range(NC):
                        pe.matmul(bank[4 + c], w_xdiag[:, 0, :], x4T[:, c, :], start=True, stop=True).then_inc(qx_full, 1)
                if 0 <= n < NX:
                    g, t = XU[n]
                    if n == 0:
                        pe.wait_ge(kx_out, 2)
                        pe.wait_ge(qx_out, NC)
                    if n >= 2:
                        pe.wait_ge(xs_out, n - 1)
                    pe.matmul(bank[2 + n % 2][:, 0:HG * S2], qxT[:, g, t * P:(t + 1) * P],
                              kxpad[:, g * HG:(g + 1) * HG, :].rearrange("p h k -> p (h k)"),
                              start=True, stop=True).then_inc(xs_full, 1)
                if NT <= m <= NX and m % NT == 0:
                    g = m // NT - 1
                    pe.wait_ge(xpT_out, m)
                    if g >= 2:
                        pe.wait_ge(xa_out, g - 1)
                    for h in range(HG):
                        mm = pe.matmul(psum[h * DH:(h + 1) * DH, 4 + g % 2, :], vx[:, (g * HG + h) * DH:(g * HG + h + 1) * DH],
                                       pxT[g % 2][:, h, :], start=True, stop=True)
                    mm.then_inc(xa_full, 1)
                if 0 <= m < NX:
                    pe.wait_ge(xprobs_ready, m + 1)
                    if m >= 2:
                        pe.wait_ge(xpT_out, m - 1)
                    for h in range(HG):
                        mm = pe.transpose(bank[6 + m % 2][0:S2, h * P:(h + 1) * P], px[m % 4][:, h, :], ident[:, :])
                    mm.then_inc(xpT_full, 1)
                if step == AFTER:
                    pe.wait_ge(xa_out, NC)
                    pe.wait_ge(xs_out, NX)
                    for t in range(NT):
                        for c in range(NC):
                            mm = pe.matmul(bank[4 + t], yxT[:, c, t * P:(t + 1) * P], w_xo[:, c, :],
                                           start=(c == 0), stop=(c == NC - 1))
                        mm.then_inc(xo_full, 1)
                if step == AFTER + 4:
                    transposes(pe, 1)
                if step == AFTER + 5:
                    pe.wait_ge(t_out, 2 * NT)
                    for br in range(2):
                        for c in range(NC):
                            mm = pe.matmul(psum[c * DH:(c + 1) * DH, 2 + br, :], w_conv[:, br, c, :], x5T[:, c, :],
                                           start=True, stop=True)
                        mm.then_inc(conv_full, 1)
                yield

        def tail_act(act):
            for step in range(TAIL_STEPS):
                n = step - FIRST_UNIT
                m = n - XLAG
                if step == 0:
                    act.wait_ge(kx_zero, 2)
                    act.wait_ge(kx_full, 1)
                    for h in range(HG):
                        r = slice(h * DH, (h + 1) * DH)
                        last = act.activation(kxpad[r, :, :].rearrange("p (c h) k -> p c h k", h=HG)[:, :, h, :],
                                              psum[r, 2, 0:NC * S2].rearrange("p (c k) -> p c k", k=S2), ACT.Copy)
                    last.then_inc(kx_out, 1)
                    act.wait_ge(kx_full, 2)
                    act.activation(vx[0:S2, :], psum[0:S2, 3, :], ACT.Copy).then_inc(kx_out, 1)
                if step == 4:
                    transposes_out(act, 0, x4T)
                if step == 5:
                    for c in range(NC):
                        act.wait_ge(qx_full, c + 1)
                        act.activation(qxT[:, c, :], bank[4 + c], ACT.Copy).then_inc(qx_out, 1)
                if 0 <= n < NX:
                    act.wait_ge(xsub_done, n + 1)
                    act.activation(px[n % 4], px[n % 4], ACT.Exp, scale=XSCALE).then_inc(xexp_done, 1)
                if 0 <= m < NX:
                    g, t = XU[m]
                    act.wait_ge(xpT_full, m + 1)
                    act.activation(pxT[g % 2][0:S2, :, t * P:(t + 1) * P],
                                   psum[0:S2, 6 + m % 2, :].rearrange("p (h q) -> p h q", q=P), ACT.Copy)\
                        .then_inc(xpT_out, 1)
                if NT <= m <= NX and m % NT == 0:
                    g = m // NT - 1
                    act.wait_ge(xa_full, g + 1)
                    act.activation(yxT[:, g, :], bank[4 + g % 2], ACT.Copy).then_inc(xa_out, 1)
                if step == AFTER + 4:
                    transposes_out(act, 1, x5T)
                if step == AFTER + 5:
                    for br in range(2):
                        act.wait_ge(conv_full, br + 1)
                        act.activation(xc[:, br, :], bank[2 + br], ACT.Identity, bias=b_conv[:, br:br + 1])\
                            .then_inc(conv_out, 1)
                yield

        def tail_dve(dve):
            link = chain_of(dve, norm.chain)
            xlink = chain_of(dve, chain_x)

            def each(a):
                return a.rearrange("p (h o) -> p h o", o=1).to_broadcast([P, HG, S2])

            for step in range(TAIL_STEPS):
                n = step - FIRST_UNIT
                m = n - 1
                if step == 4:
                    dve.wait_ge(seen_in, 16)
                    xlink(dve.tensor_scalar(floor[:, :, :], seen[:, :, :], 0.0, -TAKEN, ALU.not_equal, ALU.mult))
                    xlink(dve.tensor_scalar(floor[:, :, :], floor[:, :, :], 1e20, None, ALU.subtract))
                if step == 1:
                    for t in range(NT):
                        dve.wait_ge(o_full, t + 1)
                        dve.tensor_tensor(x[:, t, :], bank[4 + t], x[:, t, :], ALU.add).then_inc(res1, 1)
                    dve.wait_ge(res1, NT)
                if step == 2:
                    norm.statistics(dve, link, x)
                if step == 3:
                    norm.normalise(dve, 0, x)
                if 0 <= n < NX:
                    g, t = XU[n]
                    dve.wait_ge(xs_full, n + 1)
                    if n >= 4:
                        dve.wait_ge(xpT_full, n - 3)
                    dve.tensor_tensor(px[n % 4], bank[2 + n % 2][:, 0:HG * S2].rearrange("p (h k) -> p h k", h=HG),
                                      floor[:, t, :].rearrange("p (o k) -> p o k", o=1).to_broadcast([P, HG, S2]),
                                      ALU.min).then_inc(xs_out, 1)
                    dve.wait_ge(xs_out, n + 1)
                    xlink(dve.tensor_reduce(xmax[:, n % 4, :], px[n % 4], AX.X, ALU.max))
                    dve.tensor_tensor(px[n % 4], px[n % 4], each(xmax[:, n % 4, :]), ALU.subtract).then_inc(xsub_done, 1)
                if 0 <= m < NX:
                    dve.wait_ge(xexp_done, m + 1)
                    xlink(dve.tensor_reduce(xsum[:, m % 4, :], px[m % 4], AX.X, ALU.add))
                    if m >= 4:
                        dve.wait_ge(xprobs_ready, m - 3)
                    dve.reciprocal(xrsum[:, m % 4, :], xsum[:, m % 4, :]).then_inc(xrsum_ready, 1)
                if step == AFTER + 1:
                    for t in range(NT):
                        dve.wait_ge(xo_full, t + 1)
                        dve.wait_ge(resid2, t + 1)
                        dve.tensor_tensor(x[:, t, :], bank[4 + t], x[:, t, :], ALU.add).then_inc(res2, 1)
                    dve.wait_ge(res2, NT)
                if step == AFTER + 2:
                    norm.statistics(dve, link, x)
                if step == AFTER + 3:
                    norm.normalise(dve, 1, x)
                yield

        def tail_pool(pool):
            for step in range(TAIL_STEPS):
                m = step - FIRST_UNIT - 1
                if step == 0:
                    pool.memset(kxpad, 0.0).then_inc(kx_zero, 1)
                    pool.memset(vx, 0.0).then_inc(kx_zero, 1)
                if step == 2:
                    norm.reciprocal_root(pool, 0)
                if 0 <= m < NX:
                    pool.wait_ge(xrsum_ready, m + 1)
                    pool.tensor_tensor(px[m % 4], px[m % 4], xrsum[:, m % 4, :].rearrange("p (h o) -> p h o", o=1)
                                       .to_broadcast([P, HG, S2]), ALU.mult).then_inc(xprobs_ready, 1)
                if 3 <= m < 3 + NT:
                    t = m - 3
                    pool.wait_ge(t_full, NT)
                    pool.tensor_tensor(x[:, t, :], x[:, t, :], b_xo[:, :], ALU.add).then_inc(resid2, 1)
                if step == AFTER + 2:
                    norm.reciprocal_root(pool, 1)
                yield

        def tail_stores(sp, b):
            sp.wait_ge(norm.done, 2 * NT)
            sp.dma_start(scr["x5"].rearrange("(b t p) n -> b p t n", p=P, t=NT)[b], x[:, :, :]).then_inc(stored, 16)
            sp.wait_ge(t_out, 2 * NT)
            sp.dma_start(scr["x5T"][b].rearrange("(c p) n -> p c n", p=P), x5T).then_inc(stored, 16)
            sp.wait_ge(conv_out, 2)
            sp.dma_start(scr["xc"][b], xc).then_inc(stored, 16)
            sp.wait_ge(stored, 48)

        ORDER = "stttttsttstttsttssttttttsttttsttsttstttttt"

        def in_order(tail, start):
            programs = {"t": tail, "s": start}
            for which in ORDER:
                if programs[which] is not None:
                    next(programs[which], None)
            for program in programs.values():
                if program is not None:
                    for _ in program:
                        pass

        LATE_LOADS = 2 + 3 * HG

        def late_loads(sp):
            for dst, src in ((w_o, A["w_o1"]), (w_xo, A["w_xo"])):
                sp.dma_start(dst[:, :, :], src.rearrange("(c p) n -> p c n", p=P)).then_inc(late_in, 16)
            for i in range(3):
                for h in range(HG):
                    sp.dma_start(w_xdiag[h * DH:(h + 1) * DH, i, h * DH:(h + 1) * DH], A["w_x"][i]).then_inc(late_in, 16)

        def between_heads(end, start):
            with nc.Block() as block:
                @block.sync
                def _(sp):
                    if end is not None:
                        sp.dma_start(seen, A["mask"][end].rearrange("(t p) n -> p t n", p=P)).then_inc(seen_in, 16)
                    if start is not None:
                        sp.dma_start(x_new[:, :, :], scr["acc"][0:T, :].rearrange("(b t p) n -> b p t n", p=P, t=NT)[start])\
                            .then_inc(loaded, 16)
                        if end is None:
                            late_loads(sp)
                        for u in range(RING):
                            wait_drained(sp, PROJ.index(("k", u // 2)))
                            stack_pair(sp, u)
                    if end is not None:
                        tail_stores(sp, end)

                @block.tensor
                def _(pe):
                    in_order(None if end is None else tail_pe(pe), None if start is None else start_pe(pe))

                @block.scalar
                def _(act):
                    in_order(None if end is None else tail_act(act), None if start is None else start_act(act))

                @block.vector
                def _(dve):
                    in_order(None if end is None else tail_dve(dve), None if start is None else start_dve(dve))

                @block.gpsimd
                def _(pool):
                    in_order(None if end is None else tail_pool(pool), None if start is None else start_pool(pool))

        def clear():
            with nc.Block() as block:
                @block.vector
                def _(dve):
                    for s in sems:
                        dve.sem_clear(s)

        between_heads(None, 0)
        heads(0, first=True)
        clear()
        with nc.Fori(0, trips - 1) as b:
            between_heads(b, b + 1)
            heads(b + 1)
            clear()
        between_heads(trips - 1, None)
        clear()


PER_TRIP = 4
TT = PER_TRIP * NT


def gated_layer_stage(nc, A, scr, out, cst, trips):
    ident = cst["ident"]
    with ExitStack() as ctx:
        def sb(name, shape, dt=FP32):
            return ctx.enter_context(nc.sbuf_tensor("gl_" + name, shape, dt))

        sems = []

        def sem(name):
            s = ctx.enter_context(nc.semaphore("gl_" + name))
            sems.append(s)
            return s

        psum = ctx.enter_context(nc.psum_tensor("gl_psum", [P, 8, 512], FP32))
        bank = [psum[:, i, :] for i in range(8)]

        w = sb("w", [P, NC, D])
        w_lin = sb("w_lin", [P, 2, D])
        b_lin = sb("b_lin", [P, 2, D])
        b_out = sb("b_out", [P, D])
        gamma = sb("gamma", [P, 2])
        beta = sb("beta", [P, 2])
        conv = sb("conv", [P, 2, B, S])
        bstats = sb("bstats", [P, 2, B, 6])
        bmv = sb("bmv", [P, 2, 2])
        bvare = sb("bvare", [P, 2])
        brstd = sb("brstd", [P, 2])
        bscale = sb("bscale", [P, 2])
        bshift = sb("bshift", [P, 2])
        act_b = sb("act_b", [P, 2, TT * P])
        x = sb("x", [P, TT, D])
        xb = sb("xb", [P, TT, D])
        xT = sb("xT", [P, PER_TRIP, NC, S])
        expv = sb("expv", [P, 4, D])
        left = sb("left", [P, 4, D])
        top = sb("top", [P, 4, 8])
        nmax = sb("nmax", [P, 4])
        esum = sb("esum", [P, 4])
        rsum = sb("rsum", [P, 4])
        zo = sb("zo", [P, 2, D])
        xs = sb("xs", [P, 2, D])
        xsT = sb("xsT", [P, 2, NC, P])
        z = sb("z", [P, 2, D])
        stats = sb("stats", [P, 2, 6])
        mv = sb("mv", [P, 2, 2])
        vare = sb("vare", [P, 2])
        rstd = sb("rstd", [P, 2])
        nmean = sb("nmean", [P, 2])

        setup_in, bn_step, bn_var, bn_rstd, bn_ready, gelu_done = (
            sem(n) for n in ("setup_in", "bn_step", "bn_var", "bn_rstd", "bn_ready", "gelu_done"))
        conv_in = [sem(f"conv_in{b}") for b in range(B)]
        with nc.Block() as block:
            @block.sync
            def _(sp):
                for b in range(B):
                    sp.dma_start(conv[:, :, b, :], scr["xc"][b]).then_inc(conv_in[b], 16)
                sp.dma_start(w[:, :, :], A["w_ffn1"].rearrange("(c p) n -> p c n", p=P)).then_inc(setup_in, 16)
                sp.dma_start(w_lin[:, :, :], A["w_lin"]).then_inc(setup_in, 16)
                sp.dma_start(gamma[:, :], A["gamma"]).then_inc(setup_in, 16)
                sp.dma_start(beta[:, :], A["beta"]).then_inc(setup_in, 16)
                for br in range(2):
                    sp.dma_start(b_lin[:, br, :], A["b_lin"][br:br + 1, :].to_broadcast([P, D])).then_inc(setup_in, 16)
                sp.dma_start(b_out[:, :], A["b_ffn1"].rearrange("(a n) -> a n", a=1).to_broadcast([P, D]))\
                    .then_inc(setup_in, 16)
                sp.wait_ge(setup_in, 16 * 7)

            @block.vector
            def _(dve):
                link = chain_of(dve, bn_step)
                for b in range(B):
                    dve.wait_ge(conv_in[b], 16)
                    for br in range(2):
                        dve.bn_stats(bstats[:, br, b, :], conv[:, br, b, :]).then_inc(bn_step, 1)
                link.skip(2 * B)
                for br in range(2):
                    dve.bn_aggr(bmv[:, br, :], bstats[:, br, :, :].rearrange("p b s -> p (b s)")).then_inc(bn_step, 1)
                link.skip(2)
                dve.tensor_scalar(bvare[:, :], bmv[:, :, 1], EPS, None, ALU.add).then_inc(bn_var, 1)
                dve.wait_ge(bn_rstd, 1)
                dve.wait_ge(setup_in, 16 * 7)
                link(dve.tensor_tensor(bscale[:, :], brstd[:, :], gamma[:, :], ALU.mult))
                link(dve.tensor_tensor(bshift[:, :], bmv[:, :, 0], bscale[:, :], ALU.mult))
                dve.tensor_tensor(bshift[:, :], beta[:, :], bshift[:, :], ALU.subtract).then_inc(bn_ready, 1)

            @block.gpsimd
            def _(pool):
                pool.wait_ge(bn_var, 1)
                pool.tensor_tensor(brstd[:, :], bvare[:, :], cst["mhalf"][:, 0:2], ALU.pow).then_inc(bn_rstd, 1)

            @block.scalar
            def _(act):
                act.wait_ge(bn_ready, 1)
                for br in range(2):
                    part = conv[:, br, :, :].rearrange("p b s -> p (b s)")
                    act.activation(part, part, ACT.Gelu, scale=bscale[:, br:br + 1], bias=bshift[:, br:br + 1])\
                        .then_inc(gelu_done, 1)

        loaded = [sem(f"loaded{i}") for i in range(PER_TRIP)]
        act_ready, xb_ready = sem("act_ready"), sem("xb_ready")
        lin_full, logit_done = sem("lin_full"), sem("logit_done")
        exp_done = sem("exp_done")
        chain = sem("chain")
        top_done, sel_done = sem("top_done"), sem("sel_done")
        full_full, zo_done = sem("full_full"), sem("zo_done")
        xs_done = sem("xs_done")
        xsT_full, xsT_out = sem("xsT_full"), sem("xsT_out")
        in_full, z_done = sem("in_full"), sem("z_done")
        zr_done = sem("zr_done")
        nmean_done = sem("nmean_done")
        ln_step, ln_var, ln_rstd, ln_done = (sem(n) for n in ("ln_step", "ln_var", "ln_rstd", "ln_done"))
        stored = [sem(f"stored{i}") for i in range(2)]

        def batches(b):
            with nc.Block() as block:
                @block.sync
                def _(sp):
                    for i in range(PER_TRIP):
                        sp.dma_start(xT[:, i, :, :], scr["x5T"][b + i].rearrange("(c p) n -> p c n", p=P))\
                            .then_inc(loaded[i], 16)
                        sp.dma_start(x[:, i * NT:(i + 1) * NT, :],
                                     scr["x5"].rearrange("(b t p) n -> b p t n", p=P, t=NT)[b + i]).then_inc(loaded[i], 16)
                    rows = out.rearrange("b (t p) n -> b t p n", p=P)
                    for t in range(TT):
                        sp.wait_ge(ln_done, t + 1)
                        sp.dma_start(rows[b + t // NT, t % NT], z[:, t % 2, :]).then_inc(stored[t % 2], 16)
                    for i in range(2):
                        sp.wait_ge(stored[i], 16 * TT // 2)

                @block.tensor
                def _(pe):
                    def lin(t):
                        for br in range(2):
                            if t >= 2:
                                pe.wait_ge(logit_done, 2 * (t - 2) + br + 1)
                            pe.matmul(bank[2 * (t % 2) + br], act_b[:, br, t * P:(t + 1) * P], w_lin[:, br, :],
                                      start=True, stop=True).then_inc(lin_full, 1)

                    def full(t):
                        if t >= 2:
                            pe.wait_ge(zo_done, t - 1)
                        pe.wait_ge(loaded[t // NT], 32)
                        q = t % NT
                        for c in range(NC):
                            mm = pe.matmul(bank[4 + t % 2], xT[:, t // NT, c, q * P:(q + 1) * P], w[:, c, :],
                                           start=(c == 0), stop=(c == NC - 1))
                        mm.then_inc(full_full, 1)

                    pe.wait_ge(act_ready, 1)
                    lin(0)
                    lin(1)
                    full(0)
                    full(1)
                    for t in range(TT):
                        if t + 2 < TT:
                            lin(t + 2)
                        pe.wait_ge(xs_done, t + 1)
                        if t >= 1:
                            pe.wait_ge(xsT_out, t)
                        for c in range(NC):
                            mm = pe.transpose(bank[6][:, c * P:(c + 1) * P], xs[:, t % 2, c * P:(c + 1) * P], ident[:, :])
                        mm.then_inc(xsT_full, 1)
                        if t + 2 < TT:
                            full(t + 2)
                        pe.wait_ge(xsT_out, t + 1)
                        if t >= 1:
                            pe.wait_ge(z_done, t)
                        for c in range(NC):
                            mm = pe.matmul(bank[7], xsT[:, t % 2, c, :], w[:, c, :], start=(c == 0), stop=(c == NC - 1))
                        mm.then_inc(in_full, 1)

                @block.scalar
                def _(act):
                    act.activation(act_b[:, :, :], conv[:, :, bass.ds(b, PER_TRIP), :].rearrange("p g o s -> p g (o s)"),
                                   ACT.Copy).then_inc(act_ready, 1)

                    def exps(t):
                        for br in range(2):
                            u = 2 * t + br
                            act.wait_ge(logit_done, u + 1)
                            act.activation(expv[:, u % 4, :], expv[:, u % 4, :], ACT.Exp, scale=-1.0,
                                           bias=nmax[:, u % 4:u % 4 + 1], accum_out=esum[:, u % 4:u % 4 + 1])\
                                .then_inc(exp_done, 1)

                    def normalise(t):
                        act.wait_ge(nmean_done, t + 1)
                        act.activation(z[:, t % 2, :], z[:, t % 2, :], ACT.Identity, scale=rstd[:, t % 2:t % 2 + 1],
                                       bias=nmean[:, t % 2:t % 2 + 1]).then_inc(ln_done, 1)

                    exps(0)
                    for t in range(TT):
                        if t + 1 < TT:
                            exps(t + 1)
                        act.wait_ge(xsT_full, t + 1)
                        if t >= 2:
                            act.wait_ge(in_full, t - 1)
                        act.activation(xsT[:, t % 2, :, :], bank[6].rearrange("p (c q) -> p c q", q=P), ACT.Copy)\
                            .then_inc(xsT_out, 1)
                        if t >= 2:
                            normalise(t - 2)
                    normalise(TT - 2)
                    normalise(TT - 1)

                @block.vector
                def _(dve):
                    link = chain_of(dve, chain)
                    ln = chain_of(dve, ln_step)

                    def logits(t):
                        for br in range(2):
                            u = 2 * t + br
                            dve.wait_ge(lin_full, u + 1)
                            if u >= 4:
                                dve.wait_ge(sel_done, t - 1)
                            dve.tensor_tensor_reduce(out=expv[:, u % 4, :], in0=bank[2 * (t % 2) + br], in1=b_lin[:, br, :],
                                                     scale=-1.0, scalar=-TAKEN, op0=ALU.add, op1=ALU.min,
                                                     accum_out=nmax[:, u % 4:u % 4 + 1]).then_inc(logit_done, 1)

                    def weigh(t):
                        u = 2 * t % 4
                        dve.wait_ge(sel_done, t + 1)
                        dve.wait_ge(full_full, t + 1)
                        if t >= 2:
                            dve.wait_ge(z_done, t - 1)
                        dve.scalar_tensor_tensor(out=zo[:, t % 2, :], in0=left[:, u, :], scalar=rsum[:, u:u + 1],
                                                 in1=bank[4 + t % 2], op0=ALU.mult, op1=ALU.mult).then_inc(zo_done, 1)

                    def finish(t):
                        dve.wait_ge(in_full, t + 1)
                        dve.wait_ge(zr_done, t + 1)
                        if t >= 2:
                            dve.wait_ge(stored[t % 2], 16 * (t // 2))
                        u = (2 * t + 1) % 4
                        dve.scalar_tensor_tensor(out=z[:, t % 2, :], in0=bank[7], scalar=rsum[:, u:u + 1],
                                                 in1=zo[:, t % 2, :], op0=ALU.mult, op1=ALU.add).then_inc(z_done, 1)
                        dve.wait_ge(z_done, t + 1)
                        ln(dve.bn_stats(stats[:, t % 2, :], z[:, t % 2, :]))
                        ln(dve.bn_aggr(mv[:, t % 2, :], stats[:, t % 2, :]))
                        dve.tensor_scalar(vare[:, t % 2:t % 2 + 1], mv[:, t % 2, 1:2], EPS, None, ALU.add).then_inc(ln_var, 1)

                    def shift(t):
                        dve.wait_ge(ln_rstd, t + 1)
                        if t >= 2:
                            dve.wait_ge(ln_done, t - 1)
                        dve.tensor_scalar(nmean[:, t % 2:t % 2 + 1], mv[:, t % 2, 0:1], -1.0, rstd[:, t % 2:t % 2 + 1],
                                          ALU.mult, ALU.mult).then_inc(nmean_done, 1)

                    logits(0)
                    for t in range(TT):
                        if t + 1 < TT:
                            logits(t + 1)
                        if t >= 1:
                            weigh(t - 1)
                        us = [(2 * t + br) % 4 for br in range(2)]
                        dve.wait_ge(exp_done, 2 * t + 2)
                        link(dve.reciprocal(rsum[:, us[0]:us[0] + 2], esum[:, us[0]:us[0] + 2]))
                        if t >= 2:
                            dve.wait_ge(xs_done, t - 1)
                        for r in range(KGATE // 8):
                            for u in us:
                                dve.max(top[:, u, :], (left if r else expv)[:, u, :]).then_inc(chain, 1)
                            link.skip(2)
                            for i, u in enumerate(us):
                                ins = dve.match_replace(left[:, u, :], top[:, u, :], (left if r else expv)[:, u, :], 0.0)
                                if r < KGATE // 8 - 1:
                                    ins.then_inc(chain, 1)
                                else:
                                    ins.then_inc(top_done, 1)
                            if r < KGATE // 8 - 1:
                                link.skip(2)
                        if t >= 2:
                            shift(t - 2)
                        if t >= 1:
                            finish(t - 1)
                    weigh(TT - 1)
                    shift(TT - 2)
                    finish(TT - 1)
                    shift(TT - 1)

                @block.gpsimd
                def _(pool):
                    for t in range(TT):
                        pool.wait_ge(loaded[t // NT], 32)
                        pool.tensor_tensor(xb[:, t, :], x[:, t, :], b_out[:, :], ALU.add).then_inc(xb_ready, 1)
                    for t in range(TT):
                        pool.wait_ge(top_done, 2 * t + 2)
                        u0 = 2 * (t % 2)
                        pool.tensor_tensor(left[:, u0:u0 + 2, :], expv[:, u0:u0 + 2, :], left[:, u0:u0 + 2, :], ALU.subtract)\
                            .then_inc(sel_done, 1)
                        pool.wait_ge(sel_done, t + 1)
                        if t >= 2:
                            pool.wait_ge(xsT_full, t - 1)
                        pool.tensor_tensor(xs[:, t % 2, :], left[:, u0 + 1, :], x[:, t, :], ALU.mult).then_inc(xs_done, 1)
                        if t >= 1:
                            pool.wait_ge(ln_var, t)
                            if t >= 3:
                                pool.wait_ge(ln_done, t - 2)
                            pool.tensor_tensor(rstd[:, (t - 1) % 2:(t - 1) % 2 + 1], vare[:, (t - 1) % 2:(t - 1) % 2 + 1],
                                               cst["mhalf"][:, 0:1], ALU.pow).then_inc(ln_rstd, 1)
                        pool.wait_ge(zo_done, t + 1)
                        pool.wait_ge(xb_ready, t + 1)
                        pool.tensor_tensor(zo[:, t % 2, :], zo[:, t % 2, :], xb[:, t, :], ALU.add).then_inc(zr_done, 1)
                    pool.wait_ge(ln_var, TT)
                    pool.wait_ge(ln_done, TT - 2)
                    pool.tensor_tensor(rstd[:, (TT - 1) % 2:(TT - 1) % 2 + 1], vare[:, (TT - 1) % 2:(TT - 1) % 2 + 1],
                                       cst["mhalf"][:, 0:1], ALU.pow).then_inc(ln_rstd, 1)

        with nc.Fori(0, trips // PER_TRIP) as i:
            batches(i * PER_TRIP)
            with nc.Block() as block:
                @block.vector
                def _(dve):
                    for s in sems:
                        dve.sem_clear(s)


def decoder_program(nc, A, out):
    scr = {}
    for name, shape in (("rows", [T + CAP, XW]), ("slots", [E * CAP + 1, 1]), ("acc", [T + CAP, D]),
                        ("x5", [T, D]), ("x5T", [B, D, S]), ("xc", [B, P, 2, S])):
        scr[name] = nc.dram_tensor("scratch_" + name, shape, FP32, kind="Internal").ap()
    with ExitStack() as ctx:
        cst = constants(nc, ctx)
        pruned_attention_stage(nc, A, scr, cst, B)
        experts_stage(nc, A, scr, cst)
        layer1_attention_stage(nc, A, scr, cst, B)
        gated_layer_stage(nc, A, scr, out, cst, B)


def kernel(**inputs):
    import numpy as _np
    import concourse.bacc as _bacc
    from concourse import mybir as _mybir
    from concourse.bass_utils import run_bass_kernel_spmd as _run

    a = {k: _np.asarray(v) for k, v in inputs.items()}

    def columns(*vectors):
        return _np.concatenate(vectors).reshape(-1, P).T

    def gates(name, axis, order=None):
        pair = [a["L1_ffn_so_" + name], a["L1_ffn_si_" + name]]
        return _np.stack([p.T if order else p for p in pair], axis)

    conv_w = gates("conv_w", 0).reshape(2, D // P, P).transpose(2, 0, 1)
    laid = {
        "x": a["x"], "xT": a["x"].transpose(0, 2, 1),
        "ctx": a["ctx_1024"], "ctxT": a["ctx_1024"].transpose(0, 2, 1),
        "mask": a["mask_Bx1xSxS2_if1"].reshape(B, S, S2),
        "w_qkv0": a["L0_attn_w_attn"].T, "b_qkv0": columns(a["L0_attn_b_attn"]),
        "w_proj0": a["L0_attn_w_proj"].T, "b_proj0": a["L0_attn_b_proj"],
        "w_router": a["L0_ffn_router_w"].T, "w_sgu": a["L0_ffn_ws_gate_up"], "w_sdown": a["L0_ffn_ws_down"],
        "w_gate": a["L0_ffn_w_gate"], "w_up": a["L0_ffn_w_up"], "w_down": a["L0_ffn_w_down"],
        "w_qkv1": _np.concatenate([a["L1_attn_W" + k].T for k in "qkv"], 1),
        "b_qkv1": columns(*(a["L1_attn_b" + k] for k in "qkv")),
        "w_o1": a["L1_attn_Wo"].T, "b_o1": a["L1_attn_bo"],
        "w_x": _np.stack([a["L1_xattn_W" + k].T for k in "qkv"]),
        "w_xo": a["L1_xattn_Wo"].T, "b_xo": a["L1_xattn_bo"],
        "conv_w": conv_w, "conv_b": gates("conv_b", 1),
        "gamma": gates("gamma", 1), "beta": gates("beta", 1),
        "w_lin": gates("lin_w", 1, order="T"), "b_lin": gates("lin_b", 0),
        "w_ffn1": a["L1_ffn_weight"], "b_ffn1": a["L1_ffn_bias"],
    }
    nc = _bacc.Bacc("TRN2", target_bir_lowering=False, num_devices=1)
    arrays, aps = {}, {}
    for name, value in laid.items():
        value = _np.ascontiguousarray(value)
        arrays[f"in_{name}"] = value
        aps[name] = nc.dram_tensor(f"in_{name}", value.shape, _mybir.dt.from_np(value.dtype), kind="ExternalInput").ap()
    out = nc.dram_tensor("out_0", (B, S, D), _mybir.dt.float32, kind="ExternalOutput").ap()
    decoder_program(nc, aps, out)
    r = _run(nc, [arrays], core_ids=[0])
    return r.results[0]["out_0"]
```
